# Optimizing a Trainium2 kernel written in Bass

```python
import numpy as np
import jax
import jax.numpy as jnp

def _softmax(x, axis=-1):
    return jax.nn.softmax(x, axis=axis)

def _gelu(x):
    return jax.nn.gelu(x, approximate=True)

def _silu(x):
    return jax.nn.silu(x)

def _sigmoid(x):
    return jax.nn.sigmoid(x)

def _layernorm(x, axis=-1, eps=1e-05):
    m = jnp.mean(x, axis=axis, keepdims=True)
    v = jnp.var(x, axis=axis, keepdims=True)
    return (x - m) / jnp.sqrt(v + eps)

def _scatter_add(tgt, idx, src, axis=0):
    return tgt.at[idx].add(src)

def _segment_sum(src, seg, n):
    return jax.ops.segment_sum(src, seg, n)
kernel_name = 'mk_adj_preln_d4_adj_r2_9004e2'

def setup_inputs(seed: int=0):
    np.random.seed(seed)
    _w = jnp.asarray

    def _rec_inputs():
        import jax
        import jax.numpy as jnp
        _gk = jax.random.key(seed)
        x = -0.0002928 + 1 * jax.random.normal(jax.random.fold_in(_gk, 1), (16, 512, 128), jnp.float32)
        _w = (1.0 + jnp.arange(512, dtype=jnp.float32)) ** (-0.5)
        _w = _w / _w.mean()
        _pij = jnp.clip(0.015625 * _w[:, None] * _w[None, :], 0.0, 1.0)
        _a = jax.random.uniform(jax.random.fold_in(_gk, 2), (16, 512, 512)) < _pij
        _a = jnp.logical_or(_a, jnp.eye(512, dtype=bool))
        _af = _a.astype(jnp.float32)
        _af = _af * jax.random.uniform(jax.random.fold_in(_gk, 3), (16, 512, 512), jnp.float32, 0.05, 1)
        adj = _af
        return (x, adj)
    x, adj = _rec_inputs()

    def _L0_gnn_setup():
        import jax, jax.numpy as jnp
        import numpy as np
        D_IN = 128
        D_OUT = 128
        key = jax.random.key(seed)
        k1, k2, k3 = jax.random.split(key, 3)
        B, N = (4, 2048)
        seq = jax.random.normal(k1, (B, N, D_IN), dtype=jnp.float32)
        adj = jax.random.uniform(k2, (B, N, N), dtype=jnp.float32)
        limit = float(np.sqrt(6.0 / (D_IN + D_OUT)))
        W = jax.random.uniform(k3, (D_IN, D_OUT), dtype=jnp.float32, minval=-limit, maxval=limit)
        bias = jnp.zeros((D_OUT,), dtype=jnp.float32)
        prelu_a = jnp.array(0.25, dtype=jnp.float32)
        return {'seq': seq, 'adj': adj, 'W': W, 'bias': bias, 'prelu_a': prelu_a}
    _L0_gnn_all = _L0_gnn_setup()
    _L0_gnn_in = {k: v for k, v in _L0_gnn_all.items() if k in ('W', 'bias', 'prelu_a')}
    del _L0_gnn_all

    def _L1_gnn_setup():
        import jax, jax.numpy as jnp
        import numpy as np
        LN_EPS = 1e-05
        key = jax.random.key(seed)
        k1, k2, k3, k4 = jax.random.split(key, 4)
        B, N, F, O = (8, 1024, 128, 128)
        x = jax.random.normal(k1, (B, N, F), dtype=jnp.float32)
        adj = jax.random.uniform(k2, (B, N, N), dtype=jnp.float32)
        gamma = jnp.ones((F,), jnp.float32)
        beta = jnp.zeros((F,), jnp.float32)
        W_self = jax.random.normal(k3, (F, O), dtype=jnp.float32) * (1.0 / np.sqrt(F))
        W_neigh = jax.random.normal(k4, (F, O), dtype=jnp.float32) * (1.0 / np.sqrt(F))
        return {'x': x, 'adj': adj, 'gamma': gamma, 'beta': beta, 'W_self': W_self, 'W_neigh': W_neigh}
    _L1_gnn_all = _L1_gnn_setup()
    _L1_gnn_in = {k: v for k, v in _L1_gnn_all.items() if k in ('gamma', 'beta', 'W_self', 'W_neigh')}
    del _L1_gnn_all

    def _L2_gnn_setup():
        import math
        import jax, jax.numpy as jnp
        import numpy as np
        HIDDEN = 128
        HEADS = 8
        HEAD_DIM = HIDDEN // HEADS
        key = jax.random.key(seed)
        ks = jax.random.split(key, 8)
        b, n = (2, 2048)
        node_state = jax.random.normal(ks[0], (b, n, HIDDEN), dtype=jnp.float32)
        adjacency = jax.random.uniform(ks[1], (b, n, n), dtype=jnp.float32)
        s = 1.0 / math.sqrt(HIDDEN)
        Wq = jax.random.uniform(ks[2], (HIDDEN, HIDDEN), jnp.float32, -s, s)
        Wk = jax.random.uniform(ks[3], (HIDDEN, HIDDEN), jnp.float32, -s, s)
        Wv = jax.random.uniform(ks[4], (HIDDEN, HIDDEN), jnp.float32, -s, s)
        Wo = jax.random.uniform(ks[5], (HIDDEN, HIDDEN), jnp.float32, -s, s)
        bo = jax.random.uniform(ks[6], (HIDDEN,), jnp.float32, -s, s)
        return {'node_state': node_state, 'adjacency': adjacency, 'Wq': Wq, 'Wk': Wk, 'Wv': Wv, 'Wo': Wo, 'bo': bo}
    _L2_gnn_all = _L2_gnn_setup()
    _L2_gnn_in = {k: v for k, v in _L2_gnn_all.items() if k in ('Wq', 'Wk', 'Wv', 'Wo', 'bo')}
    del _L2_gnn_all

    def _L3_gnn_setup():
        import jax, jax.numpy as jnp
        import numpy as np
        from jax import lax
        DIM = 128
        EPS = 1e-05

        def _bn(h, g, b, m, v):
            scale = g / jnp.sqrt(v + EPS)
            return h * scale[None, :, None] + (b - m * scale)[None, :, None]

        def _conv1d(h, w, pad):
            return lax.conv_general_dilated(h, w, window_strides=(1,), padding=[(pad, pad)], dimension_numbers=('NCH', 'OIH', 'NCH'))
        key = jax.random.key(seed)
        ks = jax.random.split(key, 16)
        bs, n, d = (16, 1024, DIM)
        s = 0.05
        return {'x': jax.random.normal(ks[0], (bs, n, d), jnp.float32), 'mask': jnp.ones((bs, n, n), jnp.float32), 'w_se': jax.random.normal(ks[1], (3, d), jnp.float32) * s, 'b_se': jnp.zeros((3,), jnp.float32), 'conv1_w': jax.random.normal(ks[2], (d, d, 1), jnp.float32) * s, 'bn1_g': jnp.ones((d,), jnp.float32), 'bn1_b': jnp.zeros((d,), jnp.float32), 'bn1_m': jnp.zeros((d,), jnp.float32), 'bn1_v': jnp.ones((d,), jnp.float32), 'conv2_w': jax.random.normal(ks[3], (d, d, 17), jnp.float32) * s, 'bn2_g': jnp.ones((d,), jnp.float32), 'bn2_b': jnp.zeros((d,), jnp.float32), 'bn2_m': jnp.zeros((d,), jnp.float32), 'bn2_v': jnp.ones((d,), jnp.float32), 'w_msg': jax.random.normal(ks[4], (d, d), jnp.float32) * s, 'b_msg': jnp.zeros((d,), jnp.float32), 'w_ih': jax.random.normal(ks[5], (3 * d, 2 * d), jnp.float32) * s, 'b_ih': jnp.zeros((3 * d,), jnp.float32), 'w_hh': jax.random.normal(ks[6], (3 * d, d), jnp.float32) * s, 'b_hh': jnp.zeros((3 * d,), jnp.float32)}
    _L3_gnn_all = _L3_gnn_setup()
    _L3_gnn_in = {k: v for k, v in _L3_gnn_all.items() if k in ('w_se', 'b_se', 'conv1_w', 'bn1_g', 'bn1_b', 'bn1_m', 'bn1_v', 'conv2_w', 'bn2_g', 'bn2_b', 'bn2_m', 'bn2_v', 'w_msg', 'b_msg', 'w_ih', 'b_ih', 'w_hh', 'b_hh')}
    del _L3_gnn_all
    return {'x': x, 'adj': adj, 'L0_gnn_W': _L0_gnn_in['W'], 'L0_gnn_bias': _L0_gnn_in['bias'], 'L0_gnn_prelu_a': _L0_gnn_in['prelu_a'], 'L1_gnn_gamma': _L1_gnn_in['gamma'], 'L1_gnn_beta': _L1_gnn_in['beta'], 'L1_gnn_W_self': _L1_gnn_in['W_self'], 'L1_gnn_W_neigh': _L1_gnn_in['W_neigh'], 'L2_gnn_Wq': _L2_gnn_in['Wq'], 'L2_gnn_Wk': _L2_gnn_in['Wk'], 'L2_gnn_Wv': _L2_gnn_in['Wv'], 'L2_gnn_Wo': _L2_gnn_in['Wo'], 'L2_gnn_bo': _L2_gnn_in['bo'], 'L3_gnn_w_se': _L3_gnn_in['w_se'], 'L3_gnn_b_se': _L3_gnn_in['b_se'], 'L3_gnn_conv1_w': _L3_gnn_in['conv1_w'], 'L3_gnn_bn1_g': _L3_gnn_in['bn1_g'], 'L3_gnn_bn1_b': _L3_gnn_in['bn1_b'], 'L3_gnn_bn1_m': _L3_gnn_in['bn1_m'], 'L3_gnn_bn1_v': _L3_gnn_in['bn1_v'], 'L3_gnn_conv2_w': _L3_gnn_in['conv2_w'], 'L3_gnn_bn2_g': _L3_gnn_in['bn2_g'], 'L3_gnn_bn2_b': _L3_gnn_in['bn2_b'], 'L3_gnn_bn2_m': _L3_gnn_in['bn2_m'], 'L3_gnn_bn2_v': _L3_gnn_in['bn2_v'], 'L3_gnn_w_msg': _L3_gnn_in['w_msg'], 'L3_gnn_b_msg': _L3_gnn_in['b_msg'], 'L3_gnn_w_ih': _L3_gnn_in['w_ih'], 'L3_gnn_b_ih': _L3_gnn_in['b_ih'], 'L3_gnn_w_hh': _L3_gnn_in['w_hh'], 'L3_gnn_b_hh': _L3_gnn_in['b_hh']}

def reference(x, adj, L0_gnn_W, L0_gnn_bias, L0_gnn_prelu_a, L1_gnn_gamma, L1_gnn_beta, L1_gnn_W_self, L1_gnn_W_neigh, L2_gnn_Wq, L2_gnn_Wk, L2_gnn_Wv, L2_gnn_Wo, L2_gnn_bo, L3_gnn_w_se, L3_gnn_b_se, L3_gnn_conv1_w, L3_gnn_bn1_g, L3_gnn_bn1_b, L3_gnn_bn1_m, L3_gnn_bn1_v, L3_gnn_conv2_w, L3_gnn_bn2_g, L3_gnn_bn2_b, L3_gnn_bn2_m, L3_gnn_bn2_v, L3_gnn_w_msg, L3_gnn_b_msg, L3_gnn_w_ih, L3_gnn_b_ih, L3_gnn_w_hh, L3_gnn_b_hh):
    import jax
    import jax.numpy as jnp

    def _L0_gnn_ref(seq, adj, W, bias, prelu_a):
        import jax, jax.numpy as jnp
        import numpy as np
        D_IN = 128
        D_OUT = 128
        seq_fts = jnp.einsum('bnd,de->bne', seq, W)
        out = jnp.einsum('bnm,bme->bne', adj, seq_fts) + bias
        return jnp.where(out >= 0, out, prelu_a * out)

    def _L1_gnn_ref(x, adj, gamma, beta, W_self, W_neigh):
        import jax, jax.numpy as jnp
        import numpy as np
        LN_EPS = 1e-05
        mu = jnp.mean(x, axis=-1, keepdims=True)
        var = jnp.mean(jnp.square(x - mu), axis=-1, keepdims=True)
        xn = (x - mu) * jax.lax.rsqrt(var + LN_EPS) * gamma + beta
        d_out = jnp.sum(adj, axis=1)
        d_in = jnp.sum(adj, axis=2)
        s_out = jnp.where(d_out != 0, jax.lax.rsqrt(d_out), 0.0)
        s_in = jnp.where(d_in != 0, jax.lax.rsqrt(d_in), 0.0)
        A_norm = s_out[:, :, None] * adj * s_in[:, None, :]
        eye = jnp.eye(adj.shape[1], dtype=adj.dtype)
        L = eye[None, :, :] - A_norm
        neighbor = jnp.einsum('bij,bjf->bif', L, xn)
        pre = xn @ W_self + neighbor @ W_neigh
        return jax.nn.softplus(pre)

    def _L2_gnn_ref(node_state, adjacency, Wq, Wk, Wv, Wo, bo):
        import math
        import jax, jax.numpy as jnp
        import numpy as np
        HIDDEN = 128
        HEADS = 8
        HEAD_DIM = HIDDEN // HEADS
        b, n, _ = node_state.shape

        def split_heads(x):
            return x.reshape(b, n, HEADS, HEAD_DIM).transpose(0, 2, 1, 3)
        q = split_heads(node_state @ Wq.T)
        k = split_heads(node_state @ Wk.T)
        v = split_heads(node_state @ Wv.T)
        scores = jnp.einsum('bhqd,bhkd->bhqk', q, k) / math.sqrt(HEAD_DIM)
        log_adj = jnp.log(adjacency + 1e-06)
        scores = scores + log_adj[:, None, :, :]
        attn = jax.nn.softmax(scores, axis=-1)
        out = jnp.einsum('bhqk,bhkd->bhqd', attn, v)
        out = out.transpose(0, 2, 1, 3).reshape(b, n, HIDDEN)
        return out @ Wo.T + bo

    def _L3_gnn_ref(x, mask, w_se, b_se, conv1_w, bn1_g, bn1_b, bn1_m, bn1_v, conv2_w, bn2_g, bn2_b, bn2_m, bn2_v, w_msg, b_msg, w_ih, b_ih, w_hh, b_hh):
        import jax, jax.numpy as jnp
        import numpy as np
        from jax import lax
        DIM = 128
        EPS = 1e-05

        def _bn(h, g, b, m, v):
            scale = g / jnp.sqrt(v + EPS)
            return h * scale[None, :, None] + (b - m * scale)[None, :, None]

        def _conv1d(h, w, pad):
            return lax.conv_general_dilated(h, w, window_strides=(1,), padding=[(pad, pad)], dimension_numbers=('NCH', 'OIH', 'NCH'))
        d = x.shape[-1]
        xc = jnp.transpose(x, (0, 2, 1))
        h = _bn(_conv1d(xc, conv1_w, 0), bn1_g, bn1_b, bn1_m, bn1_v)
        h = jax.nn.relu(h)
        h = _bn(_conv1d(h, conv2_w, 8), bn2_g, bn2_b, bn2_m, bn2_v)
        x_conv = jnp.transpose(jax.nn.relu(h + xc), (0, 2, 1))
        s = x @ w_se.T + b_se
        sq = jnp.sum(s * s, axis=-1)
        dist = sq[:, :, None] + sq[:, None, :] - 2.0 * jnp.einsum('bnd,bmd->bnm', s, s)
        A = jnp.exp(-dist) * mask
        msg = jax.nn.relu(x @ w_msg.T + b_msg)
        x_nmp = jnp.einsum('bnm,bmd->bnd', A, msg)
        x_in = jnp.concatenate([x_conv, x_nmp], axis=-1)
        gi = x_in @ w_ih.T + b_ih
        gh = x @ w_hh.T + b_hh
        gi_r, gi_z, gi_n = (gi[..., :d], gi[..., d:2 * d], gi[..., 2 * d:])
        gh_r, gh_z, gh_n = (gh[..., :d], gh[..., d:2 * d], gh[..., 2 * d:])
        r = jax.nn.sigmoid(gi_r + gh_r)
        z = jax.nn.sigmoid(gi_z + gh_z)
        nn_ = jnp.tanh(gi_n + r * gh_n)
        return (1.0 - z) * nn_ + z * x
    h = jnp.maximum(_layernorm(x, axis=-1), 0.0)
    x = x + _L0_gnn_ref(h, adj, L0_gnn_W, L0_gnn_bias, L0_gnn_prelu_a)
    h = jnp.maximum(_layernorm(x, axis=-1), 0.0)
    x = x + _L1_gnn_ref(h, adj, L1_gnn_gamma, L1_gnn_beta, L1_gnn_W_self, L1_gnn_W_neigh)
    h = jnp.maximum(_layernorm(x, axis=-1), 0.0)
    x = x + _L2_gnn_ref(h, adj, L2_gnn_Wq, L2_gnn_Wk, L2_gnn_Wv, L2_gnn_Wo, L2_gnn_bo)
    h = jnp.maximum(_layernorm(x, axis=-1), 0.0)
    x = x + _L3_gnn_ref(h, adj, L3_gnn_w_se, L3_gnn_b_se, L3_gnn_conv1_w, L3_gnn_bn1_g, L3_gnn_bn1_b, L3_gnn_bn1_m, L3_gnn_bn1_v, L3_gnn_conv2_w, L3_gnn_bn2_g, L3_gnn_bn2_b, L3_gnn_bn2_m, L3_gnn_bn2_v, L3_gnn_w_msg, L3_gnn_b_msg, L3_gnn_w_ih, L3_gnn_b_ih, L3_gnn_w_hh, L3_gnn_b_hh)
    return x

_drawn_inputs = setup_inputs


def setup_inputs(seed=0):
    import zlib

    import numpy as np

    out = dict(_drawn_inputs(seed))
    spreads = {'L0_gnn_bias': (0.0, 0.1),
     'L1_gnn_gamma': (1.0, 0.2),
     'L1_gnn_beta': (0.0, 0.1),
     'L3_gnn_b_se': (0.0, 2.0),
     'L3_gnn_bn1_g': (1.0, 0.6),
     'L3_gnn_bn1_b': (0.0, 0.74),
     'L3_gnn_bn1_m': (0.0, 0.613),
     'L3_gnn_bn1_v': (1.0, 0.6),
     'L3_gnn_bn2_g': (1.0, 0.6),
     'L3_gnn_bn2_b': (0.0, 0.8),
     'L3_gnn_bn2_m': (0.0, 0.8),
     'L3_gnn_bn2_v': (1.0, 0.6),
     'L3_gnn_b_msg': (0.0, 2.0),
     'L3_gnn_b_ih': (0.0, 0.55),
     'L3_gnn_b_hh': (0.0, 0.8)}
    factors = {'L2_gnn_Wq': 8.0, 'L2_gnn_Wk': 8.0, 'L3_gnn_w_se': 44.744, 'L3_gnn_w_msg': 4.506}
    for name, (base, spread) in spreads.items():
        noise = np.random.default_rng([zlib.crc32(name.encode()), seed]).standard_normal(out[name].shape)
        drawn = base * np.exp(spread * noise) if base else spread * noise
        out[name] = jnp.asarray(drawn.astype(out[name].dtype))
    for name, factor in factors.items():
        out[name] = (out[name] * factor).astype(out[name].dtype)
    return out
```

```python
from contextlib import ExitStack

import concourse.bass as bass
from concourse import mybir

F32 = mybir.dt.float32
BF16 = mybir.dt.bfloat16
ALU = mybir.AluOpType
ACT = mybir.ActivationFunctionType
AX = mybir.AxisListType

P = 128
B, N, D = 16, 512, 128
NT = N // P
HEADS, HD = 8, 16
HW = 32
TAPS = 17
PAD = TAPS // 2
EPS = 1e-5
ADJ_EPS = 1e-6
Q_PARTS = [0, 0, 1, 0, 2, 1]
K_PARTS = [0, 1, 0, 2, 0, 1]
SPLITS = len(Q_PARTS)
SCORE_ROWS = SPLITS * HD
MAX_ROWS = 3
NSE = 3
DIST_SQ = SPLITS * NSE

(GAMMA, BETA, PRELU, BN1G, BN1B, BN1M, BN1V, BN2G, BN2B, BN2M, BN2V, BIH, BHH) = (
    0, 1, 2, 3, 4, 5, 6, 7, 8, 9, 10, 11, 14)
NPAR = 17

SLOTS = 34
MAXES = 16
EXPS = 16
SLOT = dict(
    max0=0, maxT0=8, max1=9, maxT1=17, exp0=16, exp1=24,
    stats0=0, relu0=1, turn0=2, seq=3, agg=5, gcn=8, stats1=9, relu1=10, stats2=11, scale2=12, turn2=14,
    uv=15, lap=17, soft=20, stats3=22, relu3=23, turn3=25, qkv=26, split=27, shuffle=28,
    outT=0, norm=1, turnY=2, proj=3, stats4=4, relu4=5, turn4=6, conv1=7, emb=8, turnE=10, conv2=8,
    dist=12, mask=13, nmp=14, nmpT=16, xconv=25, gru=26, gates=27, back=33,
)


class Graph:

    def __init__(self, c, turn=None):
        self.c, self.turn = c, turn
        self.par = c % 2

    def __add__(self, k):
        return Graph(self.c + k, self.turn)

    def __sub__(self, k):
        return Graph(self.c - k, self.turn)

    def index(self):
        return self.c if self.turn is None else self.turn * 2 + self.c

    def count(self, per, k=0):
        first = per * self.c + k
        if self.turn is None:
            return max(first, 0)
        assert first > 0
        return self.turn * (2 * per) + first

    def loads(self, k=1):
        half = self.c // 2 + k
        if self.turn is None:
            return max(16 * half, 0)
        assert half > 0
        return self.turn * 16 + 16 * half


def wait(eng, sem, value):
    if isinstance(value, int) and value <= 0:
        return
    eng.wait_ge(sem, value)


def wait_alone(eng, sem, value, passed):
    if isinstance(value, int) and value <= 0:
        return
    eng.wait_ge(sem, value)
    eng.sem_inc(passed, 1)


def pipeline(eng, iteration):
    iteration(Graph(0), None, None)
    iteration(Graph(1), Graph(0), None)
    iteration(Graph(2), Graph(1), Graph(0))
    with eng.Fori(0, (B - 4) // 2) as turn:
        iteration(Graph(3, turn), Graph(2, turn), Graph(1, turn))
        iteration(Graph(4, turn), Graph(3, turn), Graph(2, turn))
    iteration(Graph(B - 1), Graph(B - 2), Graph(B - 3))
    iteration(None, Graph(B - 1), Graph(B - 2))
    iteration(None, None, Graph(B - 1))


def build(nc, x, adj_t, weights, rows, params, conv2, out):
    ctx = ExitStack()
    with ctx:
        def sb(name, shape, dt=F32):
            return ctx.enter_context(nc.sbuf_tensor(name, shape, dt))

        def ps(name, shape):
            return ctx.enter_context(nc.psum_tensor(name, shape, F32))

        def sem(name):
            return ctx.enter_context(nc.semaphore(name))

        wt = sb("wt", [P, 6, D])
        w_lap = sb("w_lap", [P, 2, D])
        w_self = sb("w_self", [P, D])
        w_emb = sb("w_emb", [P, D + NSE])
        w_gru = sb("w_gru", [P, 3, 3 * D])
        w_conv2 = sb("w_conv2", [P, TAPS, D])
        row = sb("row", [P, 3 * D + NSE])
        par = sb("par", [P, NPAR])
        bn_scale = sb("bn_scale", [P, 2])
        bn_shift = sb("bn_shift", [P, 2])
        bn_tmp = sb("bn_tmp", [P, 2])
        gate_bias = sb("gate_bias", [P, 3])
        half_pow = sb("half_pow", [P, 2 * NT])
        one_col = sb("one_col", [P, 1])
        ident = sb("ident", [P, P])
        ident_b = sb("ident_b", [P, P], BF16)

        x_in = sb("x_in", [P, 2, NT, D])
        adj_T = sb("adj_T", [P, 2, NT, N])
        f_stat = sb("f_stat", [P, NT, 6])
        f_mom = sb("f_mom", [P, NT, 2])
        f_var = sb("f_var", [P, NT])
        f_rstd = sb("f_rstd", [P, NT])
        f_shift = sb("f_shift", [P, NT])
        f_h = sb("f_h", [P, NT, D])
        f_z = sb("f_z", [P, NT, D])
        f_hT = sb("f_hT", [P, N])
        seq = sb("seq", [P, NT, D + 1])
        gcn_pre = sb("gcn_pre", [P, NT, D])
        x1 = sb("x1", [P, NT, D])
        deg = sb("deg", [P, 2, NT])
        deg_nz = sb("deg_nz", [P, 2 * NT])
        deg_floor = sb("deg_floor", [P, 2 * NT])
        deg_pow = sb("deg_pow", [P, 2 * NT])
        deg_rs = sb("deg_rs", [P, 2, NT])
        u_scaled = sb("u_scaled", [P, NT, D])
        v_lap = sb("v_lap", [P, NT, D])
        pre = sb("pre", [P, NT, D])
        soft = sb("soft", [P, NT, D])
        junk = sb("junk", [P, NT, N], BF16)
        x2 = sb("x2", [P, NT, D])
        x2b = sb("x2b", [P, 2, NT, D])
        qf = sb("qf", [P, N])
        kf = sb("kf", [P, N])
        q_part = sb("q_part", [P, 3, N], BF16)
        k_part = sb("k_part", [P, 3, N], BF16)
        q_st = sb("q_st", [P, 2, HEADS, N], BF16)
        k_st = sb("k_st", [P, 2, HEADS, N], BF16)
        vals = sb("vals", [P, 2, NT, HEADS, HW])
        maxes = sb("maxes", [P, HEADS, NT])
        neg_max = sb("neg_max", [HEADS // 2 * NT, 2, P])
        max_part = sb("max_part", [HEADS // 2 * NT, 2, 3, P], BF16)
        ex = sb("ex", [P, 3, 2, N])
        pr = sb("pr", [P, 3, 2, N])
        o_T = sb("o_T", [P, 2, N])
        r_sum = sb("r_sum", [P, 2, NT, 4])
        y = sb("y", [P, NT, D])
        y_T = sb("y_T", [P, N])
        x3 = sb("x3", [P, NT, D])
        t_stat = sb("t_stat", [P, NT, 6])
        t_mom = sb("t_mom", [P, NT, 2])
        t_var = sb("t_var", [P, NT])
        t_rstd = sb("t_rstd", [P, NT])
        t_shift = sb("t_shift", [P, NT])
        t_h = sb("t_h", [P, NT, D])
        t_hT = sb("t_hT", [P, N])
        conv_in = sb("conv_in", [P, N + 2 * PAD])
        emb = sb("emb", [P, NT, D + NSE])
        msg = sb("msg", [P, NT, D])
        s_rest = sb("s_rest", [P, 2, NT, NSE])
        s_sq = sb("s_sq", [P, NT, NSE])
        sq = sb("sq", [P, NT])
        nsq = sb("nsq", [P, NT])
        sq_rest = sb("sq_rest", [P, 2, NT])
        dl = sb("dl", [P, NT, P], BF16)
        dr = sb("dr", [P, NT, P], BF16)
        dl_T = sb("dl_T", [P, N], BF16)
        dr_T = sb("dr_T", [P, N], BF16)
        mask_T = sb("mask_T", [P, NT, N])
        near = sb("near", [P, NT, N])
        nmp_T = sb("nmp_T", [P, N])
        xconv_T = sb("xconv_T", [P, N])
        t_r = sb("t_r", [P, N])
        t_z = sb("t_z", [P, N])
        h_n = sb("h_n", [P, N])
        n_T = sb("n_T", [P, N])
        new_T = sb("new_T", [P, N])
        x4 = sb("x4", [P, NT, D])

        q_dram = nc.dram_tensor("q_dram", [2, 3, P, N], BF16).ap()
        k_dram = nc.dram_tensor("k_dram", [2, 3, P, N], BF16).ap()

        p_max = ps("p_max", [P, 2, N])
        p_exp = ps("p_exp", [P, 2, N])
        p_out = ps("p_out", [P, N])
        p_conv = ps("p_conv", [P, N])
        p_f = ps("p_f", [P, 2, N])
        p_f4 = p_f[:, :, :].rearrange("p a (b n) -> p (a b) n", b=2)
        p_e4 = p_exp[:, :, :].rearrange("p a (b n) -> p (a b) n", b=2)

        s_weights = sem("weights_loaded")
        s_const = sem("constants_ready")
        s_bn = sem("bn_folded")
        s_bnv = sem("bn_var")
        s_x = [sem("x_loaded0"), sem("x_loaded1")]
        s_adj = [sem("adj_loaded0"), sem("adj_loaded1")]
        s_mask = sem("mask_loaded")
        s_fstat = sem("f_stats")
        s_fmom = sem("f_moments")
        s_fvar = sem("f_var_eps")
        s_frstd = sem("f_rstd")
        s_fshift = sem("f_shift")
        s_fh = sem("f_relu_h")
        s_fz = sem("f_scaled_z")
        s_fturn = sem("f_turned")
        s_fhT = sem("f_turned_copied")
        s_seqp = sem("seq_product")
        s_seq = sem("seq_ready")
        s_agg = sem("adj_seq_product")
        s_gpre = sem("gcn_pre")
        s_gneg = sem("gcn_negative_part")
        s_gact = sem("gcn_act")
        s_x1 = sem("x1_ready")
        s_dout = sem("column_sums")
        s_din = sem("row_sums")
        s_dfl = sem("degree_floor")
        s_dpow = sem("degree_pow")
        s_drs = sem("degree_rsqrt")
        s_uv = sem("uv_product")
        s_us = sem("u_scaled_ready")
        s_vl = sem("v_copied")
        s_lap = sem("laplacian_product")
        s_rl = sem("r_scaled")
        s_pre = sem("softplus_in")
        s_abs = sem("softplus_abs")
        s_se = sem("softplus_exp")
        s_sl = sem("softplus_log")
        s_sp = sem("softplus_ready")
        s_x2 = sem("x2_ready")
        s_x2b = sem("x2b_ready")
        s_qp = sem("q_product")
        s_kp = sem("k_product")
        s_vp = sem("v_product")
        s_qf = sem("q_copied")
        s_kf = sem("k_copied")
        s_v = sem("v_ready")
        s_qs = sem("q_split")
        s_ks = sem("k_split")
        s_qd = sem("q_written")
        s_kd = sem("k_written")
        s_qst = [sem("q_stacked0"), sem("q_stacked1")]
        s_kst = [sem("k_stacked0"), sem("k_stacked1")]
        s_mp = sem("max_scores")
        s_mx = sem("max_taken")
        s_mT = sem("max_turned")
        s_mpart = sem("max_split")
        s_mrow = [sem("max_rows0"), sem("max_rows1")]
        s_ep = sem("exp_scores")
        s_e = sem("exp_ready")
        s_pr = sem("probs_ready")
        s_pv = sem("probs_used")
        s_oT = sem("attention_out")
        s_on = sem("out_turned")
        s_rs = sem("row_sum_inverse")
        s_y = sem("out_normed")
        s_yTp = sem("out_turned_back")
        s_yT = sem("out_T_copied")
        s_pj = sem("projected")
        s_x3 = sem("x3_ready")
        s_tstat = sem("t_stats")
        s_tmom = sem("t_moments")
        s_tvar = sem("t_var_eps")
        s_trstd = sem("t_rstd")
        s_tshift = sem("t_shift")
        s_th = sem("t_relu_h")
        s_tturn = sem("t_turned")
        s_thT = sem("t_hT_ready")
        s_c1 = sem("conv1_product")
        s_cin = sem("conv2_in")
        s_c2 = sem("conv2_product")
        s_embp = sem("embedding_product")
        s_emb = sem("embedding_biased")
        s_msg = sem("messages_ready")
        s_sc = sem("embedding_split")
        s_dT = sem("distance_turned")
        s_dc = sem("distance_copied")
        s_dp = sem("distances")
        s_near = sem("near_ready")
        s_nm = sem("near_masked")
        s_np = sem("message_product")
        s_nmp = sem("nmp_ready")
        s_cs = sem("conv_summed")
        s_xc = sem("xconv_ready")
        s_gr = sem("gate_r_product")
        s_gz = sem("gate_z_product")
        s_gh = sem("gate_h_product")
        s_gn = sem("gate_n_product")
        s_tr = sem("gate_r")
        s_tz = sem("gate_z")
        s_hn = sem("gate_h")
        s_rn = sem("r_times_h")
        s_ni = sem("n_in_ready")
        s_n = sem("n_ready")
        s_hm = sem("h_minus_n_ready")
        s_zp = sem("z_part_ready")
        s_new = sem("new_state")
        s_nb = sem("new_turned_back")
        s_x4 = sem("x4_ready")
        s_passed_sp = sem("sp_waits_passed")
        s_passed_pool = sem("pool_waits_passed")
        s_passed_dve = sem("dve_waits_passed")
        s_out = [sem("stored0"), sem("stored1")]

        W0, WQ, WK, WV, WO, WC1 = range(6)
        N_WEIGHTS = 6 + 3 + 2 + 3 + 1 + 2
        N_CONST = 13

        def head_rows(t, group):
            return [group * 4 + (t % 2) * 2 + b for b in range(2)]

        block = ctx.enter_context(nc.Block())

        @block.sync
        def _(sp):
            for n, k in enumerate((0, 3, 4, 5, 6, 7)):
                sp.dma_start(wt[:, n, :], weights[k]).then_inc(s_weights, 16)
            sp.dma_start(w_self[:, :], weights[1]).then_inc(s_weights, 16)
            sp.dma_start(w_lap[:, 0, :], weights[2]).then_inc(s_weights, 16)
            sp.dma_start(w_emb[:, 0:D], weights[8]).then_inc(s_weights, 16)
            sp.dma_start(w_emb[:, D:D + NSE], rows[:, 3 * D + NSE:3 * D + 2 * NSE]).then_inc(s_weights, 16)
            sp.dma_start(row[:, :], rows[:, 0:3 * D + NSE]).then_inc(s_weights, 16)
            for k in range(3):
                sp.dma_start(w_gru[:, k, :].rearrange("p (a n) -> p a n", a=3),
                             weights[9 + 3 * k:12 + 3 * k].rearrange("a p n -> p a n")).then_inc(s_weights, 16)
            sp.dma_start(par[:, :], params).then_inc(s_weights, 16)
            sp.dma_start(w_conv2[:, 0:9, :], conv2[0:9].rearrange("k p n -> p k n")).then_inc(s_weights, 16)
            sp.dma_start(w_conv2[:, 9:TAPS, :], conv2[9:TAPS].rearrange("k p n -> p k n")).then_inc(s_weights, 16)

            def iteration(front, att, tail):
                if front:
                    wait_alone(sp, s_x1, (front - 2).count(1, 1), s_passed_sp)
                    sp.dma_start(x_in[:, front.par, :, :],
                                 x[front.index()].rearrange("(t p) d -> p t d", p=P)).then_inc(s_x[front.par], 16)
                    wait_alone(sp, s_pr, (front - 2).count(EXPS, EXPS), s_passed_sp)
                    sp.dma_start(adj_T[:, front.par, :, :],
                                 adj_t[front.index()].rearrange("(t p) n -> p t n", p=P)).then_inc(s_adj[front.par], 16)
                if tail:
                    wait_alone(sp, s_nm, tail.count(NT), s_passed_sp)
                    sp.dma_start(mask_T[:, :, :],
                                 adj_t[tail.index()].rearrange("(t p) n -> p t n", p=P)).then_inc(s_mask, 16)
                for group in range(2):
                    if att:
                        wait_alone(sp, s_mpart, att.count(10, 5 * (group + 1)), s_passed_sp)
                        for j in range(MAX_ROWS):
                            sp.dma_start(q_st[SCORE_ROWS + j:SCORE_ROWS + j + 1, att.par, 4 * group:4 * group + 4, :],
                                         max_part[:, group, j, :]).then_inc(s_mrow[group], 16)
                if front:
                    wait_alone(sp, s_qs, front.count(4, 4), s_passed_sp)
                    sp.dma_start(q_dram[front.par].rearrange("a p n -> p a n"), q_part[:, :, :]).then_inc(s_qd, 16)
                    wait_alone(sp, s_ks, front.count(4, 4), s_passed_sp)
                    sp.dma_start(k_dram[front.par].rearrange("a p n -> p a n"), k_part[:, :, :]).then_inc(s_kd, 16)
                    wait_alone(sp, s_ep, (front - 2).count(EXPS, EXPS), s_passed_sp)
                    wait_alone(sp, s_qd, front.count(16, 16), s_passed_sp)
                    for s, part in enumerate(Q_PARTS):
                        sp.dma_start(q_st[HD * s:HD * s + HD, front.par, :, :],
                                     q_dram[front.par, part].rearrange("(h d) n -> d h n", d=HD)
                                     ).then_inc(s_qst[front.par], 16)
                    wait_alone(sp, s_kd, front.count(16, 16), s_passed_sp)
                    for s, part in enumerate(K_PARTS):
                        sp.dma_start(k_st[HD * s:HD * s + HD, front.par, :, :],
                                     k_dram[front.par, part].rearrange("(h d) n -> d h n", d=HD)
                                     ).then_inc(s_kst[front.par], 16)
                if tail:
                    wait_alone(sp, s_x4, tail.count(1, 1), s_passed_sp)
                    sp.dma_start(out[tail.index()].rearrange("(t p) d -> p t d", p=P),
                                 x4[:, :, :]).then_inc(s_out[tail.par], 16)

            pipeline(sp, iteration)
            for parity in range(2):
                sp.wait_ge(s_out[parity], 16 * (B // 2))

        @block.gpsimd
        def _(pool):
            pool.memset(ident[:, :], 0.0).then_inc(s_const, 1)
            pool.wait_ge(s_const, 1)
            pool.affine_select(out=ident[:, :], in_=ident[:, :], compare_op=ALU.not_equal, fill=1.0, base=0,
                               pattern=[[-1, P]], channel_multiplier=1).then_inc(s_const, 1)
            pool.wait_ge(s_const, 2)
            pool.tensor_copy(ident_b[:, :], ident[:, :]).then_inc(s_const, 1)
            pool.memset(half_pow[:, :], -0.5).then_inc(s_const, 1)
            pool.memset(one_col[:, :], 1.0).then_inc(s_const, 1)
            pool.memset(seq[:, :, D:D + 1], 1.0).then_inc(s_const, 1)
            pool.memset(vals[:, :, :, :, HD:HW], 0.0).then_inc(s_const, 1)
            pool.wait_ge(s_const, 7)
            pool.memset(vals[:, :, :, :, HD:HD + 1], 1.0).then_inc(s_const, 1)
            pool.wait_ge(s_const, 8)
            pool.memset(k_st[SCORE_ROWS:P, :, :, :], 1.0).then_inc(s_const, 1)
            pool.wait_ge(s_const, 9)
            pool.memset(conv_in[:, :], 0.0).then_inc(s_const, 1)
            pool.memset(dl[:, :, :], 0.0).then_inc(s_const, 1)
            pool.memset(dr[:, :, :], 0.0).then_inc(s_const, 1)
            pool.wait_ge(s_const, 12)
            pool.memset(dr[:, :, DIST_SQ:DIST_SQ + 3], 0.0).then_inc(s_const, 1)
            pool.wait_ge(s_weights, 16 * N_WEIGHTS)
            pool.tensor_tensor(w_lap[:, 1, :], w_self[:, :], w_lap[:, 0, :], ALU.add).then_inc(s_bn, 1)
            pool.tensor_scalar(bn_tmp[:, :], par[:, BN1V:BN2V + 1:BN2V - BN1V], EPS, None, ALU.add).then_inc(s_bnv, 1)
            pool.wait_ge(s_bnv, 1)
            pool.tensor_tensor(bn_shift[:, :], bn_tmp[:, :], half_pow[:, 0:2], ALU.pow).then_inc(s_bnv, 1)

            def inverse_root(var, mom, out_, s_mom, s_var, s_rstd, value):
                wait_alone(pool, s_mom, value, s_passed_pool)
                pool.tensor_scalar(var[:, :], mom[:, :, 1], EPS, None, ALU.add).then_inc(s_var, 1)
                pool.wait_ge(s_var, value)
                pool.tensor_tensor(out_[:, :], var[:, :], half_pow[:, 0:NT], ALU.pow).then_inc(s_rstd, 1)

            def iteration(front, att, tail):
                for slot in range(SLOTS):
                    if front:
                        for k, step in enumerate(("stats0", "stats1", "stats2", "stats3")):
                            if slot == SLOT[step]:
                                inverse_root(f_var, f_mom, f_rstd, s_fmom, s_fvar, s_frstd, front.count(4, k + 1))
                        if slot == SLOT["gcn"]:
                            pool.wait_ge(s_dfl, front.count(1, 1))
                            pool.tensor_tensor(deg_pow[:, :], deg_floor[:, :], half_pow[:, :], ALU.pow
                                               ).then_inc(s_dpow, 1)
                        if slot == SLOT["scale2"]:
                            pool.wait_ge(s_frstd, front.count(4, 3))
                            wait_alone(pool, s_fturn, front.count(3), s_passed_pool)
                            for t in range(NT):
                                last = pool.tensor_scalar(f_z[:, t, :], f_h[:, t, :], f_mom[:, t, 0:1],
                                                          f_rstd[:, t:t + 1], ALU.subtract, ALU.mult)
                            last.then_inc(s_fz, 1)
                        if slot == SLOT["stats3"]:
                            pool.wait_ge(s_x2, front.count(1, 1))
                            wait(pool, s_x3, (front - 2).count(1, 1))
                            pool.tensor_tensor(x2b[:, front.par, :, :], x2[:, :, :],
                                               row[:, D:2 * D].unsqueeze(1).to_broadcast([P, NT, D]), ALU.add
                                               ).then_inc(s_x2b, 1)
                        if slot == SLOT["split"]:
                            pool.wait_ge(s_kf, front.count(1, 1))
                            wait_alone(pool, s_kd, front.count(16), s_passed_pool)
                            pool.tensor_scalar(k_part[:, 0, :], kf[:, :], 1.0, None, ALU.mult).then_inc(s_ks, 1)
                            pool.wait_ge(s_ks, front.count(4, 1))
                            pool.tensor_tensor(kf[:, :], kf[:, :], k_part[:, 0, :], ALU.subtract).then_inc(s_ks, 1)
                            wait_alone(pool, s_ks, front.count(4, 2), s_passed_pool)
                            pool.tensor_scalar(k_part[:, 1, :], kf[:, :], 1.0, None, ALU.mult).then_inc(s_ks, 1)
                            pool.wait_ge(s_ks, front.count(4, 3))
                            pool.tensor_tensor(k_part[:, 2, :], kf[:, :], k_part[:, 1, :], ALU.subtract
                                               ).then_inc(s_ks, 1)
                    if tail:
                        if slot == SLOT["stats4"]:
                            inverse_root(t_var, t_mom, t_rstd, s_tmom, s_tvar, s_trstd, tail.count(1, 1))
                        if slot == SLOT["mask"]:
                            pool.wait_ge(s_mask, tail.count(16, 16))
                            for t in range(NT):
                                pool.wait_ge(s_near, tail.count(NT, t + 1))
                                pool.tensor_tensor(near[:, t, :], near[:, t, :], mask_T[:, t, :], ALU.mult
                                                   ).then_inc(s_nm, 1)

            pipeline(pool, iteration)

        @block.vector
        def _(dve):
            dve.wait_ge(s_bnv, 2)
            dve.tensor_tensor(bn_scale[:, :], bn_shift[:, :], par[:, BN1G:BN2G + 1:BN2G - BN1G], ALU.mult).then_inc(s_bnv, 1)
            dve.wait_ge(s_bnv, 3)
            dve.tensor_tensor(bn_tmp[:, :], bn_scale[:, :], par[:, BN1M:BN2M + 1:BN2M - BN1M], ALU.mult).then_inc(s_bnv, 1)
            dve.wait_ge(s_bnv, 4)
            dve.tensor_tensor(bn_shift[:, :], par[:, BN1B:BN2B + 1:BN2B - BN1B], bn_tmp[:, :], ALU.subtract).then_inc(s_bn, 1)
            dve.tensor_tensor(gate_bias[:, 0:2], par[:, BIH:BIH + 2], par[:, BHH:BHH + 2], ALU.add).then_inc(s_bnv, 1)
            dve.tensor_copy(gate_bias[:, 2:3], par[:, BHH + 2:BHH + 3]).then_inc(s_bnv, 1)
            dve.wait_ge(s_bnv, 6)
            dve.tensor_scalar(gate_bias[:, :], gate_bias[:, :], 0.5, None, ALU.mult).then_inc(s_bn, 1)
            dve.wait_ge(s_const, N_CONST)

            def norm_stats(src, stat, mom, s_stat, s_mom, value):
                for t in range(NT):
                    last = dve.bn_stats(stat[:, t, :], src[:, t, :])
                last.then_inc(s_stat, 1)
                wait_alone(dve, s_stat, value, s_passed_dve)
                for t in range(NT):
                    last = dve.bn_aggr(mom[:, t, :], stat[:, t, :])
                last.then_inc(s_mom, 1)

            def norm_shift(mom, rstd, shift, s_rstd, s_shift, value):
                dve.wait_ge(s_rstd, value)
                dve.scalar_tensor_tensor(out=shift[:, :], in0=mom[:, :, 0], scalar=-1.0, in1=rstd[:, :],
                                         op0=ALU.mult, op1=ALU.mult).then_inc(s_shift, 1)

            def take_max(att, k):
                h, half = k // 2, k % 2
                dve.wait_ge(s_mp, att.count(MAXES, k + 1))
                dve.tensor_reduce(maxes[:, h, 2 * half:2 * half + 2], p_max[:, :, :], AX.X, ALU.max).then_inc(s_mx, 1)

            def split_max(att, group):
                v = lambda k: att.count(10, 5 * group + k)
                dve.wait_ge(s_mT, att.count(2, group + 1))
                wait(dve, s_mrow[group], att.count(16 * MAX_ROWS))
                nm, part = neg_max[:, group, :], max_part[:, group, :, :]
                dve.tensor_scalar(nm, p_max[0:16, 0, 0:P], -1.0, None, ALU.mult).then_inc(s_mpart, 1)
                dve.wait_ge(s_mpart, v(1))
                dve.tensor_copy(part[:, 0, :], nm).then_inc(s_mpart, 1)
                dve.wait_ge(s_mpart, v(2))
                dve.tensor_tensor(nm, nm, part[:, 0, :], ALU.subtract).then_inc(s_mpart, 1)
                dve.wait_ge(s_mpart, v(3))
                dve.tensor_copy(part[:, 1, :], nm).then_inc(s_mpart, 1)
                dve.wait_ge(s_mpart, v(4))
                dve.tensor_tensor(part[:, 2, :], nm, part[:, 1, :], ALU.subtract).then_inc(s_mpart, 1)

            def probs(att, k):
                t = (k % 8) // 2
                dve.wait_ge(s_e, att.count(EXPS, k + 1))
                wait(dve, s_pv, att.count(EXPS, k + 1 - 3))
                r = k % 3
                dve.scalar_tensor_tensor(out=pr[:, r, :, :],
                                         in0=adj_T[:, att.par, t, :].unsqueeze(1).to_broadcast([P, 2, N]),
                                         scalar=ADJ_EPS, in1=ex[:, r, :, :], op0=ALU.add, op1=ALU.mult
                                         ).then_inc(s_pr, 1)

            def per_node(col):
                return col.unsqueeze(2).to_broadcast([P, NT, D])

            def iteration(front, att, tail):
                for slot in range(SLOTS):
                    if att:
                        for group in range(2):
                            k = slot - SLOT[f"max{group}"]
                            if 0 <= k < MAXES // 2:
                                take_max(att, k + group * MAXES // 2)
                            if slot == SLOT[f"maxT{group}"]:
                                split_max(att, group)
                            k = slot - SLOT[f"exp{group}"]
                            if 0 <= k < EXPS // 2:
                                probs(att, k + group * EXPS // 2)
                    if front:
                        if slot == SLOT["stats0"]:
                            dve.wait_ge(s_x[front.par], front.loads())
                            norm_stats(x_in[:, front.par], f_stat, f_mom, s_fstat, s_fmom, front.count(4, 1))
                            norm_shift(f_mom, f_rstd, f_shift, s_frstd, s_fshift, front.count(4, 1))
                        if slot == SLOT["seq"]:
                            dve.wait_ge(s_seqp, front.count(1, 1))
                            dve.tensor_copy(seq[:, :, 0:D], p_f[:, 1, :].rearrange("p (t d) -> p t d", t=NT)
                                            ).then_inc(s_seq, 1)
                        if slot == SLOT["gcn"]:
                            dve.wait_ge(s_agg, front.count(1, 1))
                            dve.tensor_tensor(gcn_pre[:, :, :], p_f4[:, :, 0:D],
                                              row[:, 0:D].unsqueeze(1).to_broadcast([P, NT, D]), ALU.add
                                              ).then_inc(s_gpre, 1)
                            dve.tensor_copy(deg[:, 1, :], p_f4[:, :, D]).then_inc(s_din, 1)
                            dve.wait_ge(s_din, front.count(1, 1))
                            dve.wait_ge(s_dout, front.count(1, 1))
                            degs = deg[:, :, :].rearrange("p a t -> p (a t)")
                            dve.tensor_scalar(deg_nz[:, :], degs, 0.0, None, ALU.not_equal)
                            dve.tensor_scalar(deg_floor[:, :], degs, 1e-30, None, ALU.max).then_inc(s_dfl, 1)
                            dve.wait_ge(s_gpre, front.count(1, 1))
                            dve.tensor_scalar(soft[:, :, :], gcn_pre[:, :, :], 0.0, par[:, PRELU:PRELU + 1],
                                              ALU.min, ALU.mult).then_inc(s_gneg, 1)
                            dve.wait_ge(s_gneg, front.count(1, 1))
                            dve.scalar_tensor_tensor(out=gcn_pre[:, :, :], in0=gcn_pre[:, :, :], scalar=0.0,
                                                     in1=soft[:, :, :], op0=ALU.max, op1=ALU.add).then_inc(s_gact, 1)
                            dve.wait_ge(s_gact, front.count(1, 1))
                            dve.tensor_tensor(x1[:, :, :], x_in[:, front.par, :, :], gcn_pre[:, :, :], ALU.add
                                              ).then_inc(s_x1, 1)
                            dve.wait_ge(s_dpow, front.count(1, 1))
                            dve.tensor_tensor(deg_rs[:, :, :].rearrange("p a t -> p (a t)"), deg_pow[:, :],
                                              deg_nz[:, :], ALU.mult).then_inc(s_drs, 1)
                        if slot == SLOT["stats1"]:
                            dve.wait_ge(s_x1, front.count(1, 1))
                            norm_stats(x1, f_stat, f_mom, s_fstat, s_fmom, front.count(4, 2))
                            norm_shift(f_mom, f_rstd, f_shift, s_frstd, s_fshift, front.count(4, 2))
                        if slot == SLOT["stats2"]:
                            dve.wait_ge(s_fh, front.count(3, 2))
                            norm_stats(f_h, f_stat, f_mom, s_fstat, s_fmom, front.count(4, 3))
                        if slot == SLOT["uv"]:
                            dve.wait_ge(s_uv, front.count(1, 1))
                            dve.wait_ge(s_drs, front.count(1, 1))
                            dve.tensor_tensor(u_scaled[:, :, :], p_f4[:, :, 0:D], per_node(deg_rs[:, 1, :]), ALU.mult
                                              ).then_inc(s_us, 1)
                        if slot == SLOT["soft"]:
                            dve.wait_ge(s_lap, front.count(1, 1))
                            dve.wait_ge(s_vl, front.count(1, 1))
                            dve.tensor_tensor(pre[:, :, :], p_f[:, 0, :].rearrange("p (t d) -> p t d", t=NT),
                                              per_node(deg_rs[:, 0, :]), ALU.mult).then_inc(s_rl, 1)
                            dve.wait_ge(s_rl, front.count(1, 1))
                            dve.tensor_tensor(pre[:, :, :], v_lap[:, :, :], pre[:, :, :], ALU.subtract
                                              ).then_inc(s_pre, 1)
                        if slot == SLOT["soft"] + 1:
                            dve.wait_ge(s_sl, front.count(1, 1))
                            dve.scalar_tensor_tensor(out=soft[:, :, :], in0=pre[:, :, :], scalar=0.0,
                                                     in1=soft[:, :, :], op0=ALU.max, op1=ALU.add).then_inc(s_sp, 1)
                            dve.wait_ge(s_sp, front.count(1, 1))
                            wait(dve, s_x2b, front.count(1))
                            dve.tensor_tensor(x2[:, :, :], x1[:, :, :], soft[:, :, :], ALU.add).then_inc(s_x2, 1)
                        if slot == SLOT["stats3"]:
                            dve.wait_ge(s_x2, front.count(1, 1))
                            norm_stats(x2, f_stat, f_mom, s_fstat, s_fmom, front.count(4, 4))
                            norm_shift(f_mom, f_rstd, f_shift, s_frstd, s_fshift, front.count(4, 4))
                        if slot == SLOT["split"]:
                            dve.wait_ge(s_qf, front.count(1, 1))
                            wait(dve, s_qd, front.count(16))
                            dve.tensor_copy(q_part[:, 0, :], qf[:, :]).then_inc(s_qs, 1)
                            dve.wait_ge(s_qs, front.count(4, 1))
                            dve.tensor_tensor(qf[:, :], qf[:, :], q_part[:, 0, :], ALU.subtract).then_inc(s_qs, 1)
                            dve.wait_ge(s_qs, front.count(4, 2))
                            dve.tensor_copy(q_part[:, 1, :], qf[:, :]).then_inc(s_qs, 1)
                            dve.wait_ge(s_qs, front.count(4, 3))
                            dve.tensor_tensor(q_part[:, 2, :], qf[:, :], q_part[:, 1, :], ALU.subtract
                                              ).then_inc(s_qs, 1)
                    if tail:
                        if slot == SLOT["norm"]:
                            dve.wait_ge(s_on, tail.count(1, 1))
                            o4 = p_exp[:, :, :].rearrange("p g (t j w) -> p g t j w", t=NT, j=4)
                            for g2 in range(2):
                                last = dve.reciprocal(r_sum[:, g2, :, :], o4[:, g2, :, :, HD])
                            last.then_inc(s_rs, 1)
                            dve.wait_ge(s_rs, tail.count(1, 1))
                            for g2 in range(2):
                                last = dve.tensor_tensor(
                                    y[:, :, g2 * 64:g2 * 64 + 64].rearrange("p t (j w) -> p t j w", j=4),
                                    o4[:, g2, :, :, 0:HD],
                                    r_sum[:, g2, :, :].unsqueeze(3).to_broadcast([P, NT, 4, HD]), ALU.mult)
                            last.then_inc(s_y, 1)
                        if slot == SLOT["stats4"]:
                            dve.wait_ge(s_pj, tail.count(1, 1))
                            dve.wait_ge(s_x2b, tail.count(1, 1))
                            dve.tensor_tensor(x3[:, :, :], p_exp[:, 1, :].rearrange("p (t d) -> p t d", t=NT),
                                              x2b[:, tail.par, :, :], ALU.add).then_inc(s_x3, 1)
                            dve.wait_ge(s_x3, tail.count(1, 1))
                            norm_stats(x3, t_stat, t_mom, s_tstat, s_tmom, tail.count(1, 1))
                            norm_shift(t_mom, t_rstd, t_shift, s_trstd, s_tshift, tail.count(1, 1))
                        if slot == SLOT["emb"]:
                            dve.wait_ge(s_embp, tail.count(1, 1))
                            dve.tensor_tensor(emb[:, :, :], p_e4[:, :, 0:D + NSE],
                                              row[:, 2 * D:3 * D + NSE].unsqueeze(1).to_broadcast([P, NT, D + NSE]),
                                              ALU.add).then_inc(s_emb, 1)
                            dve.wait_ge(s_emb, tail.count(1, 1))
                            s = emb[:, :, D:D + NSE]
                            v = lambda k: tail.count(10, k)

                            def place(tile, parts, part, src, scale):
                                for n, q in enumerate(parts):
                                    if q == part:
                                        last = dve.tensor_scalar(tile[:, :, NSE * n:NSE * n + NSE], src, scale, None, ALU.mult)
                                return last

                            place(dl, Q_PARTS, 0, s, 2.0)
                            place(dr, K_PARTS, 0, s, 1.0).then_inc(s_sc, 1)
                            dve.tensor_tensor(s_sq[:, :, :], s, s, ALU.mult).then_inc(s_sc, 1)
                            dve.tensor_scalar(msg[:, :, :], emb[:, :, 0:D], 0.0, None, ALU.max).then_inc(s_msg, 1)
                            dve.wait_ge(s_sc, v(2))
                            dve.tensor_tensor(s_rest[:, 0, :, :], s, dr[:, :, 0:NSE], ALU.subtract)
                            dve.tensor_reduce(nsq[:, :], s_sq[:, :, :], AX.X, ALU.add, negate=True).then_inc(s_sc, 1)
                            dve.wait_ge(s_sc, v(3))
                            place(dl, Q_PARTS, 1, s_rest[:, 0, :, :], 2.0)
                            place(dr, K_PARTS, 1, s_rest[:, 0, :, :], 1.0)
                            dve.tensor_copy(dr[:, :, DIST_SQ], nsq[:, :]).then_inc(s_sc, 1)
                            dve.wait_ge(s_sc, v(4))
                            dve.tensor_tensor(s_rest[:, 1, :, :], s_rest[:, 0, :, :], dr[:, :, NSE:2 * NSE], ALU.subtract)
                            dve.tensor_tensor(sq_rest[:, 0, :], nsq[:, :], dr[:, :, DIST_SQ], ALU.subtract).then_inc(s_sc, 1)
                            dve.wait_ge(s_sc, v(5))
                            place(dl, Q_PARTS, 2, s_rest[:, 1, :, :], 2.0)
                            place(dr, K_PARTS, 2, s_rest[:, 1, :, :], 1.0)
                            dve.tensor_copy(dr[:, :, DIST_SQ + 1], sq_rest[:, 0, :]).then_inc(s_sc, 1)
                            dve.wait_ge(s_sc, v(6))
                            dve.tensor_tensor(sq_rest[:, 1, :], sq_rest[:, 0, :], dr[:, :, DIST_SQ + 1], ALU.subtract
                                              ).then_inc(s_sc, 1)
                            dve.wait_ge(s_sc, v(7))
                            dve.tensor_copy(dr[:, :, DIST_SQ + 2], sq_rest[:, 1, :]).then_inc(s_sc, 1)
                            dve.memset(dl[:, :, DIST_SQ:DIST_SQ + 3], 1.0).then_inc(s_sc, 1)
                            dve.wait_ge(s_sc, v(9))
                            dve.tensor_copy(sq[:, :], nsq[:, :]).then_inc(s_sc, 1)
                        if slot == SLOT["turnE"]:
                            dve.wait_ge(s_dT, tail.count(1, 1))
                            dve.tensor_copy(dl_T[:, :], p_exp[:, 0, 0:N // 2].bitcast(BF16))
                            dve.tensor_copy(dr_T[:, :], p_exp[:, 1, 0:N // 2].bitcast(BF16)).then_inc(s_dc, 1)
                        if slot == SLOT["xconv"]:
                            dve.wait_ge(s_c2, tail.count(1, 1))
                            dve.scalar_tensor_tensor(out=xconv_T[:, :], in0=p_conv[:, :], scalar=bn_scale[:, 1:2],
                                                     in1=t_hT[:, :], op0=ALU.mult, op1=ALU.add).then_inc(s_cs, 1)
                            dve.wait_ge(s_cs, tail.count(1, 1))
                            dve.tensor_scalar(xconv_T[:, :], xconv_T[:, :], bn_shift[:, 1:2], 0.0, ALU.add, ALU.max
                                              ).then_inc(s_xc, 1)
                        if slot == SLOT["gates"] + 3:
                            dve.wait_ge(s_hn, tail.count(1, 1))
                            dve.wait_ge(s_tr, tail.count(1, 1))
                            dve.scalar_tensor_tensor(out=h_n[:, :], in0=t_r[:, :], scalar=1.0, in1=h_n[:, :],
                                                     op0=ALU.add, op1=ALU.mult).then_inc(s_rn, 1)
                            dve.wait_ge(s_rn, tail.count(1, 1))
                            dve.wait_ge(s_gn, tail.count(1, 1))
                            dve.tensor_tensor(h_n[:, :], p_max[:, 0, :], h_n[:, :], ALU.add).then_inc(s_ni, 1)
                        if slot == SLOT["gates"] + 4:
                            dve.wait_ge(s_n, tail.count(1, 1))
                            dve.tensor_tensor(new_T[:, :], t_hT[:, :], n_T[:, :], ALU.subtract).then_inc(s_hm, 1)
                            dve.wait_ge(s_hm, tail.count(1, 1))
                            dve.scalar_tensor_tensor(out=new_T[:, :], in0=t_z[:, :], scalar=1.0, in1=new_T[:, :],
                                                     op0=ALU.add, op1=ALU.mult).then_inc(s_zp, 1)
                            dve.wait_ge(s_zp, tail.count(1, 1))
                            dve.scalar_tensor_tensor(out=new_T[:, :], in0=new_T[:, :], scalar=0.5, in1=n_T[:, :],
                                                     op0=ALU.mult, op1=ALU.add).then_inc(s_new, 1)
                        if slot == SLOT["back"]:
                            dve.wait_ge(s_nb, tail.count(1, 1))
                            wait(dve, s_out[(tail - 1).par], (tail - 1).loads())
                            dve.tensor_tensor(x4[:, :, :], p_conv[:, :].rearrange("p (t d) -> p t d", t=NT),
                                              x3[:, :, :], ALU.add).then_inc(s_x4, 1)

            pipeline(dve, iteration)

        @block.scalar
        def _(act):
            act.wait_ge(s_bn, 3)
            act.wait_ge(s_const, N_CONST)

            def relu_norm(dst, src, rstd, shift):
                for t in range(NT):
                    last = act.activation(dst[:, t, :], src[:, t, :], ACT.Relu, bias=shift[:, t:t + 1],
                                          scale=rstd[:, t:t + 1])
                return last

            def exps(att, k):
                act.wait_ge(s_ep, att.count(EXPS, k + 1))
                wait(act, s_pr, att.count(EXPS, k + 1 - 3))
                act.activation(ex[:, k % 3, :, :], p_exp[:, :, :], ACT.Exp).then_inc(s_e, 1)

            def iteration(front, att, tail):
                for slot in range(SLOTS):
                    if att:
                        for group in range(2):
                            k = slot - SLOT[f"exp{group}"]
                            if 0 <= k < EXPS // 2:
                                exps(att, k + group * EXPS // 2)
                            if k == EXPS // 2 + 1:
                                act.wait_ge(s_pv, att.count(EXPS, (group + 1) * EXPS // 2))
                                wait(act, s_on, att.count(1))
                                act.activation(o_T[:, group, :], p_out[:, :], ACT.Copy).then_inc(s_oT, 1)
                    if front:
                        if slot == SLOT["relu0"]:
                            act.wait_ge(s_fshift, front.count(3, 1))
                            relu_norm(f_h, x_in[:, front.par], f_rstd, f_shift).then_inc(s_fh, 1)
                        if slot == SLOT["turn0"]:
                            act.wait_ge(s_fturn, front.count(3, 1))
                            act.activation(f_hT[:, :], p_f[:, 0, :], ACT.Copy).then_inc(s_fhT, 1)
                        if slot == SLOT["agg"]:
                            act.wait_ge(s_adj[front.par], front.loads())
                            for t in range(NT):
                                last = act.activation(junk[:, t, :], adj_T[:, front.par, t, :], ACT.Copy,
                                                      accum_out=deg[:, 0, t:t + 1])
                            last.then_inc(s_dout, 1)
                        if slot == SLOT["relu1"]:
                            act.wait_ge(s_fshift, front.count(3, 2))
                            relu_norm(f_h, x1, f_rstd, f_shift).then_inc(s_fh, 1)
                        if slot == SLOT["turn2"]:
                            act.wait_ge(s_fturn, front.count(3, 2))
                            act.activation(f_hT[:, :], p_f[:, 0, :], ACT.Identity, bias=par[:, BETA:BETA + 1],
                                           scale=par[:, GAMMA:GAMMA + 1]).then_inc(s_fhT, 1)
                        if slot == SLOT["uv"]:
                            act.wait_ge(s_us, front.count(1, 1))
                            act.activation(v_lap[:, :, :], p_f4[:, :, D:2 * D], ACT.Copy).then_inc(s_vl, 1)
                        if slot == SLOT["soft"]:
                            act.wait_ge(s_pre, front.count(1, 1))
                            act.activation(soft[:, :, :], pre[:, :, :], ACT.Abs).then_inc(s_abs, 1)
                            act.wait_ge(s_abs, front.count(1, 1))
                            act.activation(soft[:, :, :], soft[:, :, :], ACT.Exp, scale=-1.0).then_inc(s_se, 1)
                            act.wait_ge(s_se, front.count(1, 1))
                            act.activation(soft[:, :, :], soft[:, :, :], ACT.Ln, bias=one_col[:, 0:1]).then_inc(s_sl, 1)
                        if slot == SLOT["relu3"]:
                            act.wait_ge(s_fshift, front.count(3, 3))
                            relu_norm(f_h, x2, f_rstd, f_shift).then_inc(s_fh, 1)
                        if slot == SLOT["turn3"]:
                            act.wait_ge(s_fturn, front.count(3, 3))
                            act.activation(f_hT[:, :], p_f[:, 0, :], ACT.Copy).then_inc(s_fhT, 1)
                        if slot == SLOT["qkv"]:
                            act.wait_ge(s_qp, front.count(1, 1))
                            wait(act, s_qs, front.count(4))
                            act.activation(qf[:, :], p_f[:, 1, :], ACT.Copy, scale=HD ** -0.5).then_inc(s_qf, 1)
                            act.wait_ge(s_kp, front.count(1, 1))
                            wait(act, s_ks, front.count(4))
                            act.activation(kf[:, :], p_f[:, 0, :], ACT.Copy).then_inc(s_kf, 1)
                        if slot == SLOT["qkv"] + 1:
                            act.wait_ge(s_vp, front.count(1, 1))
                            wait(act, s_pv, (front - 2).count(EXPS, EXPS))
                            act.activation(vals[:, front.par, :, :, 0:HD],
                                           p_f[:, 1, :].rearrange("p (t h d) -> p t h d", t=NT, h=HEADS),
                                           ACT.Copy).then_inc(s_v, 1)
                    if tail:
                        if slot == SLOT["turnY"]:
                            act.wait_ge(s_yTp, tail.count(1, 1))
                            act.activation(y_T[:, :], p_exp[:, 0, :], ACT.Copy).then_inc(s_yT, 1)
                        if slot == SLOT["relu4"]:
                            act.wait_ge(s_tshift, tail.count(1, 1))
                            relu_norm(t_h, x3, t_rstd, t_shift).then_inc(s_th, 1)
                        if slot == SLOT["turn4"]:
                            act.wait_ge(s_tturn, tail.count(1, 1))
                            act.activation(t_hT[:, :], p_conv[:, :], ACT.Copy).then_inc(s_thT, 1)
                        if slot == SLOT["conv1"]:
                            act.wait_ge(s_c1, tail.count(1, 1))
                            act.activation(conv_in[:, PAD:PAD + N], p_conv[:, :], ACT.Relu, bias=bn_shift[:, 0:1],
                                           scale=bn_scale[:, 0:1]).then_inc(s_cin, 1)
                        for half in range(2):
                            if slot == SLOT["dist"] + half:
                                act.wait_ge(s_dp, tail.count(2, half + 1))
                                wait(act, s_np, tail.count(1))
                                for t in (2 * half, 2 * half + 1):
                                    act.activation(near[:, t, :], p_exp[:, t % 2, :], ACT.Exp,
                                                   bias=sq[:, t:t + 1]).then_inc(s_near, 1)
                        if slot == SLOT["nmpT"]:
                            act.wait_ge(s_np, tail.count(1, 1))
                            act.activation(nmp_T[:, :], p_out[:, :], ACT.Copy).then_inc(s_nmp, 1)
                        if slot == SLOT["gates"]:
                            act.wait_ge(s_gr, tail.count(1, 1))
                            act.activation(t_r[:, :], p_max[:, 0, :], ACT.Tanh, bias=gate_bias[:, 0:1],
                                           scale=0.5).then_inc(s_tr, 1)
                        if slot == SLOT["gates"] + 1:
                            act.wait_ge(s_gz, tail.count(1, 1))
                            act.activation(t_z[:, :], p_max[:, 1, :], ACT.Tanh, bias=gate_bias[:, 1:2],
                                           scale=0.5).then_inc(s_tz, 1)
                        if slot == SLOT["gates"] + 2:
                            act.wait_ge(s_gh, tail.count(1, 1))
                            act.activation(h_n[:, :], p_conv[:, :], ACT.Identity, bias=gate_bias[:, 2:3],
                                           scale=0.5).then_inc(s_hn, 1)
                        if slot == SLOT["gates"] + 4:
                            act.wait_ge(s_ni, tail.count(1, 1))
                            act.activation(n_T[:, :], h_n[:, :], ACT.Tanh, bias=par[:, BIH + 2:BIH + 3]).then_inc(s_n, 1)

            pipeline(act, iteration)

        @block.tensor
        def _(pe):
            pe.wait_ge(s_bn, 3)
            pe.wait_ge(s_const, N_CONST)

            def turn(dst, src):
                for t in range(NT):
                    last = pe.transpose(dst[:, t * P:t * P + P], src(t), ident[:, :])
                return last

            def max_scores(att, k):
                h, half = k // 2, k % 2
                wait(pe, s_mx, att.count(MAXES, k))
                for b in range(2):
                    qb = 2 * half + b
                    last = pe.matmul(p_max[:, b, :], q_st[0:SCORE_ROWS, att.par, h, qb * P:qb * P + P],
                                     k_st[0:SCORE_ROWS, att.par, h, :], start=True, stop=True)
                last.then_inc(s_mp, 1)

            def exp_scores(att, k):
                group, u = k // 8, k % 8
                t = u // 2
                wait(pe, s_e, att.count(EXPS, k))
                for b, h in enumerate(head_rows(u, group)):
                    last = pe.matmul(p_exp[:, b, :], k_st[0:SCORE_ROWS + MAX_ROWS, att.par, h, t * P:t * P + P],
                                     q_st[0:SCORE_ROWS + MAX_ROWS, att.par, h, :], start=True, stop=True)
                last.then_inc(s_ep, 1)

            def use_probs(att, k):
                group, u = k // 8, k % 8
                t = u // 2
                pe.wait_ge(s_pr, att.count(EXPS, k + 1))
                if u == 0:
                    wait(pe, s_oT, att.count(2, group))
                for b, h in enumerate(head_rows(u, group)):
                    j = h % 4
                    last = pe.matmul(p_out[HW * j:HW * j + HW, :], vals[:, att.par, t, h, :], pr[:, k % 3, b, :],
                                     start=(t == 0), stop=(t == NT - 1), skip_group_check=True)
                last.then_inc(s_pv, 1)

            def iteration(front, att, tail):
                for slot in range(SLOTS):
                    if att:
                        for group in range(2):
                            k = slot - SLOT[f"max{group}"]
                            if 0 <= k < MAXES // 2:
                                if k == 0 and group == 0:
                                    pe.wait_ge(s_qst[att.par], att.loads() * SPLITS)
                                    pe.wait_ge(s_kst[att.par], att.loads() * SPLITS)
                                    wait(pe, s_ni, (att - 1).count(1))
                                    wait(pe, s_tz, (att - 1).count(1))
                                if k == 0 and group == 1:
                                    pe.wait_ge(s_mpart, att.count(10, 1))
                                max_scores(att, k + group * MAXES // 2)
                            if slot == SLOT[f"maxT{group}"]:
                                pe.wait_ge(s_mx, att.count(MAXES, (group + 1) * MAXES // 2))
                                pe.transpose(p_max[0:16, 0, 0:P],
                                             maxes[:, 4 * group:4 * group + 4, :].rearrange("p h t -> p (h t)"),
                                             ident[:, :]).then_inc(s_mT, 1)
                            k = slot - SLOT[f"exp{group}"]
                            if 0 <= k < EXPS // 2:
                                if k == 0:
                                    pe.wait_ge(s_mrow[group], att.count(16 * MAX_ROWS, 16 * MAX_ROWS))
                                if k == 0 and group == 0 and tail:
                                    pe.wait_ge(s_near, tail.count(NT, NT))
                                exp_scores(att, k + group * EXPS // 2)
                            if 1 <= k < EXPS // 2 + 1:
                                if k == 1 and group == 0 and tail:
                                    pe.wait_ge(s_nmp, tail.count(1, 1))
                                if k == 1 and group == 0:
                                    pe.wait_ge(s_v, att.count(1, 1))
                                use_probs(att, k - 1 + group * EXPS // 2)
                    if front:
                        if slot == SLOT["turn0"]:
                            pe.wait_ge(s_fh, front.count(3, 1))
                            wait(pe, s_kf, front.count(1))
                            wait(pe, s_v, front.count(1))
                            turn(p_f[:, 0, :], lambda t: f_h[:, t, :]).then_inc(s_fturn, 1)
                        if slot == SLOT["seq"]:
                            pe.wait_ge(s_fhT, front.count(3, 1))
                            for t in range(NT):
                                last = pe.matmul(p_f[:, 1, t * P:t * P + P], f_hT[:, t * P:t * P + P], wt[:, W0, :],
                                                 start=True, stop=True)
                            last.then_inc(s_seqp, 1)
                        for half in range(2):
                            if slot == SLOT["agg"] + half:
                                pe.wait_ge(s_seq, front.count(1, 1))
                                pe.wait_ge(s_adj[front.par], front.loads())
                                for i in (2 * half, 2 * half + 1):
                                    for t in range(NT):
                                        last = pe.matmul(p_f4[:, i, 0:D + 1], adj_T[:, front.par, t, i * P:i * P + P],
                                                         seq[:, t, :], start=(t == 0), stop=(t == NT - 1))
                                if half:
                                    last.then_inc(s_agg, 1)
                        if slot == SLOT["turn2"]:
                            pe.wait_ge(s_fz, front.count(1, 1))
                            pe.wait_ge(s_din, front.count(1, 1))
                            turn(p_f[:, 0, :], lambda t: f_z[:, t, :]).then_inc(s_fturn, 1)
                        if slot == SLOT["uv"]:
                            pe.wait_ge(s_fhT, front.count(3, 2))
                            for t in range(NT):
                                last = pe.matmul(p_f4[:, t, :], f_hT[:, t * P:t * P + P],
                                                 w_lap[:, :, :].rearrange("p a n -> p (a n)"), start=True, stop=True)
                            last.then_inc(s_uv, 1)
                        for half in range(2):
                            if slot == SLOT["lap"] + half:
                                pe.wait_ge(s_vl, front.count(1, 1))
                                for i in (2 * half, 2 * half + 1):
                                    for t in range(NT):
                                        last = pe.matmul(p_f[:, 0, i * P:i * P + P],
                                                         adj_T[:, front.par, t, i * P:i * P + P], u_scaled[:, t, :],
                                                         start=(t == 0), stop=(t == NT - 1))
                                if half:
                                    last.then_inc(s_lap, 1)
                        if slot == SLOT["turn3"]:
                            pe.wait_ge(s_fh, front.count(3, 3))
                            pe.wait_ge(s_rl, front.count(1, 1))
                            turn(p_f[:, 0, :], lambda t: f_h[:, t, :]).then_inc(s_fturn, 1)
                        if slot == SLOT["qkv"]:
                            pe.wait_ge(s_fhT, front.count(3, 3))
                            pe.matmul(p_f[:, 1, :], wt[:, WQ, :], f_hT[:, :], start=True, stop=True).then_inc(s_qp, 1)
                            pe.matmul(p_f[:, 0, :], wt[:, WK, :], f_hT[:, :], start=True, stop=True).then_inc(s_kp, 1)
                        if slot == SLOT["qkv"] + 1:
                            pe.wait_ge(s_qf, front.count(1, 1))
                            for t in range(NT):
                                last = pe.matmul(p_f[:, 1, t * P:t * P + P], f_hT[:, t * P:t * P + P], wt[:, WV, :],
                                                 start=True, stop=True)
                            last.then_inc(s_vp, 1)
                    if tail:
                        if slot == SLOT["outT"]:
                            pe.wait_ge(s_oT, tail.count(2, 2))
                            for group in range(2):
                                last = turn(p_exp[:, group, :], lambda t: o_T[:, group, t * P:t * P + P])
                            last.then_inc(s_on, 1)
                        if slot == SLOT["turnY"]:
                            pe.wait_ge(s_y, tail.count(1, 1))
                            turn(p_exp[:, 0, :], lambda t: y[:, t, :]).then_inc(s_yTp, 1)
                        if slot == SLOT["proj"]:
                            pe.wait_ge(s_yT, tail.count(1, 1))
                            for t in range(NT):
                                last = pe.matmul(p_exp[:, 1, t * P:t * P + P], y_T[:, t * P:t * P + P], wt[:, WO, :],
                                                 start=True, stop=True)
                            last.then_inc(s_pj, 1)
                        if slot == SLOT["turn4"]:
                            pe.wait_ge(s_th, tail.count(1, 1))
                            wait(pe, s_x4, tail.count(1))
                            turn(p_conv[:, :], lambda t: t_h[:, t, :]).then_inc(s_tturn, 1)
                        if slot == SLOT["conv1"]:
                            pe.wait_ge(s_thT, tail.count(1, 1))
                            pe.matmul(p_conv[:, :], wt[:, WC1, :], t_hT[:, :], start=True, stop=True).then_inc(s_c1, 1)
                            pe.wait_ge(s_x3, tail.count(1, 1))
                            for t in range(NT):
                                last = pe.matmul(p_e4[:, t, 0:D + NSE], t_hT[:, t * P:t * P + P], w_emb[:, :],
                                                 start=True, stop=True)
                            last.then_inc(s_embp, 1)
                        k = slot - SLOT["conv2"]
                        if 0 <= k < TAPS:
                            if k == 0:
                                pe.wait_ge(s_cin, tail.count(1, 1))
                            mm = pe.matmul(p_conv[:, :], w_conv2[:, k, :], conv_in[:, k:k + N],
                                           start=(k == 0), stop=(k == TAPS - 1))
                            if k == TAPS - 1:
                                mm.then_inc(s_c2, 1)
                        if slot == SLOT["turnE"]:
                            pe.wait_ge(s_sc, tail.count(10, 9))
                            for side, tile in enumerate((dl, dr)):
                                for t in range(NT):
                                    last = pe.transpose(p_exp[:, side, t * P // 2:(t + 1) * P // 2].bitcast(BF16),
                                                        tile[:, t, :], ident_b[:, :])
                            last.then_inc(s_dT, 1)
                        for half in range(2):
                            if slot == SLOT["dist"] + half:
                                pe.wait_ge(s_dc, tail.count(1, 1))
                                wait(pe, s_near, tail.count(NT, 2 * half))
                                for t in (2 * half, 2 * half + 1):
                                    last = pe.matmul(p_exp[:, t % 2, :], dl_T[:, t * P:t * P + P], dr_T[:, :],
                                                     start=True, stop=True)
                                last.then_inc(s_dp, 1)
                        if SLOT["nmp"] <= slot < SLOT["nmp"] + 2:
                            for t in (2 * (slot - SLOT["nmp"]), 2 * (slot - SLOT["nmp"]) + 1):
                                pe.wait_ge(s_nm, tail.count(NT, t + 1))
                                if t == 0:
                                    pe.wait_ge(s_msg, tail.count(1, 1))
                                mm = pe.matmul(p_out[:, :], msg[:, t, :], near[:, t, :], start=(t == 0),
                                               stop=(t == NT - 1))
                            if t == NT - 1:
                                mm.then_inc(s_np, 1)
                        def gate(dst, cols, parts):
                            for n, (k, rhs) in enumerate(parts):
                                last = pe.matmul(dst, w_gru[:, k, cols * D:cols * D + D], rhs[:, :], start=(n == 0),
                                                 stop=(n == len(parts) - 1))
                            return last

                        x_parts = [(1, nmp_T), (0, xconv_T)]
                        if slot == SLOT["gru"]:
                            if att:
                                pe.wait_ge(s_mpart, att.count(10, 6))
                            pe.wait_ge(s_nmp, tail.count(1, 1))
                            pe.wait_ge(s_xc, tail.count(1, 1))
                            gate(p_max[:, 0, :], 0, [(2, t_hT)] + x_parts).then_inc(s_gr, 1)
                        if slot == SLOT["gru"] + 1:
                            gate(p_max[:, 1, :], 1, [(2, t_hT)] + x_parts).then_inc(s_gz, 1)
                        if slot == SLOT["gru"] + 2:
                            gate(p_conv[:, :], 2, [(2, t_hT)]).then_inc(s_gh, 1)
                        if slot == SLOT["gru"] + 3:
                            pe.wait_ge(s_tr, tail.count(1, 1))
                            gate(p_max[:, 0, :], 2, x_parts).then_inc(s_gn, 1)
                        if slot == SLOT["back"]:
                            pe.wait_ge(s_new, tail.count(1, 1))
                            turn(p_conv[:, :], lambda t: new_T[:, t * P:t * P + P]).then_inc(s_nb, 1)

            pipeline(pe, iteration)


def kernel(**inputs):
    import numpy as np
    import concourse.bacc as bacc
    from concourse.bass_utils import run_bass_kernel_spmd

    a = {k: np.asarray(v) for k, v in inputs.items()}
    f = np.float32
    ih, hh = a["L3_gnn_w_ih"], a["L3_gnn_w_hh"]
    blocks = [a["L0_gnn_W"], a["L1_gnn_W_self"], a["L1_gnn_W_neigh"], a["L2_gnn_Wq"].T, a["L2_gnn_Wk"].T,
              a["L2_gnn_Wv"].T, a["L2_gnn_Wo"].T, a["L3_gnn_conv1_w"][:, :, 0].T, a["L3_gnn_w_msg"].T]
    blocks += [ih[k * D:k * D + D, 0:D].T for k in range(3)]
    blocks += [ih[k * D:k * D + D, D:2 * D].T for k in range(3)]
    blocks += [hh[k * D:k * D + D, :].T for k in range(3)]
    rows = np.concatenate([np.broadcast_to(v, (P, v.size)) for v in (
        a["L0_gnn_bias"], a["L2_gnn_bo"], a["L3_gnn_b_msg"], a["L3_gnn_b_se"])] + [a["L3_gnn_w_se"].T], axis=1)
    params = np.stack([a["L1_gnn_gamma"], a["L1_gnn_beta"], np.broadcast_to(a["L0_gnn_prelu_a"], (P,)),
                       a["L3_gnn_bn1_g"], a["L3_gnn_bn1_b"], a["L3_gnn_bn1_m"], a["L3_gnn_bn1_v"],
                       a["L3_gnn_bn2_g"], a["L3_gnn_bn2_b"], a["L3_gnn_bn2_m"], a["L3_gnn_bn2_v"],
                       *a["L3_gnn_b_ih"].reshape(3, D), *a["L3_gnn_b_hh"].reshape(3, D)], axis=1)
    arrays = {
        "x": a["x"],
        "adj_t": np.transpose(a["adj"], (0, 2, 1)),
        "weights": np.stack(blocks),
        "rows": rows,
        "params": params,
        "conv2": np.transpose(a["L3_gnn_conv2_w"], (2, 1, 0)),
    }
    arrays = {k: np.ascontiguousarray(v) for k, v in arrays.items()}
    nc = bacc.Bacc("TRN2", target_bir_lowering=False, num_devices=1)
    args = [nc.dram_tensor(k, v.shape, mybir.dt.from_np(v.dtype), kind="ExternalInput").ap()
            for k, v in arrays.items()]
    out = nc.dram_tensor("out", (B, N, D), F32, kind="ExternalOutput").ap()
    build(nc, *args, out)
    r = run_bass_kernel_spmd(nc, [arrays], core_ids=[0])
    return r.results[0]["out"]
```

```python
from contextlib import ExitStack

import concourse.bass as bass
from concourse import mybir

F32 = mybir.dt.float32
BF16 = mybir.dt.bfloat16
F32R = mybir.dt.float32r
ALU = mybir.AluOpType
ACT = mybir.ActivationFunctionType
AX = mybir.AxisListType

P = 128
B, N, D = 16, 512, 128
NT = N // P
HEADS, HD = 8, 16
HW = 32
TAPS = 17
PAD = TAPS // 2
EPS = 1e-5
ADJ_EPS = 1e-6
Q_PARTS = [0, 0, 1, 0, 2, 1]
K_PARTS = [0, 1, 0, 2, 0, 1]
SPLITS = len(Q_PARTS)
SCORE_ROWS = SPLITS * HD
MAX_ROWS = 3
NSE = 3
DIST_SQ = SPLITS * NSE

(GAMMA, BETA, PRELU, BN1G, BN1B, BN1M, BN1V, BN2G, BN2B, BN2M, BN2V, BIH, BHH) = (
    0, 1, 2, 3, 4, 5, 6, 7, 8, 9, 10, 11, 14)
NPAR = 17

SLOTS = 55
MAXES = 16
EXPS = 16
RING = 6
SLOT = dict(
    outcopy0=38, outcopy1=50, turnM0=11, splitM0=14, turnM1=27, splitM1=27,
    stats0=40, rstd0=42, shift0=44, relu0=45,
    turn0=0, hT0=0, seq=2, seqcopy=0, gcn=7, neg=8, degpow=8, x1=9, degrs=11, stats1=10, rstd1=9,
    shift1=11, relu1=13, stats2=14, rstd2=14, scale2=14, turn2=17, xnT=15, uv=18, uscale=18, vcopy=21,
    softin=25, soft=27, x2=29, x2b=29, stats3=29, rstd3=29, shift3=30, relu3=31, turn3=35, hT3=35,
    qk=37, qkcopy=37, v=38, vcopy3=39, qsplit=38, ksplit=36,
    outT=1, norm=1, turnY=3, yT=5, proj=4, x3=4, stats4=6, rstd4=6, shift4=7, relu4=8, turn4=9, hT4=11,
    conv1=12, conv1relu=13, convsplit=14, emb=14, msg=13, parts=14, turnE=15, copyE=16,
    nmpT=22, xconv=28, xrelu=28, grur=32, gruz=29, gruh=35, gater=35, gatez=31,
    gateh=35, grun=37, nin=38, nact=40, new=40, back=42, x4=43,
)
STEPS = dict(
    max=(1, 2, 4, 5, 7, 8, 9, 11, 15, 16, 18, 19, 21, 22, 24, 25),
    exp=(23, 24, 26, 27, 29, 30, 32, 33, 35, 36, 38, 39, 41, 42, 44, 45),
    probs=(24, 25, 27, 28, 30, 31, 33, 34, 36, 37, 39, 40, 42, 44, 45, 46),
    use=(27, 28, 30, 31, 33, 34, 36, 37, 39, 40, 42, 43, 45, 46, 48, 49),
    agg=(4, 6, 7, 7),
    lap=(23, 24, 25, 25),
    conv2=(13, 14, 15, 15, 17, 18, 19, 20, 21, 22, 22, 24, 25, 26, 27, 28, 28),
    colsum=(6, 6, 6, 8),
    dist=(18, 21),
    near=(22, 22),
    mask=(19, 19, 20, 21),
    nmp=(21, 22, 22, 22),
)


def due(slot, step):
    return [k for k, at in enumerate(STEPS[step]) if at == slot]


class Graph:

    def __init__(self, c, turn=None):
        self.c, self.turn = c, turn
        self.par = c % 2

    def __add__(self, k):
        return Graph(self.c + k, self.turn)

    def __sub__(self, k):
        return Graph(self.c - k, self.turn)

    def index(self):
        return self.c if self.turn is None else self.turn * 2 + self.c

    def count(self, per, k=0):
        first = per * self.c + k
        if self.turn is None:
            return max(first, 0)
        assert first > 0
        return self.turn * (2 * per) + first

    def loads(self, k=1):
        half = self.c // 2 + k
        if self.turn is None:
            return max(16 * half, 0)
        assert half > 0
        return self.turn * 16 + 16 * half


def is_first(graph):
    return graph is not None and graph.turn is None and graph.c == 0


def wait(eng, sem, value):
    if isinstance(value, int) and value <= 0:
        return
    eng.wait_ge(sem, value)


def wait_alone(eng, sem, value, passed):
    if isinstance(value, int) and value <= 0:
        return
    eng.wait_ge(sem, value)
    eng.sem_inc(passed, 1)


def pipeline(eng, iteration):
    iteration(Graph(0), None, None, None)
    iteration(Graph(1), Graph(0), None, None)
    iteration(Graph(2), Graph(1), Graph(0), None)
    iteration(Graph(3), Graph(2), Graph(1), Graph(0))
    with eng.Fori(0, (B - 4) // 2) as turn:
        iteration(Graph(4, turn), Graph(3, turn), Graph(2, turn), Graph(1, turn))
        iteration(Graph(5, turn), Graph(4, turn), Graph(3, turn), Graph(2, turn))
    iteration(None, Graph(B - 1), Graph(B - 2), Graph(B - 3))
    iteration(None, None, Graph(B - 1), Graph(B - 2))
    iteration(None, None, None, Graph(B - 1))


def build(nc, x, adj_t, weights, rows, params, conv2, out):
    ctx = ExitStack()
    with ctx:
        def sb(name, shape, dt=F32):
            return ctx.enter_context(nc.sbuf_tensor(name, shape, dt))

        def ps(name, shape):
            return ctx.enter_context(nc.psum_tensor(name, shape, F32))

        def sem(name):
            return ctx.enter_context(nc.semaphore(name))

        wt = sb("wt", [P, 6, D])
        w_lap = sb("w_lap", [P, 2, D])
        w_self = sb("w_self", [P, D])
        w_emb = sb("w_emb", [P, D + NSE])
        w_gru = sb("w_gru", [P, 3, 3 * D])
        w_conv2h = sb("w_conv2h", [P, TAPS, D], F32R)
        w_conv2l = sb("w_conv2l", [P, TAPS, D], F32R)
        row = sb("row", [P, 3 * D + NSE])
        par = sb("par", [P, NPAR])
        bn_scale = sb("bn_scale", [P, 2])
        bn_shift = sb("bn_shift", [P, 2])
        bn_tmp = sb("bn_tmp", [P, 2])
        gate_bias = sb("gate_bias", [P, 3])
        half_pow = sb("half_pow", [P, 2 * NT])
        neg_slope = sb("neg_slope", [P, 1])
        one_col = sb("one_col", [P, 1])
        ident = sb("ident", [P, P])
        ident_b = sb("ident_b", [P, P], BF16)

        x_in = sb("x_in", [P, 2, NT, D])
        adj_T = sb("adj_T", [P, 2, NT, N])
        f_stat = sb("f_stat", [P, NT, 6])
        f_mom = sb("f_mom", [P, NT, 2])
        f_var = sb("f_var", [P, NT])
        f_rstd = sb("f_rstd", [P, NT])
        f_shift = sb("f_shift", [P, NT])
        f_h = sb("f_h", [P, NT, D])
        f_z = sb("f_z", [P, NT, D])
        f_hT = sb("f_hT", [P, N])
        seq = sb("seq", [P, NT, D + 1])
        gcn_pre = sb("gcn_pre", [P, NT, D])
        x1 = sb("x1", [P, NT, D])
        deg = sb("deg", [P, 2, NT])
        deg_nz = sb("deg_nz", [P, 2 * NT])
        deg_floor = sb("deg_floor", [P, 2 * NT])
        deg_pow = sb("deg_pow", [P, 2 * NT])
        deg_rs = sb("deg_rs", [P, 2, NT])
        u_scaled = sb("u_scaled", [P, NT, D])
        v_lap = sb("v_lap", [P, NT, D])
        pre = sb("pre", [P, NT, D])
        soft = sb("soft", [P, NT, D])
        junk = [tile[:, half:half + 2, :].rearrange("p t d -> p (t d)").bitcast(BF16)
                for tile in (soft, pre) for half in (0, 2)]
        x2 = sb("x2", [P, NT, D])
        x2b = sb("x2b", [P, 2, NT, D])
        qf = sb("qf", [P, N])
        kf = sb("kf", [P, N])
        q_part = sb("q_part", [P, 3, N], BF16)
        k_part = sb("k_part", [P, 3, N], BF16)
        q_st = sb("q_st", [P, 2, HEADS, N], BF16)
        k_st = sb("k_st", [P, 2, HEADS, N], BF16)
        vals = sb("vals", [P, 2, NT, HEADS, HW])
        maxes = sb("maxes", [P, HEADS, NT])
        neg_max = sb("neg_max", [HEADS // 2 * NT, 2, P])
        max_part = sb("max_part", [HEADS // 2 * NT, 2, 3, P], BF16)
        pr = sb("pr", [P, RING, 2, N])
        o_T = sb("o_T", [P, 2, N])
        r_sum = sb("r_sum", [P, 2, NT, 4])
        y = sb("y", [P, NT, D])
        x3 = sb("x3", [P, NT, D])
        t_stat = sb("t_stat", [P, NT, 6])
        t_mom = sb("t_mom", [P, NT, 2])
        t_var = sb("t_var", [P, NT])
        t_rstd = sb("t_rstd", [P, NT])
        t_shift = sb("t_shift", [P, NT])
        t_h = y
        t_hT = sb("t_hT", [P, N])
        conv_h = sb("conv_h", [P, N + 2 * PAD], F32R)
        conv_l = sb("conv_l", [P, N + 2 * PAD], F32R)
        emb = sb("emb", [P, NT, D + NSE])
        msg = sb("msg", [P, NT, D])
        s_rest = sb("s_rest", [P, 2, NT, NSE])
        s_sq = sb("s_sq", [P, NT, NSE])
        sq = sb("sq", [P, NT])
        nsq = sb("nsq", [P, NT])
        sq_rest = sb("sq_rest", [P, 2, NT])
        dl = sb("dl", [P, NT, P], BF16)
        dr = sb("dr", [P, NT, P], BF16)
        dl_T = sb("dl_T", [P, N], BF16)
        dr_T = sb("dr_T", [P, N], BF16)
        mask_T = sb("mask_T", [P, NT, N])
        near = sb("near", [P, NT, N])
        nmp_T = sb("nmp_T", [P, N])
        y_T = nmp_T
        xconv_T = sb("xconv_T", [P, N])
        t_r = sb("t_r", [P, N])
        t_z = sb("t_z", [P, N])
        h_n = sb("h_n", [P, N])
        n_T = sb("n_T", [P, N])
        new_T = sb("new_T", [P, N])

        w_conv2 = pr[:, :, :, :].rearrange("p a b n -> p (a b n)")[:, 0:TAPS * D].rearrange("p (k n) -> p k n", n=D)

        q_dram = nc.dram_tensor("q_dram", [2, 3, P, N], BF16).ap()
        k_dram = nc.dram_tensor("k_dram", [2, 3, P, N], BF16).ap()

        p_max = ps("p_max", [P, 2, N])
        p_exp = ps("p_exp", [P, 2, N])
        p_out = ps("p_out", [P, N])
        p_conv = ps("p_conv", [P, N])
        p_f = ps("p_f", [P, 2, N])
        p_f4 = p_f[:, :, :].rearrange("p a (b n) -> p (a b) n", b=2)
        p_e4 = p_exp[:, :, :].rearrange("p a (b n) -> p (a b) n", b=2)

        s_weights = sem("weights_loaded")
        s_tail_weights = sem("tail_weights_loaded")
        s_wlap = sem("laplacian_weights_ready")
        s_const = sem("constants_ready")
        s_bn = sem("bn_folded")
        s_slope = sem("slope_negated")
        s_bnv = sem("bn_var")
        s_x = [sem("x_loaded0"), sem("x_loaded1")]
        s_adj = [sem("adj_loaded0"), sem("adj_loaded1")]
        s_mask = sem("mask_loaded")
        s_fstat = sem("f_stats")
        s_fmom = sem("f_moments")
        s_fvar = sem("f_var_eps")
        s_frstd = sem("f_rstd")
        s_fshift = sem("f_shift")
        s_fh = sem("f_relu_h")
        s_fz = sem("f_scaled_z")
        s_fturn = sem("f_turned")
        s_fhT = sem("f_turned_copied")
        s_seqp = sem("seq_product")
        s_seq = sem("seq_ready")
        s_agg = sem("adj_seq_product")
        s_gpre = sem("gcn_pre")
        s_gneg = sem("gcn_negative_part")
        s_gact = sem("gcn_positive_part")
        s_x1 = sem("x1_ready")
        s_dout = sem("column_sums")
        s_din = sem("row_sums")
        s_dfl = sem("degree_floor")
        s_dpow = sem("degree_pow")
        s_drs = sem("degree_rsqrt")
        s_uv = sem("uv_product")
        s_us = sem("u_scaled_ready")
        s_vl = sem("v_copied")
        s_lap = sem("laplacian_product")
        s_pre = sem("softplus_in_negated")
        s_abs = sem("softplus_abs")
        s_se = sem("softplus_exp")
        s_sl = sem("softplus_log")
        s_sp = sem("softplus_ready")
        s_x2 = sem("x2_ready")
        s_x2b = sem("x2b_ready")
        s_qp = sem("q_product")
        s_kp = sem("k_product")
        s_vp = sem("v_product")
        s_qf = sem("q_copied")
        s_kf = sem("k_copied")
        s_v = sem("v_ready")
        s_qs = sem("q_split")
        s_ks = sem("k_split")
        s_qd = sem("q_written")
        s_kd = sem("k_written")
        s_qst = [sem("q_stacked0"), sem("q_stacked1")]
        s_kst = [sem("k_stacked0"), sem("k_stacked1")]
        s_mp = sem("max_scores")
        s_mx = sem("max_taken")
        s_mT = sem("max_turned")
        s_mpart = sem("max_split")
        s_mrow = [sem("max_rows0"), sem("max_rows1")]
        s_ep = sem("exp_scores")
        s_e = sem("exp_ready")
        s_pr = sem("probs_ready")
        s_pv = sem("probs_used")
        s_oT = sem("attention_out")
        s_on = sem("out_turned")
        s_rs = sem("row_sum_inverse")
        s_y = sem("out_normed")
        s_yTp = sem("out_turned_back")
        s_yT = sem("out_T_copied")
        s_pj = sem("projected")
        s_x3 = sem("x3_ready")
        s_tstat = sem("t_stats")
        s_tmom = sem("t_moments")
        s_tvar = sem("t_var_eps")
        s_trstd = sem("t_rstd")
        s_tshift = sem("t_shift")
        s_th = sem("t_relu_h")
        s_tturn = sem("t_turned")
        s_thT = sem("t_hT_ready")
        s_c1 = sem("conv1_product")
        s_cin = sem("conv2_in")
        s_cl = sem("conv2_in_low")
        s_c2 = sem("conv2_product")
        s_embp = sem("embedding_product")
        s_emb = sem("embedding_biased")
        s_msg = sem("messages_ready")
        s_sc = sem("embedding_split")
        s_dT = sem("distance_turned")
        s_dc = sem("distance_copied")
        s_dp = sem("distances")
        s_near = sem("near_ready")
        s_nm = sem("near_masked")
        s_np = sem("message_product")
        s_nmp = sem("nmp_ready")
        s_cs = sem("conv_summed")
        s_xc = sem("xconv_ready")
        s_gr = sem("gate_r_product")
        s_gz = sem("gate_z_product")
        s_gh = sem("gate_h_product")
        s_gn = sem("gate_n_product")
        s_tr = sem("gate_r")
        s_tz = sem("gate_z")
        s_hn = sem("gate_h")
        s_rn = sem("r_times_h")
        s_ni = sem("n_in_ready")
        s_n = sem("n_ready")
        s_hm = sem("h_minus_n_ready")
        s_zp = sem("z_part_ready")
        s_new = sem("new_state")
        s_nb = sem("new_turned_back")
        s_x4 = sem("x4_ready")
        s_passed_sp = sem("sp_waits_passed")
        s_passed_pool = sem("pool_waits_passed")
        s_passed_dve = sem("dve_waits_passed")
        s_out = [sem("stored0"), sem("stored1")]

        W0, WQ, WK, WV, WO, WC1 = range(6)
        N_WEIGHTS = 6
        N_TAIL_WEIGHTS = 2 + 2 + 3
        N_CONST = 14

        def head_rows(t, group):
            return [group * 4 + (t % 2) * 2 + b for b in range(2)]

        block = ctx.enter_context(nc.Block())

        @block.sync
        def _(sp):
            def load_front_weights():
                sp.dma_start(wt[:, 0, :], weights[0]).then_inc(s_weights, 16)
                sp.dma_start(row[:, :], rows[:, 0:3 * D + NSE]).then_inc(s_weights, 16)
                sp.dma_start(par[:, :], params).then_inc(s_weights, 16)
                sp.dma_start(w_self[:, :], weights[1]).then_inc(s_weights, 16)
                sp.dma_start(w_lap[:, 0, :], weights[2]).then_inc(s_weights, 16)
                sp.dma_start(wt[:, 1:6, :], weights[3:8].rearrange("a p n -> p a n")).then_inc(s_weights, 16)

            def load_tail_weights():
                sp.dma_start(w_conv2[:, 0:9, :], conv2[0:9].rearrange("k p n -> p k n")).then_inc(s_tail_weights, 16)
                sp.dma_start(w_conv2[:, 9:TAPS, :], conv2[9:TAPS].rearrange("k p n -> p k n")
                             ).then_inc(s_tail_weights, 16)
                sp.dma_start(w_emb[:, 0:D], weights[8]).then_inc(s_tail_weights, 16)
                sp.dma_start(w_emb[:, D:D + NSE], rows[:, 3 * D + NSE:3 * D + 2 * NSE]).then_inc(s_tail_weights, 16)
                for k in range(3):
                    sp.dma_start(w_gru[:, k, :].rearrange("p (a n) -> p a n", a=3),
                                 weights[9 + 3 * k:12 + 3 * k].rearrange("a p n -> p a n")
                                 ).then_inc(s_tail_weights, 16)

            def iteration(head, front, att, tail):
                if head:
                    wait_alone(sp, s_x1, (head - 2).count(1, 1), s_passed_sp)
                    sp.dma_start(x_in[:, head.par, :, :],
                                 x[head.index()].rearrange("(t p) d -> p t d", p=P)).then_inc(s_x[head.par], 16)
                if is_first(head):
                    load_front_weights()
                if front:
                    wait_alone(sp, s_pr, (front - 2).count(EXPS, EXPS), s_passed_sp)
                    sp.dma_start(adj_T[:, front.par, :, :],
                                 adj_t[front.index()].rearrange("(t p) n -> p t n", p=P)).then_inc(s_adj[front.par], 16)
                if is_first(front):
                    load_tail_weights()
                if tail:
                    wait_alone(sp, s_nm, tail.count(NT), s_passed_sp)
                    sp.dma_start(mask_T[:, :, :],
                                 adj_t[tail.index()].rearrange("(t p) n -> p t n", p=P)).then_inc(s_mask, 16)
                for group in range(2):
                    if att:
                        wait_alone(sp, s_mpart, att.count(10, 5 * (group + 1)), s_passed_sp)
                        for j in range(MAX_ROWS):
                            sp.dma_start(q_st[SCORE_ROWS + j:SCORE_ROWS + j + 1, att.par, 4 * group:4 * group + 4, :],
                                         max_part[:, group, j, :]).then_inc(s_mrow[group], 16)
                if front:
                    wait_alone(sp, s_qs, front.count(3, 3), s_passed_sp)
                    sp.dma_start(q_dram[front.par].rearrange("a p n -> p a n"), q_part[:, :, :]).then_inc(s_qd, 16)
                    wait_alone(sp, s_ks, front.count(3, 3), s_passed_sp)
                    sp.dma_start(k_dram[front.par].rearrange("a p n -> p a n"), k_part[:, :, :]).then_inc(s_kd, 16)
                    wait_alone(sp, s_ep, (front - 2).count(2 * EXPS, 2 * EXPS), s_passed_sp)
                    wait_alone(sp, s_qd, front.count(16, 16), s_passed_sp)
                    for s, part in enumerate(Q_PARTS):
                        sp.dma_start(q_st[HD * s:HD * s + HD, front.par, :, :],
                                     q_dram[front.par, part].rearrange("(h d) n -> d h n", d=HD)
                                     ).then_inc(s_qst[front.par], 16)
                    wait_alone(sp, s_kd, front.count(16, 16), s_passed_sp)
                    for s, part in enumerate(K_PARTS):
                        sp.dma_start(k_st[HD * s:HD * s + HD, front.par, :, :],
                                     k_dram[front.par, part].rearrange("(h d) n -> d h n", d=HD)
                                     ).then_inc(s_kst[front.par], 16)
                if tail:
                    wait_alone(sp, s_x4, tail.count(1, 1), s_passed_sp)
                    sp.dma_start(out[tail.index()].rearrange("(t p) d -> p t d", p=P),
                                 x3[:, :, :]).then_inc(s_out[tail.par], 16)

            pipeline(sp, iteration)
            for parity in range(2):
                sp.wait_ge(s_out[parity], 16 * (B // 2))

        @block.gpsimd
        def _(pool):
            pool.memset(ident[:, :], 0.0).then_inc(s_const, 1)
            pool.wait_ge(s_const, 1)
            pool.affine_select(out=ident[:, :], in_=ident[:, :], compare_op=ALU.not_equal, fill=1.0, base=0,
                               pattern=[[-1, P]], channel_multiplier=1).then_inc(s_const, 1)
            pool.wait_ge(s_const, 2)
            pool.tensor_copy(ident_b[:, :], ident[:, :]).then_inc(s_const, 1)
            pool.memset(half_pow[:, :], -0.5).then_inc(s_const, 1)
            pool.memset(one_col[:, :], 1.0).then_inc(s_const, 1)
            pool.memset(seq[:, :, D:D + 1], 1.0).then_inc(s_const, 1)
            pool.memset(vals[:, :, :, :, HD:HW], 0.0).then_inc(s_const, 1)
            pool.wait_ge(s_const, 7)
            pool.memset(vals[:, :, :, :, HD:HD + 1], 1.0).then_inc(s_const, 1)
            pool.wait_ge(s_const, 8)
            pool.memset(k_st[SCORE_ROWS:P, :, :, :], 1.0).then_inc(s_const, 1)
            pool.wait_ge(s_const, 9)
            pool.memset(conv_h[:, :].bitcast(F32), 0.0).then_inc(s_const, 1)
            pool.memset(conv_l[:, :].bitcast(F32), 0.0).then_inc(s_const, 1)
            pool.memset(dl[:, :, :], 0.0).then_inc(s_const, 1)
            pool.memset(dr[:, :, :], 0.0).then_inc(s_const, 1)
            pool.wait_ge(s_const, 13)
            pool.memset(dr[:, :, DIST_SQ:DIST_SQ + 3], 0.0).then_inc(s_const, 1)
            pool.wait_ge(s_weights, 16 * N_WEIGHTS)
            pool.tensor_tensor(w_lap[:, 1, :], w_self[:, :], w_lap[:, 0, :], ALU.add).then_inc(s_wlap, 1)
            pool.tensor_scalar(bn_tmp[:, :], par[:, BN1V:BN2V + 1:BN2V - BN1V], EPS, None, ALU.add).then_inc(s_bnv, 1)
            pool.wait_ge(s_bnv, 1)
            pool.tensor_tensor(bn_shift[:, :], bn_tmp[:, :], half_pow[:, 0:2], ALU.pow).then_inc(s_bnv, 1)

            def inverse_root(var, mom, out_, s_mom, s_var, s_rstd, value):
                wait_alone(pool, s_mom, value, s_passed_pool)
                pool.tensor_scalar(var[:, :], mom[:, :, 1], EPS, None, ALU.add).then_inc(s_var, 1)
                pool.wait_ge(s_var, value)
                pool.tensor_tensor(out_[:, :], var[:, :], half_pow[:, 0:NT], ALU.pow).then_inc(s_rstd, 1)

            def iteration(head, front, att, tail):
                for slot in range(SLOTS):
                    if head and slot == SLOT["rstd0"]:
                        inverse_root(f_var, f_mom, f_rstd, s_fmom, s_fvar, s_frstd, head.count(4, 1))
                    if front:
                        for k, step in enumerate(("rstd1", "rstd2", "rstd3")):
                            if slot == SLOT[step]:
                                inverse_root(f_var, f_mom, f_rstd, s_fmom, s_fvar, s_frstd, front.count(4, k + 2))
                        if slot == SLOT["degpow"]:
                            pool.wait_ge(s_dfl, front.count(1, 1))
                            pool.tensor_tensor(deg_pow[:, :], deg_floor[:, :], half_pow[:, :], ALU.pow
                                               ).then_inc(s_dpow, 1)
                        if slot == SLOT["scale2"]:
                            pool.wait_ge(s_frstd, front.count(4, 3))
                            wait_alone(pool, s_fturn, front.count(3), s_passed_pool)
                            for t in range(NT):
                                last = pool.tensor_scalar(f_z[:, t, :], f_h[:, t, :], f_mom[:, t, 0:1],
                                                          f_rstd[:, t:t + 1], ALU.subtract, ALU.mult)
                            last.then_inc(s_fz, 1)
                        if slot == SLOT["x2b"]:
                            pool.wait_ge(s_x2, front.count(1, 1))
                            wait(pool, s_x3, (front - 2).count(1, 1))
                            pool.tensor_tensor(x2b[:, front.par, :, :], x2[:, :, :],
                                               row[:, D:2 * D].unsqueeze(1).to_broadcast([P, NT, D]), ALU.add
                                               ).then_inc(s_x2b, 1)
                        if slot == SLOT["ksplit"]:
                            pool.wait_ge(s_kf, front.count(1, 1))
                            pool.tensor_tensor(kf[:, :], kf[:, :], k_part[:, 0, :], ALU.subtract).then_inc(s_ks, 1)
                            wait_alone(pool, s_ks, front.count(3, 1), s_passed_pool)
                            pool.tensor_scalar(k_part[:, 1, :], kf[:, :], 1.0, None, ALU.mult).then_inc(s_ks, 1)
                            pool.wait_ge(s_ks, front.count(3, 2))
                            pool.tensor_tensor(k_part[:, 2, :], kf[:, :], k_part[:, 1, :], ALU.subtract
                                               ).then_inc(s_ks, 1)
                    if tail:
                        if slot == SLOT["rstd4"]:
                            inverse_root(t_var, t_mom, t_rstd, s_tmom, s_tvar, s_trstd, tail.count(1, 1))
                        for t in due(slot, "mask"):
                            pool.wait_ge(s_mask, tail.count(16, 16))
                            pool.wait_ge(s_near, tail.count(NT, t + 1))
                            pool.tensor_tensor(near[:, t, :], near[:, t, :], mask_T[:, t, :], ALU.mult
                                               ).then_inc(s_nm, 1)

            pipeline(pool, iteration)

        @block.vector
        def _(dve):
            dve.wait_ge(s_weights, 16 * N_WEIGHTS)
            dve.tensor_scalar(neg_slope[:, :], par[:, PRELU:PRELU + 1], -1.0, None, ALU.mult).then_inc(s_slope, 1)
            dve.wait_ge(s_const, N_CONST)

            def fold_parameters():
                dve.wait_ge(s_bnv, 2)
                dve.tensor_tensor(bn_scale[:, :], bn_shift[:, :], par[:, BN1G:BN2G + 1:BN2G - BN1G], ALU.mult).then_inc(s_bnv, 1)
                dve.wait_ge(s_bnv, 3)
                dve.tensor_tensor(bn_tmp[:, :], bn_scale[:, :], par[:, BN1M:BN2M + 1:BN2M - BN1M], ALU.mult).then_inc(s_bnv, 1)
                dve.wait_ge(s_bnv, 4)
                dve.tensor_tensor(bn_shift[:, :], par[:, BN1B:BN2B + 1:BN2B - BN1B], bn_tmp[:, :], ALU.subtract).then_inc(s_bn, 1)
                dve.tensor_tensor(gate_bias[:, 0:2], par[:, BIH:BIH + 2], par[:, BHH:BHH + 2], ALU.add).then_inc(s_bnv, 1)
                dve.tensor_copy(gate_bias[:, 2:3], par[:, BHH + 2:BHH + 3]).then_inc(s_bnv, 1)
                dve.wait_ge(s_bnv, 6)
                dve.tensor_scalar(gate_bias[:, :], gate_bias[:, :], 0.5, None, ALU.mult).then_inc(s_bn, 1)
                dve.wait_ge(s_tail_weights, 16 * N_TAIL_WEIGHTS)
                dve.tensor_copy(w_conv2h[:, :, :], w_conv2).then_inc(s_bnv, 1)
                dve.wait_ge(s_bnv, 7)
                dve.tensor_tensor(w_conv2l[:, :, :], w_conv2, w_conv2h[:, :, :].bitcast(F32), ALU.subtract).then_inc(s_bn, 1)

            def norm_stats(src, stat, mom, s_stat, s_mom, value):
                for t in range(NT):
                    last = dve.bn_stats(stat[:, t, :], src[:, t, :])
                last.then_inc(s_stat, 1)
                wait_alone(dve, s_stat, value, s_passed_dve)
                for t in range(NT):
                    last = dve.bn_aggr(mom[:, t, :], stat[:, t, :])
                last.then_inc(s_mom, 1)

            def norm_shift(mom, rstd, shift, s_rstd, s_shift, value):
                dve.wait_ge(s_rstd, value)
                dve.scalar_tensor_tensor(out=shift[:, :], in0=mom[:, :, 0], scalar=-1.0, in1=rstd[:, :],
                                         op0=ALU.mult, op1=ALU.mult).then_inc(s_shift, 1)

            def take_max(att, k):
                h, half = k // 2, k % 2
                for b in range(2):
                    dve.wait_ge(s_mp, att.count(2 * MAXES, 2 * k + 1 + b))
                    dve.tensor_reduce(maxes[:, h, 2 * half + b:2 * half + b + 1], p_max[:, b, :], AX.X, ALU.max
                                      ).then_inc(s_mx, 1)

            def split_max(att, group):
                v = lambda k: att.count(10, 5 * group + k)
                dve.wait_ge(s_mT, att.count(2, group + 1))
                wait(dve, s_mrow[group], att.count(16 * MAX_ROWS))
                nm, part = neg_max[:, group, :], max_part[:, group, :, :]
                dve.tensor_scalar(nm, p_max[0:16, 0, 0:P], -1.0, None, ALU.mult).then_inc(s_mpart, 1)
                dve.wait_ge(s_mpart, v(1))
                dve.tensor_copy(part[:, 0, :], nm).then_inc(s_mpart, 1)
                dve.wait_ge(s_mpart, v(2))
                dve.tensor_tensor(nm, nm, part[:, 0, :], ALU.subtract).then_inc(s_mpart, 1)
                dve.wait_ge(s_mpart, v(3))
                dve.tensor_copy(part[:, 1, :], nm).then_inc(s_mpart, 1)
                dve.wait_ge(s_mpart, v(4))
                dve.tensor_tensor(part[:, 2, :], nm, part[:, 1, :], ALU.subtract).then_inc(s_mpart, 1)

            def probs(att, k):
                t = (k % 8) // 2
                dve.wait_ge(s_e, att.count(2 * EXPS, 2 * k + 2))
                r = k % RING
                dve.scalar_tensor_tensor(out=pr[:, r, :, :],
                                         in0=adj_T[:, att.par, t, :].unsqueeze(1).to_broadcast([P, 2, N]),
                                         scalar=ADJ_EPS, in1=pr[:, r, :, :], op0=ALU.add, op1=ALU.mult
                                         ).then_inc(s_pr, 1)

            def iteration(head, front, att, tail):
                for slot in range(SLOTS):
                    if slot == SLOTS - 1 and is_first(front):
                        fold_parameters()
                    if att:
                        for k in due(slot, "max"):
                            take_max(att, k)
                        for group in range(2):
                            if slot == SLOT[f"splitM{group}"]:
                                split_max(att, group)
                        for k in due(slot, "probs"):
                            probs(att, k)
                    if head:
                        if slot == SLOT["stats0"]:
                            dve.wait_ge(s_x[head.par], head.loads())
                            norm_stats(x_in[:, head.par], f_stat, f_mom, s_fstat, s_fmom, head.count(4, 1))
                        if slot == SLOT["shift0"]:
                            norm_shift(f_mom, f_rstd, f_shift, s_frstd, s_fshift, head.count(4, 1))
                    if front:
                        if slot == SLOT["gcn"]:
                            dve.wait_ge(s_agg, front.count(1, 1))
                            dve.tensor_tensor(gcn_pre[:, :, :], p_f4[:, :, 0:D],
                                              row[:, 0:D].unsqueeze(1).to_broadcast([P, NT, D]), ALU.add
                                              ).then_inc(s_gpre, 1)
                            dve.tensor_copy(deg[:, 1, :], p_f4[:, :, D]).then_inc(s_din, 1)
                            dve.wait_ge(s_din, front.count(1, 1))
                            dve.wait_ge(s_dout, front.count(NT, NT))
                            degs = deg[:, :, :].rearrange("p a t -> p (a t)")
                            dve.tensor_scalar(deg_nz[:, :], degs, 0.0, None, ALU.not_equal)
                            dve.tensor_scalar(deg_floor[:, :], degs, 1e-30, None, ALU.max).then_inc(s_dfl, 1)
                        if slot == SLOT["x1"]:
                            dve.wait_ge(s_gpre, front.count(1, 1))
                            dve.scalar_tensor_tensor(out=x1[:, :, :], in0=gcn_pre[:, :, :], scalar=0.0,
                                                     in1=x_in[:, front.par, :, :], op0=ALU.max, op1=ALU.add
                                                     ).then_inc(s_gact, 1)
                            dve.wait_ge(s_slope, 1)
                            dve.wait_ge(s_gneg, front.count(1, 1))
                            dve.wait_ge(s_gact, front.count(1, 1))
                            dve.scalar_tensor_tensor(out=x1[:, :, :], in0=soft[:, :, :], scalar=neg_slope[:, :],
                                                     in1=x1[:, :, :], op0=ALU.mult, op1=ALU.add).then_inc(s_x1, 1)
                        if slot == SLOT["degrs"]:
                            dve.wait_ge(s_dpow, front.count(1, 1))
                            dve.tensor_tensor(deg_rs[:, :, :].rearrange("p a t -> p (a t)"), deg_pow[:, :],
                                              deg_nz[:, :], ALU.mult).then_inc(s_drs, 1)
                        if slot == SLOT["stats1"]:
                            dve.wait_ge(s_x1, front.count(1, 1))
                            norm_stats(x1, f_stat, f_mom, s_fstat, s_fmom, front.count(4, 2))
                        if slot == SLOT["shift1"]:
                            norm_shift(f_mom, f_rstd, f_shift, s_frstd, s_fshift, front.count(4, 2))
                        if slot == SLOT["stats2"]:
                            dve.wait_ge(s_fh, front.count(3, 2))
                            norm_stats(f_h, f_stat, f_mom, s_fstat, s_fmom, front.count(4, 3))
                        if slot == SLOT["softin"]:
                            dve.wait_ge(s_lap, front.count(1, 1))
                            dve.wait_ge(s_vl, front.count(1, 1))
                            for t in range(NT):
                                last = dve.scalar_tensor_tensor(
                                    out=pre[:, t, :], in0=p_f[:, 0, t * P:t * P + P], scalar=deg_rs[:, 0, t:t + 1],
                                    in1=v_lap[:, t, :], op0=ALU.mult, op1=ALU.subtract)
                            last.then_inc(s_pre, 1)
                        if slot == SLOT["x2"]:
                            dve.wait_ge(s_sl, front.count(1, 1))
                            dve.scalar_tensor_tensor(out=soft[:, :, :], in0=pre[:, :, :], scalar=0.0,
                                                     in1=soft[:, :, :], op0=ALU.min, op1=ALU.subtract).then_inc(s_sp, 1)
                            dve.wait_ge(s_sp, front.count(1, 1))
                            wait(dve, s_x2b, front.count(1))
                            dve.tensor_tensor(x2[:, :, :], x1[:, :, :], soft[:, :, :], ALU.subtract).then_inc(s_x2, 1)
                        if slot == SLOT["stats3"]:
                            dve.wait_ge(s_x2, front.count(1, 1))
                            norm_stats(x2, f_stat, f_mom, s_fstat, s_fmom, front.count(4, 4))
                        if slot == SLOT["shift3"]:
                            norm_shift(f_mom, f_rstd, f_shift, s_frstd, s_fshift, front.count(4, 4))
                        if slot == SLOT["qsplit"]:
                            dve.wait_ge(s_qf, front.count(1, 1))
                            dve.tensor_tensor(qf[:, :], qf[:, :], q_part[:, 0, :], ALU.subtract).then_inc(s_qs, 1)
                            dve.wait_ge(s_qs, front.count(3, 1))
                            dve.tensor_copy(q_part[:, 1, :], qf[:, :]).then_inc(s_qs, 1)
                            dve.wait_ge(s_qs, front.count(3, 2))
                            dve.tensor_tensor(q_part[:, 2, :], qf[:, :], q_part[:, 1, :], ALU.subtract
                                              ).then_inc(s_qs, 1)
                    if tail:
                        if slot == SLOT["norm"]:
                            dve.wait_ge(s_on, tail.count(1, 1))
                            o4 = p_exp[:, :, :].rearrange("p g (t j w) -> p g t j w", t=NT, j=4)
                            for g2 in range(2):
                                last = dve.reciprocal(r_sum[:, g2, :, :], o4[:, g2, :, :, HD])
                            last.then_inc(s_rs, 1)
                            dve.wait_ge(s_rs, tail.count(1, 1))
                            for g2 in range(2):
                                last = dve.tensor_tensor(
                                    y[:, :, g2 * 64:g2 * 64 + 64].rearrange("p t (j w) -> p t j w", j=4),
                                    o4[:, g2, :, :, 0:HD],
                                    r_sum[:, g2, :, :].unsqueeze(3).to_broadcast([P, NT, 4, HD]), ALU.mult)
                            last.then_inc(s_y, 1)
                        if slot == SLOT["x3"]:
                            dve.wait_ge(s_pj, tail.count(1, 1))
                            dve.wait_ge(s_x2b, tail.count(1, 1))
                            wait(dve, s_out[(tail - 1).par], (tail - 1).loads())
                            dve.tensor_tensor(x3[:, :, :], p_exp[:, 1, :].rearrange("p (t d) -> p t d", t=NT),
                                              x2b[:, tail.par, :, :], ALU.add).then_inc(s_x3, 1)
                        if slot == SLOT["stats4"]:
                            dve.wait_ge(s_x3, tail.count(1, 1))
                            norm_stats(x3, t_stat, t_mom, s_tstat, s_tmom, tail.count(1, 1))
                        if slot == SLOT["shift4"]:
                            norm_shift(t_mom, t_rstd, t_shift, s_trstd, s_tshift, tail.count(1, 1))
                        if slot == SLOT["convsplit"]:
                            dve.wait_ge(s_cin, tail.count(1, 1))
                            dve.tensor_tensor(conv_l[:, PAD:PAD + N], xconv_T[:, :],
                                              conv_h[:, PAD:PAD + N].bitcast(F32), ALU.subtract).then_inc(s_cl, 1)
                        if slot == SLOT["emb"]:
                            dve.wait_ge(s_embp, tail.count(1, 1))
                            dve.tensor_tensor(emb[:, :, :], p_e4[:, :, 0:D + NSE],
                                              row[:, 2 * D:3 * D + NSE].unsqueeze(1).to_broadcast([P, NT, D + NSE]),
                                              ALU.add).then_inc(s_emb, 1)
                        if slot == SLOT["parts"]:
                            dve.wait_ge(s_emb, tail.count(1, 1))
                            s = emb[:, :, D:D + NSE]
                            v = lambda k: tail.count(10, k)

                            def place(tile, parts, part, src, scale):
                                for n, q in enumerate(parts):
                                    if q == part:
                                        last = dve.tensor_scalar(tile[:, :, NSE * n:NSE * n + NSE], src, scale, None, ALU.mult)
                                return last

                            place(dl, Q_PARTS, 0, s, 2.0)
                            place(dr, K_PARTS, 0, s, 1.0).then_inc(s_sc, 1)
                            dve.tensor_tensor(s_sq[:, :, :], s, s, ALU.mult).then_inc(s_sc, 1)
                            dve.wait_ge(s_sc, v(2))
                            dve.tensor_tensor(s_rest[:, 0, :, :], s, dr[:, :, 0:NSE], ALU.subtract)
                            dve.tensor_reduce(nsq[:, :], s_sq[:, :, :], AX.X, ALU.add, negate=True).then_inc(s_sc, 1)
                            dve.wait_ge(s_sc, v(3))
                            place(dl, Q_PARTS, 1, s_rest[:, 0, :, :], 2.0)
                            place(dr, K_PARTS, 1, s_rest[:, 0, :, :], 1.0)
                            dve.tensor_copy(dr[:, :, DIST_SQ], nsq[:, :]).then_inc(s_sc, 1)
                            dve.wait_ge(s_sc, v(4))
                            dve.tensor_tensor(s_rest[:, 1, :, :], s_rest[:, 0, :, :], dr[:, :, NSE:2 * NSE], ALU.subtract)
                            dve.tensor_tensor(sq_rest[:, 0, :], nsq[:, :], dr[:, :, DIST_SQ], ALU.subtract).then_inc(s_sc, 1)
                            dve.wait_ge(s_sc, v(5))
                            place(dl, Q_PARTS, 2, s_rest[:, 1, :, :], 2.0)
                            place(dr, K_PARTS, 2, s_rest[:, 1, :, :], 1.0)
                            dve.tensor_copy(dr[:, :, DIST_SQ + 1], sq_rest[:, 0, :]).then_inc(s_sc, 1)
                            dve.wait_ge(s_sc, v(6))
                            dve.tensor_tensor(sq_rest[:, 1, :], sq_rest[:, 0, :], dr[:, :, DIST_SQ + 1], ALU.subtract
                                              ).then_inc(s_sc, 1)
                            dve.wait_ge(s_sc, v(7))
                            dve.tensor_copy(dr[:, :, DIST_SQ + 2], sq_rest[:, 1, :]).then_inc(s_sc, 1)
                            dve.memset(dl[:, :, DIST_SQ:DIST_SQ + 3], 1.0).then_inc(s_sc, 1)
                            dve.wait_ge(s_sc, v(9))
                            dve.tensor_copy(sq[:, :], nsq[:, :]).then_inc(s_sc, 1)
                        if slot == SLOT["xconv"]:
                            dve.wait_ge(s_c2, tail.count(1, 1))
                            dve.scalar_tensor_tensor(out=xconv_T[:, :], in0=p_conv[:, :], scalar=bn_scale[:, 1:2],
                                                     in1=t_hT[:, :], op0=ALU.mult, op1=ALU.add).then_inc(s_cs, 1)
                        if slot == SLOT["nin"]:
                            dve.wait_ge(s_hn, tail.count(1, 1))
                            dve.wait_ge(s_tr, tail.count(1, 1))
                            dve.scalar_tensor_tensor(out=h_n[:, :], in0=t_r[:, :], scalar=1.0, in1=h_n[:, :],
                                                     op0=ALU.add, op1=ALU.mult).then_inc(s_rn, 1)
                            dve.wait_ge(s_rn, tail.count(1, 1))
                            dve.wait_ge(s_gn, tail.count(1, 1))
                            dve.tensor_tensor(h_n[:, :], p_max[:, 0, :], h_n[:, :], ALU.add).then_inc(s_ni, 1)
                        if slot == SLOT["new"]:
                            dve.wait_ge(s_n, tail.count(1, 1))
                            dve.tensor_tensor(new_T[:, :], t_hT[:, :], n_T[:, :], ALU.subtract).then_inc(s_hm, 1)
                            dve.wait_ge(s_hm, tail.count(1, 1))
                            dve.scalar_tensor_tensor(out=new_T[:, :], in0=t_z[:, :], scalar=1.0, in1=new_T[:, :],
                                                     op0=ALU.add, op1=ALU.mult).then_inc(s_zp, 1)
                            dve.wait_ge(s_zp, tail.count(1, 1))
                            dve.scalar_tensor_tensor(out=new_T[:, :], in0=new_T[:, :], scalar=0.5, in1=n_T[:, :],
                                                     op0=ALU.mult, op1=ALU.add).then_inc(s_new, 1)
                        if slot == SLOT["x4"]:
                            dve.wait_ge(s_nb, tail.count(1, 1))
                            dve.tensor_tensor(x3[:, :, :], p_conv[:, :].rearrange("p (t d) -> p t d", t=NT),
                                              x3[:, :, :], ALU.add).then_inc(s_x4, 1)

            pipeline(dve, iteration)

        @block.scalar
        def _(act):
            act.wait_ge(s_weights, 16 * N_WEIGHTS)
            act.wait_ge(s_const, N_CONST)

            def relu_norm(dst, src, rstd, shift):
                for t in range(NT):
                    last = act.activation(dst[:, t, :], src[:, t, :], ACT.Relu, bias=shift[:, t:t + 1],
                                          scale=rstd[:, t:t + 1])
                return last

            def exps(att, k):
                wait(act, s_pv, att.count(EXPS, max(k + 1 - RING, 0)))
                for b in range(2):
                    act.wait_ge(s_ep, att.count(2 * EXPS, 2 * k + 1 + b))
                    act.activation(pr[:, k % RING, b, :], p_exp[:, b, :], ACT.Exp).then_inc(s_e, 1)

            def iteration(head, front, att, tail):
                for slot in range(SLOTS):
                    if slot == 0 and is_first(att):
                        act.wait_ge(s_bn, 3)
                    if att:
                        for k in due(slot, "exp"):
                            exps(att, k)
                        for group in range(2):
                            if slot == SLOT[f"outcopy{group}"]:
                                act.wait_ge(s_pv, att.count(EXPS, (group + 1) * EXPS // 2))
                                wait(act, s_on, att.count(1))
                                act.activation(o_T[:, group, :], p_out[:, :], ACT.Copy).then_inc(s_oT, 1)
                    if head and slot == SLOT["relu0"]:
                        act.wait_ge(s_fshift, head.count(3, 1))
                        wait(act, s_fturn, head.count(3))
                        relu_norm(f_h, x_in[:, head.par], f_rstd, f_shift).then_inc(s_fh, 1)
                    if front:
                        if slot == SLOT["hT0"]:
                            act.wait_ge(s_fturn, front.count(3, 1))
                            act.activation(f_hT[:, :], p_f[:, 0, :], ACT.Copy).then_inc(s_fhT, 1)
                        if slot == SLOT["seqcopy"]:
                            act.wait_ge(s_seqp, front.count(1, 1))
                            act.activation(seq[:, :, 0:D], p_f[:, 1, :].rearrange("p (t d) -> p t d", t=NT),
                                           ACT.Copy).then_inc(s_seq, 1)
                        for t in due(slot, "colsum"):
                            if t == 0:
                                act.wait_ge(s_adj[front.par], front.loads())
                            act.activation(junk[t], adj_T[:, front.par, t, :], ACT.Copy,
                                           accum_out=deg[:, 0, t:t + 1]).then_inc(s_dout, 1)
                        if slot == SLOT["neg"]:
                            act.wait_ge(s_gpre, front.count(1, 1))
                            act.wait_ge(s_dout, front.count(NT, NT))
                            act.activation(soft[:, :, :], gcn_pre[:, :, :], ACT.Relu, scale=-1.0).then_inc(s_gneg, 1)
                        if slot == SLOT["relu1"]:
                            act.wait_ge(s_fshift, front.count(3, 2))
                            relu_norm(f_h, x1, f_rstd, f_shift).then_inc(s_fh, 1)
                        if slot == SLOT["xnT"]:
                            act.wait_ge(s_fturn, front.count(3, 2))
                            act.activation(f_hT[:, :], p_f[:, 0, :], ACT.Identity, bias=par[:, BETA:BETA + 1],
                                           scale=par[:, GAMMA:GAMMA + 1]).then_inc(s_fhT, 1)
                        if slot == SLOT["uscale"]:
                            act.wait_ge(s_uv, front.count(1, 1))
                            act.wait_ge(s_drs, front.count(1, 1))
                            for t in range(NT):
                                last = act.activation(u_scaled[:, t, :], p_f4[:, t, 0:D], ACT.Copy,
                                                      scale=deg_rs[:, 1, t:t + 1])
                            last.then_inc(s_us, 1)
                        if slot == SLOT["vcopy"]:
                            act.wait_ge(s_uv, front.count(1, 1))
                            act.activation(v_lap[:, :, :], p_f4[:, :, D:2 * D], ACT.Copy).then_inc(s_vl, 1)
                        if slot == SLOT["soft"]:
                            act.wait_ge(s_pre, front.count(1, 1))
                            act.activation(soft[:, :, :], pre[:, :, :], ACT.Abs).then_inc(s_abs, 1)
                            act.wait_ge(s_abs, front.count(1, 1))
                            act.activation(soft[:, :, :], soft[:, :, :], ACT.Exp, scale=-1.0).then_inc(s_se, 1)
                            act.wait_ge(s_se, front.count(1, 1))
                            act.activation(soft[:, :, :], soft[:, :, :], ACT.Ln, bias=one_col[:, 0:1]).then_inc(s_sl, 1)
                        if slot == SLOT["relu3"]:
                            act.wait_ge(s_fshift, front.count(3, 3))
                            relu_norm(f_h, x2, f_rstd, f_shift).then_inc(s_fh, 1)
                        if slot == SLOT["hT3"]:
                            act.wait_ge(s_fturn, front.count(3, 3))
                            act.activation(f_hT[:, :], p_f[:, 0, :], ACT.Copy).then_inc(s_fhT, 1)
                        if slot == SLOT["qkcopy"]:
                            act.wait_ge(s_qp, front.count(1, 1))
                            wait(act, s_qd, front.count(16))
                            act.activation(q_part[:, 0, :], p_f[:, 1, :], ACT.Copy, scale=HD ** -0.5)
                            act.activation(qf[:, :], p_f[:, 1, :], ACT.Copy, scale=HD ** -0.5).then_inc(s_qf, 1)
                            act.wait_ge(s_kp, front.count(1, 1))
                            wait(act, s_kd, front.count(16))
                            act.activation(k_part[:, 0, :], p_f[:, 0, :], ACT.Copy)
                            act.activation(kf[:, :], p_f[:, 0, :], ACT.Copy).then_inc(s_kf, 1)
                        if slot == SLOT["vcopy3"]:
                            act.wait_ge(s_vp, front.count(1, 1))
                            wait(act, s_pv, (front - 2).count(EXPS, EXPS))
                            act.activation(vals[:, front.par, :, :, 0:HD],
                                           p_f[:, 1, :].rearrange("p (t h d) -> p t h d", t=NT, h=HEADS),
                                           ACT.Copy).then_inc(s_v, 1)
                    if tail:
                        if slot == SLOT["yT"]:
                            act.wait_ge(s_yTp, tail.count(1, 1))
                            act.activation(y_T[:, :], p_exp[:, 0, :], ACT.Copy).then_inc(s_yT, 1)
                        if slot == SLOT["relu4"]:
                            act.wait_ge(s_tshift, tail.count(1, 1))
                            relu_norm(t_h, x3, t_rstd, t_shift).then_inc(s_th, 1)
                        if slot == SLOT["hT4"]:
                            act.wait_ge(s_tturn, tail.count(1, 1))
                            act.activation(t_hT[:, :], p_conv[:, :], ACT.Copy).then_inc(s_thT, 1)
                        if slot == SLOT["conv1relu"]:
                            act.wait_ge(s_c1, tail.count(1, 1))
                            wait(act, s_gn, tail.count(1))
                            act.activation(xconv_T[:, :], p_conv[:, :], ACT.Relu, bias=bn_shift[:, 0:1],
                                           scale=bn_scale[:, 0:1])
                            act.activation(conv_h[:, PAD:PAD + N], p_conv[:, :], ACT.Relu, bias=bn_shift[:, 0:1],
                                           scale=bn_scale[:, 0:1]).then_inc(s_cin, 1)
                        if slot == SLOT["msg"]:
                            act.wait_ge(s_emb, tail.count(1, 1))
                            wait(act, s_np, tail.count(1))
                            act.activation(msg[:, :, :], emb[:, :, 0:D], ACT.Relu).then_inc(s_msg, 1)
                        if slot == SLOT["copyE"]:
                            act.wait_ge(s_dT, tail.count(1, 1))
                            act.activation(dl_T[:, :], p_exp[:, 0, 0:N // 2].bitcast(BF16), ACT.Copy)
                            act.activation(dr_T[:, :], p_exp[:, 1, 0:N // 2].bitcast(BF16), ACT.Copy).then_inc(s_dc, 1)
                        for half in due(slot, "near"):
                            act.wait_ge(s_dp, tail.count(2, half + 1))
                            act.wait_ge(s_sc, tail.count(10, 10))
                            wait(act, s_np, tail.count(1))
                            for t in (2 * half, 2 * half + 1):
                                act.activation(near[:, t, :], p_exp[:, t % 2, :], ACT.Exp,
                                               bias=sq[:, t:t + 1]).then_inc(s_near, 1)
                        if slot == SLOT["nmpT"]:
                            act.wait_ge(s_np, tail.count(1, 1))
                            act.activation(nmp_T[:, :], p_out[:, :], ACT.Copy).then_inc(s_nmp, 1)
                        if slot == SLOT["xrelu"]:
                            act.wait_ge(s_cs, tail.count(1, 1))
                            act.activation(xconv_T[:, :], xconv_T[:, :], ACT.Relu, bias=bn_shift[:, 1:2]).then_inc(s_xc, 1)
                        if slot == SLOT["gater"]:
                            act.wait_ge(s_gr, tail.count(1, 1))
                            act.activation(t_r[:, :], p_max[:, 0, :], ACT.Tanh, bias=gate_bias[:, 0:1],
                                           scale=0.5).then_inc(s_tr, 1)
                        if slot == SLOT["gatez"]:
                            act.wait_ge(s_gz, tail.count(1, 1))
                            act.activation(t_z[:, :], p_max[:, 1, :], ACT.Tanh, bias=gate_bias[:, 1:2],
                                           scale=0.5).then_inc(s_tz, 1)
                        if slot == SLOT["gateh"]:
                            act.wait_ge(s_gh, tail.count(1, 1))
                            act.activation(h_n[:, :], p_conv[:, :], ACT.Identity, bias=gate_bias[:, 2:3],
                                           scale=0.5).then_inc(s_hn, 1)
                        if slot == SLOT["nact"]:
                            act.wait_ge(s_ni, tail.count(1, 1))
                            act.activation(n_T[:, :], h_n[:, :], ACT.Tanh, bias=par[:, BIH + 2:BIH + 3]).then_inc(s_n, 1)

            pipeline(act, iteration)

        @block.tensor
        def _(pe):
            pe.wait_ge(s_weights, 16 * N_WEIGHTS)
            pe.wait_ge(s_wlap, 1)
            pe.wait_ge(s_const, N_CONST)

            def turn(dst, src):
                for t in range(NT):
                    last = pe.transpose(dst[:, t * P:t * P + P], src(t), ident[:, :])
                return last

            def max_scores(att, k):
                h, half = k // 2, k % 2
                for b in range(2):
                    qb = 2 * half + b
                    wait(pe, s_mx, att.count(2 * MAXES, 2 * k - 1 + b))
                    pe.matmul(p_max[:, b, :], q_st[0:SCORE_ROWS, att.par, h, qb * P:qb * P + P],
                                     k_st[0:SCORE_ROWS, att.par, h, :], start=True, stop=True).then_inc(s_mp, 1)

            def exp_scores(att, k):
                group, u = k // 8, k % 8
                t = u // 2
                for b, h in enumerate(head_rows(u, group)):
                    wait(pe, s_e, att.count(2 * EXPS, 2 * k - 1 + b))
                    pe.matmul(p_exp[:, b, :], k_st[0:SCORE_ROWS + MAX_ROWS, att.par, h, t * P:t * P + P],
                                     q_st[0:SCORE_ROWS + MAX_ROWS, att.par, h, :], start=True, stop=True
                              ).then_inc(s_ep, 1)

            def use_probs(att, k):
                group, u = k // 8, k % 8
                t = u // 2
                pe.wait_ge(s_pr, att.count(EXPS, k + 1))
                if u == 0:
                    wait(pe, s_oT, att.count(2, group))
                for b, h in enumerate(head_rows(u, group)):
                    j = h % 4
                    last = pe.matmul(p_out[HW * j:HW * j + HW, :], vals[:, att.par, t, h, :], pr[:, k % RING, b, :],
                                     start=(t == 0), stop=(t == NT - 1), skip_group_check=True)
                last.then_inc(s_pv, 1)

            def iteration(head, front, att, tail):
                for slot in range(SLOTS):
                    if slot == 0 and is_first(att):
                        pe.wait_ge(s_bn, 3)
                        pe.wait_ge(s_tail_weights, 16 * N_TAIL_WEIGHTS)
                    if att:
                        for k in due(slot, "max"):
                            if k == 0:
                                pe.wait_ge(s_qst[att.par], att.loads() * SPLITS)
                                pe.wait_ge(s_kst[att.par], att.loads() * SPLITS)
                                wait(pe, s_ni, (att - 1).count(1))
                                wait(pe, s_tz, (att - 1).count(1))
                            if k == MAXES // 2:
                                pe.wait_ge(s_mpart, att.count(10, 1))
                            max_scores(att, k)
                        for group in range(2):
                            if slot == SLOT[f"turnM{group}"]:
                                pe.wait_ge(s_mx, att.count(2 * MAXES, (group + 1) * MAXES))
                                pe.transpose(p_max[0:16, 0, 0:P],
                                             maxes[:, 4 * group:4 * group + 4, :].rearrange("p h t -> p (h t)"),
                                             ident[:, :]).then_inc(s_mT, 1)
                        for k in due(slot, "exp"):
                            if k % 8 == 0:
                                pe.wait_ge(s_mrow[k // 8], att.count(16 * MAX_ROWS, 16 * MAX_ROWS))
                            if k == 0 and tail:
                                pe.wait_ge(s_near, tail.count(NT, NT))
                            exp_scores(att, k)
                        for k in due(slot, "use"):
                            if k == 0 and tail:
                                pe.wait_ge(s_nmp, tail.count(1, 1))
                            if k == 0:
                                pe.wait_ge(s_v, att.count(1, 1))
                            use_probs(att, k)
                    if front:
                        if slot == SLOT["turn0"]:
                            pe.wait_ge(s_fh, front.count(3, 1))
                            wait(pe, s_kf, front.count(1))
                            wait(pe, s_v, front.count(1))
                            turn(p_f[:, 0, :], lambda t: f_h[:, t, :]).then_inc(s_fturn, 1)
                        if slot == SLOT["seq"]:
                            pe.wait_ge(s_fhT, front.count(3, 1))
                            for t in range(NT):
                                last = pe.matmul(p_f[:, 1, t * P:t * P + P], f_hT[:, t * P:t * P + P], wt[:, W0, :],
                                                 start=True, stop=True)
                            last.then_inc(s_seqp, 1)
                        for i in due(slot, "agg"):
                            if i == 0:
                                pe.wait_ge(s_seq, front.count(1, 1))
                                pe.wait_ge(s_adj[front.par], front.loads())
                            for t in range(NT):
                                last = pe.matmul(p_f4[:, i, 0:D + 1], adj_T[:, front.par, t, i * P:i * P + P],
                                                 seq[:, t, :], start=(t == 0), stop=(t == NT - 1))
                            if i == NT - 1:
                                last.then_inc(s_agg, 1)
                        if slot == SLOT["turn2"]:
                            pe.wait_ge(s_fz, front.count(1, 1))
                            pe.wait_ge(s_din, front.count(1, 1))
                            turn(p_f[:, 0, :], lambda t: f_z[:, t, :]).then_inc(s_fturn, 1)
                        if slot == SLOT["uv"]:
                            pe.wait_ge(s_fhT, front.count(3, 2))
                            for t in range(NT):
                                last = pe.matmul(p_f4[:, t, :], f_hT[:, t * P:t * P + P],
                                                 w_lap[:, :, :].rearrange("p a n -> p (a n)"), start=True, stop=True)
                            last.then_inc(s_uv, 1)
                        for i in due(slot, "lap"):
                            if i == 0:
                                pe.wait_ge(s_us, front.count(1, 1))
                                pe.wait_ge(s_vl, front.count(1, 1))
                            for t in range(NT):
                                last = pe.matmul(p_f[:, 0, i * P:i * P + P], adj_T[:, front.par, t, i * P:i * P + P],
                                                 u_scaled[:, t, :], start=(t == 0), stop=(t == NT - 1))
                            if i == NT - 1:
                                last.then_inc(s_lap, 1)
                        if slot == SLOT["turn3"]:
                            pe.wait_ge(s_fh, front.count(3, 3))
                            pe.wait_ge(s_pre, front.count(1, 1))
                            turn(p_f[:, 0, :], lambda t: f_h[:, t, :]).then_inc(s_fturn, 1)
                        if slot == SLOT["qk"]:
                            pe.wait_ge(s_fhT, front.count(3, 3))
                            pe.matmul(p_f[:, 1, :], wt[:, WQ, :], f_hT[:, :], start=True, stop=True).then_inc(s_qp, 1)
                            pe.matmul(p_f[:, 0, :], wt[:, WK, :], f_hT[:, :], start=True, stop=True).then_inc(s_kp, 1)
                        if slot == SLOT["v"]:
                            pe.wait_ge(s_qf, front.count(1, 1))
                            for t in range(NT):
                                last = pe.matmul(p_f[:, 1, t * P:t * P + P], f_hT[:, t * P:t * P + P], wt[:, WV, :],
                                                 start=True, stop=True)
                            last.then_inc(s_vp, 1)
                    if tail:
                        if slot == SLOT["outT"]:
                            pe.wait_ge(s_oT, tail.count(2, 2))
                            for group in range(2):
                                last = turn(p_exp[:, group, :], lambda t: o_T[:, group, t * P:t * P + P])
                            last.then_inc(s_on, 1)
                        if slot == SLOT["turnY"]:
                            pe.wait_ge(s_y, tail.count(1, 1))
                            turn(p_exp[:, 0, :], lambda t: y[:, t, :]).then_inc(s_yTp, 1)
                        if slot == SLOT["proj"]:
                            pe.wait_ge(s_yT, tail.count(1, 1))
                            for t in range(NT):
                                last = pe.matmul(p_exp[:, 1, t * P:t * P + P], y_T[:, t * P:t * P + P], wt[:, WO, :],
                                                 start=True, stop=True)
                            last.then_inc(s_pj, 1)
                        if slot == SLOT["turn4"]:
                            pe.wait_ge(s_th, tail.count(1, 1))
                            wait(pe, s_x4, tail.count(1))
                            turn(p_conv[:, :], lambda t: t_h[:, t, :]).then_inc(s_tturn, 1)
                        if slot == SLOT["conv1"]:
                            pe.wait_ge(s_thT, tail.count(1, 1))
                            pe.matmul(p_conv[:, :], wt[:, WC1, :], t_hT[:, :], start=True, stop=True).then_inc(s_c1, 1)
                            pe.wait_ge(s_x3, tail.count(1, 1))
                            for t in range(NT):
                                last = pe.matmul(p_e4[:, t, 0:D + NSE], t_hT[:, t * P:t * P + P], w_emb[:, :],
                                                 start=True, stop=True)
                            last.then_inc(s_embp, 1)
                        for k in due(slot, "conv2"):
                            if k == 0:
                                pe.wait_ge(s_cl, tail.count(1, 1))
                            pe.matmul(p_conv[:, :], w_conv2h[:, k, :], conv_h[:, k:k + N], start=(k == 0), stop=False)
                            pe.matmul(p_conv[:, :], w_conv2l[:, k, :], conv_h[:, k:k + N], start=False, stop=False)
                            mm = pe.matmul(p_conv[:, :], w_conv2h[:, k, :], conv_l[:, k:k + N], start=False,
                                           stop=(k == TAPS - 1))
                            if k == TAPS - 1:
                                mm.then_inc(s_c2, 1)
                        if slot == SLOT["turnE"]:
                            pe.wait_ge(s_sc, tail.count(10, 9))
                            for side, tile in enumerate((dl, dr)):
                                for t in range(NT):
                                    last = pe.transpose(p_exp[:, side, t * P // 2:(t + 1) * P // 2].bitcast(BF16),
                                                        tile[:, t, :], ident_b[:, :])
                            last.then_inc(s_dT, 1)
                        for half in due(slot, "dist"):
                            pe.wait_ge(s_dc, tail.count(1, 1))
                            wait(pe, s_near, tail.count(NT, 2 * half))
                            for t in (2 * half, 2 * half + 1):
                                last = pe.matmul(p_exp[:, t % 2, :], dl_T[:, t * P:t * P + P], dr_T[:, :],
                                                 start=True, stop=True)
                            last.then_inc(s_dp, 1)
                        for t in due(slot, "nmp"):
                            pe.wait_ge(s_nm, tail.count(NT, t + 1))
                            if t == 0:
                                pe.wait_ge(s_msg, tail.count(1, 1))
                            mm = pe.matmul(p_out[:, :], msg[:, t, :], near[:, t, :], start=(t == 0),
                                           stop=(t == NT - 1))
                            if t == NT - 1:
                                mm.then_inc(s_np, 1)
                        def gate(dst, cols, rows_in):
                            for n, (k, rhs) in enumerate(rows_in):
                                last = pe.matmul(dst, w_gru[:, k, cols * D:cols * D + D], rhs[:, :], start=(n == 0),
                                                 stop=(n == len(rows_in) - 1))
                            return last

                        def gate_inputs():
                            if att:
                                pe.wait_ge(s_mpart, att.count(10, 6))
                            pe.wait_ge(s_nmp, tail.count(1, 1))
                            pe.wait_ge(s_xc, tail.count(1, 1))

                        x_parts = [(1, nmp_T), (0, xconv_T)]
                        if slot == SLOT["grur"]:
                            gate_inputs()
                            gate(p_max[:, 0, :], 0, [(2, t_hT)] + x_parts).then_inc(s_gr, 1)
                        if slot == SLOT["gruz"]:
                            gate_inputs()
                            gate(p_max[:, 1, :], 1, [(2, t_hT)] + x_parts).then_inc(s_gz, 1)
                        if slot == SLOT["gruh"]:
                            pe.wait_ge(s_cs, tail.count(1, 1))
                            gate(p_conv[:, :], 2, [(2, t_hT)]).then_inc(s_gh, 1)
                        if slot == SLOT["grun"]:
                            pe.wait_ge(s_tr, tail.count(1, 1))
                            gate(p_max[:, 0, :], 2, x_parts).then_inc(s_gn, 1)
                        if slot == SLOT["back"]:
                            pe.wait_ge(s_new, tail.count(1, 1))
                            turn(p_conv[:, :], lambda t: new_T[:, t * P:t * P + P]).then_inc(s_nb, 1)

            pipeline(pe, iteration)


def kernel(**inputs):
    import numpy as np
    import concourse.bacc as bacc
    from concourse.bass_utils import run_bass_kernel_spmd

    a = {k: np.asarray(v) for k, v in inputs.items()}
    f = np.float32
    ih, hh = a["L3_gnn_w_ih"], a["L3_gnn_w_hh"]
    blocks = [a["L0_gnn_W"], a["L1_gnn_W_self"], a["L1_gnn_W_neigh"], a["L2_gnn_Wq"].T, a["L2_gnn_Wk"].T,
              a["L2_gnn_Wv"].T, a["L2_gnn_Wo"].T, a["L3_gnn_conv1_w"][:, :, 0].T, a["L3_gnn_w_msg"].T]
    blocks += [ih[k * D:k * D + D, 0:D].T for k in range(3)]
    blocks += [ih[k * D:k * D + D, D:2 * D].T for k in range(3)]
    blocks += [hh[k * D:k * D + D, :].T for k in range(3)]
    rows = np.concatenate([np.broadcast_to(v, (P, v.size)) for v in (
        a["L0_gnn_bias"], a["L2_gnn_bo"], a["L3_gnn_b_msg"], a["L3_gnn_b_se"])] + [a["L3_gnn_w_se"].T], axis=1)
    params = np.stack([a["L1_gnn_gamma"], a["L1_gnn_beta"], np.broadcast_to(a["L0_gnn_prelu_a"], (P,)),
                       a["L3_gnn_bn1_g"], a["L3_gnn_bn1_b"], a["L3_gnn_bn1_m"], a["L3_gnn_bn1_v"],
                       a["L3_gnn_bn2_g"], a["L3_gnn_bn2_b"], a["L3_gnn_bn2_m"], a["L3_gnn_bn2_v"],
                       *a["L3_gnn_b_ih"].reshape(3, D), *a["L3_gnn_b_hh"].reshape(3, D)], axis=1)
    arrays = {
        "x": a["x"],
        "adj_t": np.transpose(a["adj"], (0, 2, 1)),
        "weights": np.stack(blocks),
        "rows": rows,
        "params": params,
        "conv2": np.transpose(a["L3_gnn_conv2_w"], (2, 1, 0)),
    }
    arrays = {k: np.ascontiguousarray(v) for k, v in arrays.items()}
    nc = bacc.Bacc("TRN2", target_bir_lowering=False, num_devices=1)
    args = [nc.dram_tensor(k, v.shape, mybir.dt.from_np(v.dtype), kind="ExternalInput").ap()
            for k, v in arrays.items()]
    out = nc.dram_tensor("out", (B, N, D), F32, kind="ExternalOutput").ap()
    build(nc, *args, out)
    r = run_bass_kernel_spmd(nc, [arrays], core_ids=[0])
    return r.results[0]["out"]
```

```python
from contextlib import ExitStack

import concourse.bass as bass
from concourse import mybir

F32 = mybir.dt.float32
BF16 = mybir.dt.bfloat16
F32R = mybir.dt.float32r
ALU = mybir.AluOpType
ACT = mybir.ActivationFunctionType
AX = mybir.AxisListType

P = 128
B, N, D = 16, 512, 128
NT = N // P
HEADS, HD = 8, 16
HW = 32
TAPS = 17
PAD = TAPS // 2
EPS = 1e-5
ADJ_EPS = 1e-6
Q_PARTS = [0, 0, 1, 0, 2, 1]
K_PARTS = [0, 1, 0, 2, 0, 1]
SPLITS = len(Q_PARTS)
SCORE_ROWS = SPLITS * HD
MAX_ROWS = 3
NSE = 3
DIST_SQ = SPLITS * NSE

(GAMMA, BETA, PRELU, BN1G, BN1B, BN1M, BN1V, BN2G, BN2B, BN2M, BN2V, BIH, BHH) = (
    0, 1, 2, 3, 4, 5, 6, 7, 8, 9, 10, 11, 14)
NPAR = 17

SLOTS = 100
MAXES = 16
EXPS = 16
RING = 6
SLOT = dict(
    stats0=75, rstd0=77, shift0=84, relu0=94,
    turn0=0, hT0=12, seq=14, seqcopy=15, gcn=25, neg=25, x1=27, degpow=48, degrs=48, stats1=29, rstd1=31,
    shift1=32, relu1=34, stats2=36, rstd2=38, scale2=43, turn2=44, xnT=46, uv=48, vcopy=49, uscale=51,
    softin=60, soft=65, x2=67, x2b=79, stats3=69, rstd3=71, shift3=72, relu3=74, turn3=75, hT3=76, qk=79,
    qkcopy=81, qsplit=82, ksplit=87, v=90, vcopy3=95,
    turnM0=37, splitM0=41, turnM1=64, splitM1=66, outcopy0=86, outcopy1=99,
    outT=2, norm=4, turnY=8, yT=8, proj=13, x3=14, stats4=16, rstd4=18, shift4=19, relu4=22, turn4=23, hT4=24,
    conv1=27, conv1relu=28, convsplit=31, emb=32, msg=46, parts=39, turnE=40, copyE=42, nmpT=68, xconv=88,
    xrelu=89, grur=106, gater=99, gruz=95, gatez=98, gruh=109, gateh=110, grun=112, nin=113, nact=114,
    new=119, back=120, x4=122,
)
STEPS = dict(
    max=(1, 3, 7, 10, 15, 21, 24, 31, 41, 44, 45, 49, 52, 56, 58, 61),
    take=(2, 5, 8, 11, 21, 23, 30, 34, 43, 45, 47, 50, 53, 56, 59, 62),
    scores=(51, 55, 57, 59, 64, 69, 71, 73, 77, 82, 83, 85, 87, 89, 91, 96),
    exp=(52, 55, 58, 60, 68, 70, 72, 75, 78, 82, 84, 86, 88, 91, 92, 97),
    probs=(54, 64, 71, 73, 77, 78, 80, 84, 86, 87, 90, 91, 93, 94, 96, 98),
    use=(70, 73, 74, 81, 82, 82, 84, 85, 88, 88, 97, 97, 98, 98, 99, 99),
    agg=(17, 18, 19, 23),
    lap=(52, 54, 56, 58),
    colsum=(11, 12, 16, 17),
    conv2=(33, 34, 34, 35, 36, 37, 41, 50, 60, 61, 68, 72, 72, 76, 80, 86, 86),
    dist=(42, 46),
    near=(44, 48),
    mask=(45, 49, 51, 53),
    nmp=(63, 65, 66, 67),
)


def due(slot, step):
    return [k for k, at in enumerate(STEPS[step]) if at == slot]


class Graph:

    def __init__(self, c, turn=None):
        self.c, self.turn = c, turn
        self.par = c % 2

    def __add__(self, k):
        return Graph(self.c + k, self.turn)

    def __sub__(self, k):
        return Graph(self.c - k, self.turn)

    def index(self):
        return self.c if self.turn is None else self.turn * 2 + self.c

    def count(self, per, k=0):
        first = per * self.c + k
        if self.turn is None:
            return max(first, 0)
        assert first > 0
        return self.turn * (2 * per) + first

    def loads(self, k=1):
        half = self.c // 2 + k
        if self.turn is None:
            return max(16 * half, 0)
        assert half > 0
        return self.turn * 16 + 16 * half


def is_first(graph):
    return graph is not None and graph.turn is None and graph.c == 0


def wait(eng, sem, value):
    if isinstance(value, int) and value <= 0:
        return
    eng.wait_ge(sem, value)


def wait_alone(eng, sem, value, passed):
    if isinstance(value, int) and value <= 0:
        return
    eng.wait_ge(sem, value)
    eng.sem_inc(passed, 1)


def pipeline(eng, iteration):
    def graphs(newest):
        return [newest - k for k in range(5)]

    peeled = 6
    for i in range(peeled):
        iteration(*[Graph(i - k) if i >= k else None for k in range(5)])
    with eng.Fori(0, (B - peeled) // 2) as turn:
        iteration(*graphs(Graph(peeled, turn)))
        iteration(*graphs(Graph(peeled + 1, turn)))
    for i in range(B, B + 4):
        iteration(*[Graph(i - k) if i - k < B else None for k in range(5)])


def placed(tail, late, slot):
    return [(graph, at) for graph, at in ((late, slot + SLOTS), (tail, slot)) if graph]


def build(nc, x, adj_t, weights, rows, params, conv2, out):
    ctx = ExitStack()
    with ctx:
        def sb(name, shape, dt=F32):
            return ctx.enter_context(nc.sbuf_tensor(name, shape, dt))

        def ps(name, shape):
            return ctx.enter_context(nc.psum_tensor(name, shape, F32))

        def sem(name):
            return ctx.enter_context(nc.semaphore(name))

        wt = sb("wt", [P, 6, D])
        w_lap = sb("w_lap", [P, 2, D])
        w_self = sb("w_self", [P, D])
        w_emb = sb("w_emb", [P, D + NSE])
        w_gru = sb("w_gru", [P, 3, 3 * D])
        w_conv2h = sb("w_conv2h", [P, TAPS, D], F32R)
        w_conv2l = sb("w_conv2l", [P, TAPS, D], F32R)
        row = sb("row", [P, 3 * D + NSE])
        par = sb("par", [P, NPAR])
        bn_scale = sb("bn_scale", [P, 2])
        bn_shift = sb("bn_shift", [P, 2])
        bn_tmp = sb("bn_tmp", [P, 2])
        gate_bias = sb("gate_bias", [P, 3])
        half_pow = sb("half_pow", [P, 2 * NT])
        neg_slope = sb("neg_slope", [P, 1])
        one_col = sb("one_col", [P, 1])
        ident = sb("ident", [P, P])
        ident_b = sb("ident_b", [P, P], BF16)

        x_in = sb("x_in", [P, 2, NT, D])
        adj_T = sb("adj_T", [P, 2, NT, N])
        f_stat = sb("f_stat", [P, NT, 6])
        f_mom = sb("f_mom", [P, NT, 2])
        f_var = sb("f_var", [P, NT])
        f_rstd = sb("f_rstd", [P, NT])
        f_shift = sb("f_shift", [P, NT])
        f_h = sb("f_h", [P, NT, D])
        f_z = sb("f_z", [P, NT, D])
        f_hT = sb("f_hT", [P, N])
        seq = sb("seq", [P, NT, D + 1])
        gcn_pre = sb("gcn_pre", [P, NT, D])
        x1 = sb("x1", [P, NT, D])
        deg = sb("deg", [P, 2, NT])
        deg_nz = sb("deg_nz", [P, 2 * NT])
        deg_floor = sb("deg_floor", [P, 2 * NT])
        deg_pow = sb("deg_pow", [P, 2 * NT])
        deg_rs = sb("deg_rs", [P, 2, NT])
        u_scaled = sb("u_scaled", [P, NT, D])
        v_lap = sb("v_lap", [P, NT, D])
        pre = sb("pre", [P, NT, D])
        soft = sb("soft", [P, NT, D])
        junk = [tile[:, half:half + 2, :].rearrange("p t d -> p (t d)").bitcast(BF16)
                for tile in (soft, pre) for half in (0, 2)]
        x2 = sb("x2", [P, NT, D])
        x2b = sb("x2b", [P, 2, NT, D])
        qf = sb("qf", [P, N])
        kf = sb("kf", [P, N])
        q_part = sb("q_part", [P, 3, N], BF16)
        k_part = sb("k_part", [P, 3, N], BF16)
        q_st = sb("q_st", [P, 2, HEADS, N], BF16)
        k_st = sb("k_st", [P, 2, HEADS, N], BF16)
        vals = sb("vals", [P, 2, NT, HEADS, HW])
        maxes = sb("maxes", [P, HEADS, NT])
        neg_max = sb("neg_max", [HEADS // 2 * NT, 2, P])
        max_part = sb("max_part", [HEADS // 2 * NT, 2, 3, P], BF16)
        pr = sb("pr", [P, RING, 2, N])
        o_T = sb("o_T", [P, 2, N])
        r_sum = sb("r_sum", [P, 2, NT, 4])
        y = sb("y", [P, NT, D])
        x3 = sb("x3", [P, 2, NT, D])
        t_stat = sb("t_stat", [P, NT, 6])
        t_mom = sb("t_mom", [P, NT, 2])
        t_var = sb("t_var", [P, NT])
        t_rstd = sb("t_rstd", [P, NT])
        t_shift = sb("t_shift", [P, NT])
        t_h = y
        t_hT = sb("t_hT", [P, N])
        conv_h = sb("conv_h", [P, N + 2 * PAD], F32R)
        conv_l = sb("conv_l", [P, N + 2 * PAD], F32R)
        emb = sb("emb", [P, NT, D + NSE])
        msg = sb("msg", [P, NT, D])
        s_rest = sb("s_rest", [P, 2, NT, NSE])
        s_sq = sb("s_sq", [P, NT, NSE])
        sq = sb("sq", [P, NT])
        nsq = sb("nsq", [P, NT])
        sq_rest = sb("sq_rest", [P, 2, NT])
        dl = sb("dl", [P, NT, P], BF16)
        dr = sb("dr", [P, NT, P], BF16)
        dl_T = sb("dl_T", [P, N], BF16)
        dr_T = sb("dr_T", [P, N], BF16)
        mask_T = sb("mask_T", [P, NT, N])
        near = sb("near", [P, NT, N])
        nmp_T = sb("nmp_T", [P, N])
        y_T = sb("y_T", [P, N])
        xconv_T = sb("xconv_T", [P, N])
        t_r = sb("t_r", [P, N])
        t_z = sb("t_z", [P, N])
        h_n = sb("h_n", [P, N])
        n_T = t_r
        new_T = h_n

        w_conv2 = pr[:, :, :, :].rearrange("p a b n -> p (a b n)")[:, 0:TAPS * D].rearrange("p (k n) -> p k n", n=D)

        q_dram = nc.dram_tensor("q_dram", [2, 3, P, N], BF16).ap()
        k_dram = nc.dram_tensor("k_dram", [2, 3, P, N], BF16).ap()

        p_max = ps("p_max", [P, 2, N])
        p_exp = ps("p_exp", [P, 2, N])
        p_out = ps("p_out", [P, N])
        p_conv = ps("p_conv", [P, N])
        p_f = ps("p_f", [P, 2, N])
        p_f4 = p_f[:, :, :].rearrange("p a (b n) -> p (a b) n", b=2)
        p_e4 = p_exp[:, :, :].rearrange("p a (b n) -> p (a b) n", b=2)

        s_weights = sem("weights_loaded")
        s_tail_weights = sem("tail_weights_loaded")
        s_wlap = sem("laplacian_weights_ready")
        s_const = sem("constants_ready")
        s_late_const = sem("late_constants_ready")
        s_bn = sem("bn_folded")
        s_slope = sem("slope_negated")
        s_bnv = sem("bn_var")
        s_x = [sem("x_loaded0"), sem("x_loaded1")]
        s_adj = [sem("adj_loaded0"), sem("adj_loaded1")]
        s_mask = sem("mask_loaded")
        s_fstat = sem("f_stats")
        s_fmom = sem("f_moments")
        s_fvar = sem("f_var_eps")
        s_frstd = sem("f_rstd")
        s_fshift = sem("f_shift")
        s_fh = sem("f_relu_h")
        s_fz = sem("f_scaled_z")
        s_fturn = sem("f_turned")
        s_fhT = sem("f_turned_copied")
        s_seqp = sem("seq_product")
        s_seq = sem("seq_ready")
        s_agg = sem("adj_seq_product")
        s_gpre = sem("gcn_pre")
        s_gneg = sem("gcn_negative_part")
        s_gact = sem("gcn_positive_part")
        s_x1 = sem("x1_ready")
        s_dout = sem("column_sums")
        s_din = sem("row_sums")
        s_dfl = sem("degree_floor")
        s_dpow = sem("degree_pow")
        s_drs = sem("degree_rsqrt")
        s_uv = sem("uv_product")
        s_us = sem("u_scaled_ready")
        s_vl = sem("v_copied")
        s_lap = sem("laplacian_product")
        s_pre = sem("softplus_in_negated")
        s_abs = sem("softplus_abs")
        s_se = sem("softplus_exp")
        s_sl = sem("softplus_log")
        s_sp = sem("softplus_ready")
        s_x2 = sem("x2_ready")
        s_x2b = sem("x2b_ready")
        s_qp = sem("q_product")
        s_kp = sem("k_product")
        s_vp = sem("v_product")
        s_qf = sem("q_copied")
        s_kf = sem("k_copied")
        s_v = sem("v_ready")
        s_qs = sem("q_split")
        s_ks = sem("k_split")
        s_qd = sem("q_written")
        s_kd = sem("k_written")
        s_qst = [sem("q_stacked0"), sem("q_stacked1")]
        s_kst = [sem("k_stacked0"), sem("k_stacked1")]
        s_mp = sem("max_scores")
        s_mx = sem("max_taken")
        s_mT = sem("max_turned")
        s_mpart = sem("max_split")
        s_mrow = [sem("max_rows0"), sem("max_rows1")]
        s_ep = sem("exp_scores")
        s_e = sem("exp_ready")
        s_pr = sem("probs_ready")
        s_pv = sem("probs_used")
        s_oT = sem("attention_out")
        s_on = sem("out_turned")
        s_rs = sem("row_sum_inverse")
        s_y = sem("out_normed")
        s_yTp = sem("out_turned_back")
        s_yT = sem("out_T_copied")
        s_pj = sem("projected")
        s_x3 = sem("x3_ready")
        s_tstat = sem("t_stats")
        s_tmom = sem("t_moments")
        s_tvar = sem("t_var_eps")
        s_trstd = sem("t_rstd")
        s_tshift = sem("t_shift")
        s_th = sem("t_relu_h")
        s_tturn = sem("t_turned")
        s_thT = sem("t_hT_ready")
        s_c1 = sem("conv1_product")
        s_cin = sem("conv2_in")
        s_cl = sem("conv2_in_low")
        s_c2 = sem("conv2_product")
        s_embp = sem("embedding_product")
        s_emb = sem("embedding_biased")
        s_msg = sem("messages_ready")
        s_sc = sem("embedding_split")
        s_dT = sem("distance_turned")
        s_dc = sem("distance_copied")
        s_dp = sem("distances")
        s_near = sem("near_ready")
        s_nm = sem("near_masked")
        s_np = sem("message_product")
        s_nmp = sem("nmp_ready")
        s_cs = sem("conv_summed")
        s_xc = sem("xconv_ready")
        s_gr = sem("gate_r_product")
        s_gz = sem("gate_z_product")
        s_gh = sem("gate_h_product")
        s_gn = sem("gate_n_product")
        s_tr = sem("gate_r")
        s_tz = sem("gate_z")
        s_hn = sem("gate_h")
        s_rn = sem("r_times_h")
        s_ni = sem("n_in_ready")
        s_n = sem("n_ready")
        s_hm = sem("h_minus_n_ready")
        s_zp = sem("z_part_ready")
        s_new = sem("new_state")
        s_nb = sem("new_turned_back")
        s_x4 = sem("x4_ready")
        s_passed_sp = sem("sp_waits_passed")
        s_passed_pool = sem("pool_waits_passed")
        s_passed_dve = sem("dve_waits_passed")
        s_out = [sem("stored0"), sem("stored1")]

        W0, WQ, WK, WV, WO, WC1 = range(6)
        N_WEIGHTS = 6
        N_TAIL_WEIGHTS = 2 + 2 + 3
        N_CONST = 5
        N_LATE_CONST = 8

        def head_rows(t, group):
            return [group * 4 + (t % 2) * 2 + b for b in range(2)]

        block = ctx.enter_context(nc.Block())

        @block.sync
        def _(sp):
            def load_front_weights():
                sp.dma_start(wt[:, 0, :], weights[0]).then_inc(s_weights, 16)
                sp.dma_start(row[:, :], rows[:, 0:3 * D + NSE]).then_inc(s_weights, 16)
                sp.dma_start(par[:, :], params).then_inc(s_weights, 16)
                sp.dma_start(w_self[:, :], weights[1]).then_inc(s_weights, 16)
                sp.dma_start(w_lap[:, 0, :], weights[2]).then_inc(s_weights, 16)
                sp.dma_start(wt[:, 1:6, :], weights[3:8].rearrange("a p n -> p a n")).then_inc(s_weights, 16)

            def load_tail_weights():
                sp.dma_start(w_conv2[:, 0:9, :], conv2[0:9].rearrange("k p n -> p k n")).then_inc(s_tail_weights, 16)
                sp.dma_start(w_conv2[:, 9:TAPS, :], conv2[9:TAPS].rearrange("k p n -> p k n")
                             ).then_inc(s_tail_weights, 16)
                sp.dma_start(w_emb[:, 0:D], weights[8]).then_inc(s_tail_weights, 16)
                sp.dma_start(w_emb[:, D:D + NSE], rows[:, 3 * D + NSE:3 * D + 2 * NSE]).then_inc(s_tail_weights, 16)
                for k in range(3):
                    sp.dma_start(w_gru[:, k, :].rearrange("p (a n) -> p a n", a=3),
                                 weights[9 + 3 * k:12 + 3 * k].rearrange("a p n -> p a n")
                                 ).then_inc(s_tail_weights, 16)

            def iteration(head, front, att, newest_tail, late):
                if head:
                    wait_alone(sp, s_x1, (head - 2).count(1, 1), s_passed_sp)
                    sp.dma_start(x_in[:, head.par, :, :],
                                 x[head.index()].rearrange("(t p) d -> p t d", p=P)).then_inc(s_x[head.par], 16)
                if is_first(head):
                    load_front_weights()
                if front:
                    wait_alone(sp, s_pr, (front - 2).count(EXPS, EXPS), s_passed_sp)
                    sp.dma_start(adj_T[:, front.par, :, :],
                                 adj_t[front.index()].rearrange("(t p) n -> p t n", p=P)).then_inc(s_adj[front.par], 16)
                if is_first(front):
                    load_tail_weights()
                if newest_tail:
                    tail = newest_tail
                    wait_alone(sp, s_nm, tail.count(NT), s_passed_sp)
                    sp.dma_start(mask_T[:, :, :],
                                 adj_t[tail.index()].rearrange("(t p) n -> p t n", p=P)).then_inc(s_mask, 16)
                for group in range(2):
                    if att:
                        wait_alone(sp, s_mpart, att.count(10, 5 * (group + 1)), s_passed_sp)
                        for j in range(MAX_ROWS):
                            sp.dma_start(q_st[SCORE_ROWS + j:SCORE_ROWS + j + 1, att.par, 4 * group:4 * group + 4, :],
                                         max_part[:, group, j, :]).then_inc(s_mrow[group], 16)
                    if group == 0 and late:
                        wait_alone(sp, s_x4, late.count(1, 1), s_passed_sp)
                        sp.dma_start(out[late.index()].rearrange("(t p) d -> p t d", p=P),
                                     x3[:, late.par, :, :]).then_inc(s_out[late.par], 16)
                if front:
                    wait_alone(sp, s_qs, front.count(3, 3), s_passed_sp)
                    sp.dma_start(q_dram[front.par].rearrange("a p n -> p a n"), q_part[:, :, :]).then_inc(s_qd, 16)
                    wait_alone(sp, s_ks, front.count(3, 3), s_passed_sp)
                    sp.dma_start(k_dram[front.par].rearrange("a p n -> p a n"), k_part[:, :, :]).then_inc(s_kd, 16)
                    wait_alone(sp, s_ep, (front - 2).count(2 * EXPS, 2 * EXPS), s_passed_sp)
                    wait_alone(sp, s_qd, front.count(16, 16), s_passed_sp)
                    for s, part in enumerate(Q_PARTS):
                        sp.dma_start(q_st[HD * s:HD * s + HD, front.par, :, :],
                                     q_dram[front.par, part].rearrange("(h d) n -> d h n", d=HD)
                                     ).then_inc(s_qst[front.par], 16)
                    wait_alone(sp, s_kd, front.count(16, 16), s_passed_sp)
                    for s, part in enumerate(K_PARTS):
                        sp.dma_start(k_st[HD * s:HD * s + HD, front.par, :, :],
                                     k_dram[front.par, part].rearrange("(h d) n -> d h n", d=HD)
                                     ).then_inc(s_kst[front.par], 16)

            pipeline(sp, iteration)
            for parity in range(2):
                sp.wait_ge(s_out[parity], 16 * (B // 2))

        @block.gpsimd
        def _(pool):
            pool.memset(ident[:, :], 0.0).then_inc(s_const, 1)
            pool.memset(half_pow[:, :], -0.5).then_inc(s_const, 1)
            pool.memset(one_col[:, :], 1.0).then_inc(s_const, 1)
            pool.memset(seq[:, :, D:D + 1], 1.0).then_inc(s_const, 1)
            pool.wait_ge(s_const, 1)
            pool.affine_select(out=ident[:, :], in_=ident[:, :], compare_op=ALU.not_equal, fill=1.0, base=0,
                               pattern=[[-1, P]], channel_multiplier=1).then_inc(s_const, 1)
            pool.wait_ge(s_const, N_CONST)

            def set_late_constants():
                pool.tensor_copy(ident_b[:, :], ident[:, :]).then_inc(s_late_const, 1)
                pool.memset(vals[:, :, :, :, HD:HW], 0.0).then_inc(s_late_const, 1)
                pool.wait_ge(s_late_const, 2)
                pool.memset(vals[:, :, :, :, HD:HD + 1], 1.0).then_inc(s_late_const, 1)
                pool.wait_ge(s_late_const, 3)
                pool.memset(k_st[SCORE_ROWS:P, :, :, :], 1.0).then_inc(s_late_const, 1)
                pool.wait_ge(s_late_const, 4)
                pool.memset(conv_h[:, :].bitcast(F32), 0.0).then_inc(s_late_const, 1)
                pool.memset(conv_l[:, :].bitcast(F32), 0.0).then_inc(s_late_const, 1)
                pool.memset(dl[:, :, :], 0.0).then_inc(s_late_const, 1)
                pool.memset(dr[:, :, :], 0.0).then_inc(s_late_const, 1)

            pool.wait_ge(s_weights, 16 * N_WEIGHTS)
            pool.tensor_tensor(w_lap[:, 1, :], w_self[:, :], w_lap[:, 0, :], ALU.add).then_inc(s_wlap, 1)
            pool.tensor_scalar(bn_tmp[:, :], par[:, BN1V:BN2V + 1:BN2V - BN1V], EPS, None, ALU.add).then_inc(s_bnv, 1)
            pool.wait_ge(s_bnv, 1)
            pool.tensor_tensor(bn_shift[:, :], bn_tmp[:, :], half_pow[:, 0:2], ALU.pow).then_inc(s_bnv, 1)

            def inverse_root(var, mom, out_, s_mom, s_var, s_rstd, value, s_used, used):
                wait_alone(pool, s_mom, value, s_passed_pool)
                pool.tensor_scalar(var[:, :], mom[:, :, 1], EPS, None, ALU.add).then_inc(s_var, 1)
                wait(pool, s_used, used)
                pool.wait_ge(s_var, value)
                pool.tensor_tensor(out_[:, :], var[:, :], half_pow[:, 0:NT], ALU.pow).then_inc(s_rstd, 1)

            def iteration(head, front, att, newest_tail, late):
                for slot in range(SLOTS):
                    if slot == SLOTS - 1 and is_first(head):
                        set_late_constants()
                    if head and slot == SLOT["rstd0"]:
                        inverse_root(f_var, f_mom, f_rstd, s_fmom, s_fvar, s_frstd, head.count(4, 1),
                                     s_fh, head.count(3))
                    if front:
                        for k, step in enumerate(("rstd1", "rstd2", "rstd3")):
                            if slot == SLOT[step]:
                                inverse_root(f_var, f_mom, f_rstd, s_fmom, s_fvar, s_frstd, front.count(4, k + 2),
                                             s_fh, front.count(3, min(k + 1, 2)))
                        if slot == SLOT["degpow"]:
                            pool.wait_ge(s_dfl, front.count(1, 1))
                            pool.tensor_tensor(deg_pow[:, :], deg_floor[:, :], half_pow[:, :], ALU.pow
                                               ).then_inc(s_dpow, 1)
                        if slot == SLOT["scale2"]:
                            pool.wait_ge(s_frstd, front.count(4, 3))
                            wait_alone(pool, s_fturn, front.count(3), s_passed_pool)
                            for t in range(NT):
                                last = pool.tensor_scalar(f_z[:, t, :], f_h[:, t, :], f_mom[:, t, 0:1],
                                                          f_rstd[:, t:t + 1], ALU.subtract, ALU.mult)
                            last.then_inc(s_fz, 1)
                        if slot == SLOT["x2b"]:
                            pool.wait_ge(s_x2, front.count(1, 1))
                            wait(pool, s_x3, (front - 2).count(1, 1))
                            pool.tensor_tensor(x2b[:, front.par, :, :], x2[:, :, :],
                                               row[:, D:2 * D].unsqueeze(1).to_broadcast([P, NT, D]), ALU.add
                                               ).then_inc(s_x2b, 1)
                        if slot == SLOT["ksplit"]:
                            pool.wait_ge(s_kf, front.count(1, 1))
                            pool.tensor_tensor(kf[:, :], kf[:, :], k_part[:, 0, :], ALU.subtract).then_inc(s_ks, 1)
                            wait_alone(pool, s_ks, front.count(3, 1), s_passed_pool)
                            pool.tensor_scalar(k_part[:, 1, :], kf[:, :], 1.0, None, ALU.mult).then_inc(s_ks, 1)
                            pool.wait_ge(s_ks, front.count(3, 2))
                            pool.tensor_tensor(k_part[:, 2, :], kf[:, :], k_part[:, 1, :], ALU.subtract
                                               ).then_inc(s_ks, 1)
                    for tail, at in placed(newest_tail, late, slot):
                        if at == SLOT["rstd4"]:
                            inverse_root(t_var, t_mom, t_rstd, s_tmom, s_tvar, s_trstd, tail.count(1, 1),
                                         s_th, tail.count(1))
                        for t in due(at, "mask"):
                            pool.wait_ge(s_mask, tail.count(16, 16))
                            pool.wait_ge(s_near, tail.count(NT, t + 1))
                            pool.tensor_tensor(near[:, t, :], near[:, t, :], mask_T[:, t, :], ALU.mult
                                               ).then_inc(s_nm, 1)

            pipeline(pool, iteration)

        @block.vector
        def _(dve):
            def fold_parameters():
                dve.wait_ge(s_bnv, 2)
                dve.tensor_tensor(bn_scale[:, :], bn_shift[:, :], par[:, BN1G:BN2G + 1:BN2G - BN1G], ALU.mult
                                  ).then_inc(s_bnv, 1)
                dve.wait_ge(s_bnv, 3)
                dve.tensor_tensor(bn_tmp[:, :], bn_scale[:, :], par[:, BN1M:BN2M + 1:BN2M - BN1M], ALU.mult
                                  ).then_inc(s_bnv, 1)
                dve.wait_ge(s_bnv, 4)
                dve.tensor_tensor(bn_shift[:, :], par[:, BN1B:BN2B + 1:BN2B - BN1B], bn_tmp[:, :], ALU.subtract
                                  ).then_inc(s_bn, 1)
                dve.tensor_tensor(gate_bias[:, 0:2], par[:, BIH:BIH + 2], par[:, BHH:BHH + 2], ALU.add).then_inc(s_bnv, 1)
                dve.tensor_copy(gate_bias[:, 2:3], par[:, BHH + 2:BHH + 3]).then_inc(s_bnv, 1)
                dve.wait_ge(s_bnv, 6)
                dve.tensor_scalar(gate_bias[:, :], gate_bias[:, :], 0.5, None, ALU.mult).then_inc(s_bn, 1)
                dve.wait_ge(s_tail_weights, 16 * N_TAIL_WEIGHTS)
                dve.tensor_copy(w_conv2h[:, :, :], w_conv2).then_inc(s_bnv, 1)
                dve.wait_ge(s_bnv, 7)
                dve.tensor_tensor(w_conv2l[:, :, :], w_conv2, w_conv2h[:, :, :].bitcast(F32), ALU.subtract).then_inc(s_bn, 1)

            def norm_stats(src, stat, mom, s_stat, s_mom, value):
                for t in range(NT):
                    last = dve.bn_stats(stat[:, t, :], src[:, t, :])
                last.then_inc(s_stat, 1)
                wait_alone(dve, s_stat, value, s_passed_dve)
                for t in range(NT):
                    last = dve.bn_aggr(mom[:, t, :], stat[:, t, :])
                last.then_inc(s_mom, 1)

            def norm_shift(mom, rstd, shift, s_rstd, s_shift, value):
                dve.wait_ge(s_rstd, value)
                dve.scalar_tensor_tensor(out=shift[:, :], in0=mom[:, :, 0], scalar=-1.0, in1=rstd[:, :],
                                         op0=ALU.mult, op1=ALU.mult).then_inc(s_shift, 1)

            def take_max(att, k):
                h, half = k // 2, k % 2
                for b in range(2):
                    dve.wait_ge(s_mp, att.count(2 * MAXES, 2 * k + 1 + b))
                    dve.tensor_reduce(maxes[:, h, 2 * half + b:2 * half + b + 1], p_max[:, b, :], AX.X, ALU.max
                                      ).then_inc(s_mx, 1)

            def split_max(att, group):
                v = lambda k: att.count(10, 5 * group + k)
                dve.wait_ge(s_mT, att.count(2, group + 1))
                wait(dve, s_mrow[group], att.count(16 * MAX_ROWS))
                nm, part = neg_max[:, group, :], max_part[:, group, :, :]
                dve.tensor_scalar(nm, p_max[0:16, 0, 0:P], -1.0, None, ALU.mult).then_inc(s_mpart, 1)
                dve.wait_ge(s_mpart, v(1))
                dve.tensor_copy(part[:, 0, :], nm).then_inc(s_mpart, 1)
                dve.wait_ge(s_mpart, v(2))
                dve.tensor_tensor(nm, nm, part[:, 0, :], ALU.subtract).then_inc(s_mpart, 1)
                dve.wait_ge(s_mpart, v(3))
                dve.tensor_copy(part[:, 1, :], nm).then_inc(s_mpart, 1)
                dve.wait_ge(s_mpart, v(4))
                dve.tensor_tensor(part[:, 2, :], nm, part[:, 1, :], ALU.subtract).then_inc(s_mpart, 1)

            def probs(att, k):
                t = (k % 8) // 2
                dve.wait_ge(s_e, att.count(2 * EXPS, 2 * k + 2))
                r = k % RING
                dve.scalar_tensor_tensor(out=pr[:, r, :, :],
                                         in0=adj_T[:, att.par, t, :].unsqueeze(1).to_broadcast([P, 2, N]),
                                         scalar=ADJ_EPS, in1=pr[:, r, :, :], op0=ALU.add, op1=ALU.mult
                                         ).then_inc(s_pr, 1)

            def iteration(head, front, att, newest_tail, late):
                for slot in range(SLOTS):
                    if slot == 0 and is_first(front):
                        dve.wait_ge(s_weights, 16 * N_WEIGHTS)
                        dve.tensor_scalar(neg_slope[:, :], par[:, PRELU:PRELU + 1], -1.0, None, ALU.mult
                                          ).then_inc(s_slope, 1)
                    if slot == SLOTS - 1 and is_first(front):
                        fold_parameters()
                        dve.wait_ge(s_late_const, N_LATE_CONST)
                    if att:
                        for k in due(slot, "take"):
                            take_max(att, k)
                        for group in range(2):
                            if slot == SLOT[f"splitM{group}"]:
                                split_max(att, group)
                        for k in due(slot, "probs"):
                            probs(att, k)
                    if head:
                        if slot == SLOT["stats0"]:
                            dve.wait_ge(s_x[head.par], head.loads())
                            norm_stats(x_in[:, head.par], f_stat, f_mom, s_fstat, s_fmom, head.count(4, 1))
                        if slot == SLOT["shift0"]:
                            norm_shift(f_mom, f_rstd, f_shift, s_frstd, s_fshift, head.count(4, 1))
                    if front:
                        if slot == SLOT["gcn"]:
                            dve.wait_ge(s_agg, front.count(1, 1))
                            dve.tensor_tensor(gcn_pre[:, :, :], p_f4[:, :, 0:D],
                                              row[:, 0:D].unsqueeze(1).to_broadcast([P, NT, D]), ALU.add
                                              ).then_inc(s_gpre, 1)
                            dve.tensor_copy(deg[:, 1, :], p_f4[:, :, D]).then_inc(s_din, 1)
                            dve.wait_ge(s_din, front.count(1, 1))
                            dve.wait_ge(s_dout, front.count(NT, NT))
                            degs = deg[:, :, :].rearrange("p a t -> p (a t)")
                            dve.tensor_scalar(deg_nz[:, :], degs, 0.0, None, ALU.not_equal)
                            dve.tensor_scalar(deg_floor[:, :], degs, 1e-30, None, ALU.max).then_inc(s_dfl, 1)
                        if slot == SLOT["x1"]:
                            dve.wait_ge(s_gpre, front.count(1, 1))
                            dve.scalar_tensor_tensor(out=x1[:, :, :], in0=gcn_pre[:, :, :], scalar=0.0,
                                                     in1=x_in[:, front.par, :, :], op0=ALU.max, op1=ALU.add
                                                     ).then_inc(s_gact, 1)
                            dve.wait_ge(s_slope, 1)
                            dve.wait_ge(s_gneg, front.count(1, 1))
                            dve.wait_ge(s_gact, front.count(1, 1))
                            dve.scalar_tensor_tensor(out=x1[:, :, :], in0=soft[:, :, :], scalar=neg_slope[:, :],
                                                     in1=x1[:, :, :], op0=ALU.mult, op1=ALU.add).then_inc(s_x1, 1)
                        if slot == SLOT["degrs"]:
                            dve.wait_ge(s_dpow, front.count(1, 1))
                            dve.tensor_tensor(deg_rs[:, :, :].rearrange("p a t -> p (a t)"), deg_pow[:, :],
                                              deg_nz[:, :], ALU.mult).then_inc(s_drs, 1)
                        if slot == SLOT["stats1"]:
                            dve.wait_ge(s_x1, front.count(1, 1))
                            norm_stats(x1, f_stat, f_mom, s_fstat, s_fmom, front.count(4, 2))
                        if slot == SLOT["shift1"]:
                            norm_shift(f_mom, f_rstd, f_shift, s_frstd, s_fshift, front.count(4, 2))
                        if slot == SLOT["stats2"]:
                            dve.wait_ge(s_fh, front.count(3, 2))
                            norm_stats(f_h, f_stat, f_mom, s_fstat, s_fmom, front.count(4, 3))
                        if slot == SLOT["softin"]:
                            dve.wait_ge(s_lap, front.count(1, 1))
                            dve.wait_ge(s_vl, front.count(1, 1))
                            for t in range(NT):
                                last = dve.scalar_tensor_tensor(
                                    out=pre[:, t, :], in0=p_f[:, 0, t * P:t * P + P], scalar=deg_rs[:, 0, t:t + 1],
                                    in1=v_lap[:, t, :], op0=ALU.mult, op1=ALU.subtract)
                            last.then_inc(s_pre, 1)
                        if slot == SLOT["x2"]:
                            dve.wait_ge(s_sl, front.count(1, 1))
                            dve.scalar_tensor_tensor(out=soft[:, :, :], in0=pre[:, :, :], scalar=0.0,
                                                     in1=soft[:, :, :], op0=ALU.min, op1=ALU.subtract).then_inc(s_sp, 1)
                            dve.wait_ge(s_sp, front.count(1, 1))
                            wait(dve, s_x2b, front.count(1))
                            dve.tensor_tensor(x2[:, :, :], x1[:, :, :], soft[:, :, :], ALU.subtract).then_inc(s_x2, 1)
                        if slot == SLOT["stats3"]:
                            dve.wait_ge(s_x2, front.count(1, 1))
                            norm_stats(x2, f_stat, f_mom, s_fstat, s_fmom, front.count(4, 4))
                        if slot == SLOT["shift3"]:
                            norm_shift(f_mom, f_rstd, f_shift, s_frstd, s_fshift, front.count(4, 4))
                        if slot == SLOT["qsplit"]:
                            dve.wait_ge(s_qf, front.count(1, 1))
                            dve.tensor_tensor(qf[:, :], qf[:, :], q_part[:, 0, :], ALU.subtract).then_inc(s_qs, 1)
                            dve.wait_ge(s_qs, front.count(3, 1))
                            dve.tensor_copy(q_part[:, 1, :], qf[:, :]).then_inc(s_qs, 1)
                            dve.wait_ge(s_qs, front.count(3, 2))
                            dve.tensor_tensor(q_part[:, 2, :], qf[:, :], q_part[:, 1, :], ALU.subtract
                                              ).then_inc(s_qs, 1)
                    for tail, at in placed(newest_tail, late, slot):
                        if at == SLOT["norm"]:
                            dve.wait_ge(s_on, tail.count(1, 1))
                            o4 = p_exp[:, :, :].rearrange("p g (t j w) -> p g t j w", t=NT, j=4)
                            for g2 in range(2):
                                last = dve.reciprocal(r_sum[:, g2, :, :], o4[:, g2, :, :, HD])
                            last.then_inc(s_rs, 1)
                            dve.wait_ge(s_rs, tail.count(1, 1))
                            for g2 in range(2):
                                last = dve.tensor_tensor(
                                    y[:, :, g2 * 64:g2 * 64 + 64].rearrange("p t (j w) -> p t j w", j=4),
                                    o4[:, g2, :, :, 0:HD],
                                    r_sum[:, g2, :, :].unsqueeze(3).to_broadcast([P, NT, 4, HD]), ALU.mult)
                            last.then_inc(s_y, 1)
                        if at == SLOT["x3"]:
                            dve.wait_ge(s_pj, tail.count(1, 1))
                            dve.wait_ge(s_x2b, tail.count(1, 1))
                            wait(dve, s_out[tail.par], tail.loads(0))
                            dve.tensor_tensor(x3[:, tail.par, :, :], p_exp[:, 1, :].rearrange("p (t d) -> p t d", t=NT),
                                              x2b[:, tail.par, :, :], ALU.add).then_inc(s_x3, 1)
                        if at == SLOT["stats4"]:
                            dve.wait_ge(s_x3, tail.count(1, 1))
                            norm_stats(x3[:, tail.par], t_stat, t_mom, s_tstat, s_tmom, tail.count(1, 1))
                        if at == SLOT["shift4"]:
                            norm_shift(t_mom, t_rstd, t_shift, s_trstd, s_tshift, tail.count(1, 1))
                        if at == SLOT["convsplit"]:
                            dve.wait_ge(s_cin, tail.count(1, 1))
                            dve.tensor_tensor(conv_l[:, PAD:PAD + N], xconv_T[:, :],
                                              conv_h[:, PAD:PAD + N].bitcast(F32), ALU.subtract).then_inc(s_cl, 1)
                        if at == SLOT["emb"]:
                            dve.wait_ge(s_embp, tail.count(1, 1))
                            dve.tensor_tensor(emb[:, :, :], p_e4[:, :, 0:D + NSE],
                                              row[:, 2 * D:3 * D + NSE].unsqueeze(1).to_broadcast([P, NT, D + NSE]),
                                              ALU.add).then_inc(s_emb, 1)
                        if at == SLOT["parts"]:
                            dve.wait_ge(s_emb, tail.count(1, 1))
                            s = emb[:, :, D:D + NSE]
                            v = lambda k: tail.count(10, k)

                            def place(tile, parts, part, src, scale):
                                for n, q in enumerate(parts):
                                    if q == part:
                                        last = dve.tensor_scalar(tile[:, :, NSE * n:NSE * n + NSE], src, scale, None, ALU.mult)
                                return last

                            place(dl, Q_PARTS, 0, s, 2.0)
                            place(dr, K_PARTS, 0, s, 1.0).then_inc(s_sc, 1)
                            dve.tensor_tensor(s_sq[:, :, :], s, s, ALU.mult).then_inc(s_sc, 1)
                            dve.wait_ge(s_sc, v(2))
                            dve.tensor_tensor(s_rest[:, 0, :, :], s, dr[:, :, 0:NSE], ALU.subtract)
                            dve.tensor_reduce(nsq[:, :], s_sq[:, :, :], AX.X, ALU.add, negate=True).then_inc(s_sc, 1)
                            dve.wait_ge(s_sc, v(3))
                            place(dl, Q_PARTS, 1, s_rest[:, 0, :, :], 2.0)
                            place(dr, K_PARTS, 1, s_rest[:, 0, :, :], 1.0)
                            dve.tensor_copy(dr[:, :, DIST_SQ], nsq[:, :]).then_inc(s_sc, 1)
                            dve.wait_ge(s_sc, v(4))
                            dve.tensor_tensor(s_rest[:, 1, :, :], s_rest[:, 0, :, :], dr[:, :, NSE:2 * NSE], ALU.subtract)
                            dve.tensor_tensor(sq_rest[:, 0, :], nsq[:, :], dr[:, :, DIST_SQ], ALU.subtract).then_inc(s_sc, 1)
                            dve.wait_ge(s_sc, v(5))
                            place(dl, Q_PARTS, 2, s_rest[:, 1, :, :], 2.0)
                            place(dr, K_PARTS, 2, s_rest[:, 1, :, :], 1.0)
                            dve.tensor_copy(dr[:, :, DIST_SQ + 1], sq_rest[:, 0, :]).then_inc(s_sc, 1)
                            dve.wait_ge(s_sc, v(6))
                            dve.tensor_tensor(sq_rest[:, 1, :], sq_rest[:, 0, :], dr[:, :, DIST_SQ + 1], ALU.subtract
                                              ).then_inc(s_sc, 1)
                            dve.wait_ge(s_sc, v(7))
                            dve.tensor_copy(dr[:, :, DIST_SQ + 2], sq_rest[:, 1, :]).then_inc(s_sc, 1)
                            dve.memset(dl[:, :, DIST_SQ:DIST_SQ + 3], 1.0).then_inc(s_sc, 1)
                            dve.wait_ge(s_sc, v(9))
                            dve.tensor_copy(sq[:, :], nsq[:, :]).then_inc(s_sc, 1)
                        if at == SLOT["xconv"]:
                            dve.wait_ge(s_c2, tail.count(1, 1))
                            dve.scalar_tensor_tensor(out=xconv_T[:, :], in0=p_conv[:, :], scalar=bn_scale[:, 1:2],
                                                     in1=t_hT[:, :], op0=ALU.mult, op1=ALU.add).then_inc(s_cs, 1)
                        if at == SLOT["nin"]:
                            dve.wait_ge(s_hn, tail.count(1, 1))
                            dve.wait_ge(s_tr, tail.count(1, 1))
                            dve.scalar_tensor_tensor(out=h_n[:, :], in0=t_r[:, :], scalar=1.0, in1=h_n[:, :],
                                                     op0=ALU.add, op1=ALU.mult).then_inc(s_rn, 1)
                            dve.wait_ge(s_rn, tail.count(1, 1))
                            dve.wait_ge(s_gn, tail.count(1, 1))
                            dve.tensor_tensor(h_n[:, :], p_conv[:, :], h_n[:, :], ALU.add).then_inc(s_ni, 1)
                        if at == SLOT["new"]:
                            dve.wait_ge(s_n, tail.count(1, 1))
                            dve.tensor_tensor(new_T[:, :], t_hT[:, :], n_T[:, :], ALU.subtract).then_inc(s_hm, 1)
                            dve.wait_ge(s_hm, tail.count(1, 1))
                            dve.scalar_tensor_tensor(out=new_T[:, :], in0=t_z[:, :], scalar=1.0, in1=new_T[:, :],
                                                     op0=ALU.add, op1=ALU.mult).then_inc(s_zp, 1)
                            dve.wait_ge(s_zp, tail.count(1, 1))
                            dve.scalar_tensor_tensor(out=new_T[:, :], in0=new_T[:, :], scalar=0.5, in1=n_T[:, :],
                                                     op0=ALU.mult, op1=ALU.add).then_inc(s_new, 1)
                        if at == SLOT["x4"]:
                            dve.wait_ge(s_nb, tail.count(1, 1))
                            dve.tensor_tensor(x3[:, tail.par, :, :], p_conv[:, :].rearrange("p (t d) -> p t d", t=NT),
                                              x3[:, tail.par, :, :], ALU.add).then_inc(s_x4, 1)

            pipeline(dve, iteration)

        @block.scalar
        def _(act):
            act.wait_ge(s_weights, 16 * N_WEIGHTS)
            act.wait_ge(s_const, N_CONST)

            def relu_norm(dst, src, rstd, shift):
                for t in range(NT):
                    last = act.activation(dst[:, t, :], src[:, t, :], ACT.Relu, bias=shift[:, t:t + 1],
                                          scale=rstd[:, t:t + 1])
                return last

            def exps(att, k):
                wait(act, s_pv, att.count(EXPS, max(k + 1 - RING, 0)))
                for b in range(2):
                    act.wait_ge(s_ep, att.count(2 * EXPS, 2 * k + 1 + b))
                    act.activation(pr[:, k % RING, b, :], p_exp[:, b, :], ACT.Exp).then_inc(s_e, 1)

            def iteration(head, front, att, newest_tail, late):
                for slot in range(SLOTS):
                    if slot == 0 and is_first(att):
                        act.wait_ge(s_bn, 3)
                        act.wait_ge(s_late_const, N_LATE_CONST)
                    if att:
                        for k in due(slot, "exp"):
                            exps(att, k)
                        for group in range(2):
                            if slot == SLOT[f"outcopy{group}"]:
                                act.wait_ge(s_pv, att.count(EXPS, (group + 1) * EXPS // 2))
                                wait(act, s_on, att.count(1))
                                act.activation(o_T[:, group, :], p_out[:, :], ACT.Copy).then_inc(s_oT, 1)
                    if head and slot == SLOT["relu0"]:
                        act.wait_ge(s_fshift, head.count(3, 1))
                        wait(act, s_fturn, head.count(3))
                        relu_norm(f_h, x_in[:, head.par], f_rstd, f_shift).then_inc(s_fh, 1)
                    if front:
                        if slot == SLOT["hT0"]:
                            act.wait_ge(s_fturn, front.count(3, 1))
                            act.activation(f_hT[:, :], p_f[:, 0, :], ACT.Copy).then_inc(s_fhT, 1)
                        if slot == SLOT["seqcopy"]:
                            act.wait_ge(s_seqp, front.count(1, 1))
                            act.activation(seq[:, :, 0:D], p_f[:, 1, :].rearrange("p (t d) -> p t d", t=NT),
                                           ACT.Copy).then_inc(s_seq, 1)
                        for t in due(slot, "colsum"):
                            if t == 0:
                                act.wait_ge(s_adj[front.par], front.loads())
                            act.activation(junk[t], adj_T[:, front.par, t, :], ACT.Copy,
                                           accum_out=deg[:, 0, t:t + 1]).then_inc(s_dout, 1)
                        if slot == SLOT["neg"]:
                            act.wait_ge(s_gpre, front.count(1, 1))
                            act.wait_ge(s_dout, front.count(NT, NT))
                            act.activation(soft[:, :, :], gcn_pre[:, :, :], ACT.Relu, scale=-1.0).then_inc(s_gneg, 1)
                        if slot == SLOT["relu1"]:
                            act.wait_ge(s_fshift, front.count(3, 2))
                            relu_norm(f_h, x1, f_rstd, f_shift).then_inc(s_fh, 1)
                        if slot == SLOT["xnT"]:
                            act.wait_ge(s_fturn, front.count(3, 2))
                            act.activation(f_hT[:, :], p_f[:, 0, :], ACT.Identity, bias=par[:, BETA:BETA + 1],
                                           scale=par[:, GAMMA:GAMMA + 1]).then_inc(s_fhT, 1)
                        if slot == SLOT["uscale"]:
                            act.wait_ge(s_uv, front.count(1, 1))
                            act.wait_ge(s_drs, front.count(1, 1))
                            for t in range(NT):
                                last = act.activation(u_scaled[:, t, :], p_f4[:, t, 0:D], ACT.Copy,
                                                      scale=deg_rs[:, 1, t:t + 1])
                            last.then_inc(s_us, 1)
                        if slot == SLOT["vcopy"]:
                            act.wait_ge(s_uv, front.count(1, 1))
                            act.activation(v_lap[:, :, :], p_f4[:, :, D:2 * D], ACT.Copy).then_inc(s_vl, 1)
                        if slot == SLOT["soft"]:
                            act.wait_ge(s_pre, front.count(1, 1))
                            act.activation(soft[:, :, :], pre[:, :, :], ACT.Abs).then_inc(s_abs, 1)
                            act.wait_ge(s_abs, front.count(1, 1))
                            act.activation(soft[:, :, :], soft[:, :, :], ACT.Exp, scale=-1.0).then_inc(s_se, 1)
                            act.wait_ge(s_se, front.count(1, 1))
                            act.activation(soft[:, :, :], soft[:, :, :], ACT.Ln, bias=one_col[:, 0:1]).then_inc(s_sl, 1)
                        if slot == SLOT["relu3"]:
                            act.wait_ge(s_fshift, front.count(3, 3))
                            relu_norm(f_h, x2, f_rstd, f_shift).then_inc(s_fh, 1)
                        if slot == SLOT["hT3"]:
                            act.wait_ge(s_fturn, front.count(3, 3))
                            act.activation(f_hT[:, :], p_f[:, 0, :], ACT.Copy).then_inc(s_fhT, 1)
                        if slot == SLOT["qkcopy"]:
                            act.wait_ge(s_qp, front.count(1, 1))
                            wait(act, s_qd, front.count(16))
                            act.activation(q_part[:, 0, :], p_f[:, 1, :], ACT.Copy, scale=HD ** -0.5)
                            act.activation(qf[:, :], p_f[:, 1, :], ACT.Copy, scale=HD ** -0.5).then_inc(s_qf, 1)
                            act.wait_ge(s_kp, front.count(1, 1))
                            wait(act, s_kd, front.count(16))
                            act.activation(k_part[:, 0, :], p_f[:, 0, :], ACT.Copy)
                            act.activation(kf[:, :], p_f[:, 0, :], ACT.Copy).then_inc(s_kf, 1)
                        if slot == SLOT["vcopy3"]:
                            act.wait_ge(s_vp, front.count(1, 1))
                            wait(act, s_pv, (front - 2).count(EXPS, EXPS))
                            act.activation(vals[:, front.par, :, :, 0:HD],
                                           p_f[:, 1, :].rearrange("p (t h d) -> p t h d", t=NT, h=HEADS),
                                           ACT.Copy).then_inc(s_v, 1)
                    for tail, at in placed(newest_tail, late, slot):
                        if at == SLOT["yT"]:
                            act.wait_ge(s_yTp, tail.count(1, 1))
                            act.activation(y_T[:, :], p_exp[:, 0, :], ACT.Copy).then_inc(s_yT, 1)
                        if at == SLOT["relu4"]:
                            act.wait_ge(s_tshift, tail.count(1, 1))
                            relu_norm(t_h, x3[:, tail.par], t_rstd, t_shift).then_inc(s_th, 1)
                        if at == SLOT["hT4"]:
                            act.wait_ge(s_tturn, tail.count(1, 1))
                            act.activation(t_hT[:, :], p_conv[:, :], ACT.Copy).then_inc(s_thT, 1)
                        if at == SLOT["conv1relu"]:
                            act.wait_ge(s_c1, tail.count(1, 1))
                            wait(act, s_gn, tail.count(1))
                            act.activation(xconv_T[:, :], p_conv[:, :], ACT.Relu, bias=bn_shift[:, 0:1],
                                           scale=bn_scale[:, 0:1])
                            act.activation(conv_h[:, PAD:PAD + N], p_conv[:, :], ACT.Relu, bias=bn_shift[:, 0:1],
                                           scale=bn_scale[:, 0:1]).then_inc(s_cin, 1)
                        if at == SLOT["msg"]:
                            act.wait_ge(s_emb, tail.count(1, 1))
                            wait(act, s_np, tail.count(1))
                            act.activation(msg[:, :, :], emb[:, :, 0:D], ACT.Relu).then_inc(s_msg, 1)
                        if at == SLOT["copyE"]:
                            act.wait_ge(s_dT, tail.count(1, 1))
                            act.activation(dl_T[:, :], p_exp[:, 0, 0:N // 2].bitcast(BF16), ACT.Copy)
                            act.activation(dr_T[:, :], p_exp[:, 1, 0:N // 2].bitcast(BF16), ACT.Copy).then_inc(s_dc, 1)
                        for half in due(at, "near"):
                            act.wait_ge(s_dp, tail.count(2, half + 1))
                            act.wait_ge(s_sc, tail.count(10, 10))
                            wait(act, s_np, tail.count(1))
                            for t in (2 * half, 2 * half + 1):
                                act.activation(near[:, t, :], p_exp[:, t % 2, :], ACT.Exp,
                                               bias=sq[:, t:t + 1]).then_inc(s_near, 1)
                        if at == SLOT["nmpT"]:
                            act.wait_ge(s_np, tail.count(1, 1))
                            act.activation(nmp_T[:, :], p_out[:, :], ACT.Copy).then_inc(s_nmp, 1)
                        if at == SLOT["xrelu"]:
                            act.wait_ge(s_cs, tail.count(1, 1))
                            act.activation(xconv_T[:, :], xconv_T[:, :], ACT.Relu, bias=bn_shift[:, 1:2]).then_inc(s_xc, 1)
                        if at == SLOT["gater"]:
                            act.wait_ge(s_gr, tail.count(1, 1))
                            act.activation(t_r[:, :], p_out[:, :], ACT.Tanh, bias=gate_bias[:, 0:1],
                                           scale=0.5).then_inc(s_tr, 1)
                        if at == SLOT["gatez"]:
                            act.wait_ge(s_gz, tail.count(1, 1))
                            act.activation(t_z[:, :], p_conv[:, :], ACT.Tanh, bias=gate_bias[:, 1:2],
                                           scale=0.5).then_inc(s_tz, 1)
                        if at == SLOT["gateh"]:
                            act.wait_ge(s_gh, tail.count(1, 1))
                            act.activation(h_n[:, :], p_out[:, :], ACT.Identity, bias=gate_bias[:, 2:3],
                                           scale=0.5).then_inc(s_hn, 1)
                        if at == SLOT["nact"]:
                            act.wait_ge(s_ni, tail.count(1, 1))
                            act.activation(n_T[:, :], h_n[:, :], ACT.Tanh, bias=par[:, BIH + 2:BIH + 3]).then_inc(s_n, 1)

            pipeline(act, iteration)

        @block.tensor
        def _(pe):
            pe.wait_ge(s_weights, 16 * N_WEIGHTS)
            pe.wait_ge(s_wlap, 1)
            pe.wait_ge(s_const, N_CONST)

            def turn(dst, src):
                for t in range(NT):
                    last = pe.transpose(dst[:, t * P:t * P + P], src(t), ident[:, :])
                return last

            def max_scores(att, k):
                h, half = k // 2, k % 2
                for b in range(2):
                    qb = 2 * half + b
                    wait(pe, s_mx, att.count(2 * MAXES, 2 * k - 1 + b))
                    pe.matmul(p_max[:, b, :], q_st[0:SCORE_ROWS, att.par, h, qb * P:qb * P + P],
                                     k_st[0:SCORE_ROWS, att.par, h, :], start=True, stop=True).then_inc(s_mp, 1)

            def exp_scores(att, k):
                group, u = k // 8, k % 8
                t = u // 2
                for b, h in enumerate(head_rows(u, group)):
                    wait(pe, s_e, att.count(2 * EXPS, 2 * k - 1 + b))
                    pe.matmul(p_exp[:, b, :], k_st[0:SCORE_ROWS + MAX_ROWS, att.par, h, t * P:t * P + P],
                                     q_st[0:SCORE_ROWS + MAX_ROWS, att.par, h, :], start=True, stop=True
                              ).then_inc(s_ep, 1)

            def use_probs(att, k):
                group, u = k // 8, k % 8
                t = u // 2
                pe.wait_ge(s_pr, att.count(EXPS, k + 1))
                if u == 0:
                    wait(pe, s_oT, att.count(2, group))
                for b, h in enumerate(head_rows(u, group)):
                    j = h % 4
                    last = pe.matmul(p_out[HW * j:HW * j + HW, :], vals[:, att.par, t, h, :], pr[:, k % RING, b, :],
                                     start=(t == 0), stop=(t == NT - 1), skip_group_check=True)
                last.then_inc(s_pv, 1)

            def iteration(head, front, att, newest_tail, late):
                for slot in range(SLOTS):
                    if slot == 0 and is_first(att):
                        pe.wait_ge(s_bn, 3)
                        pe.wait_ge(s_tail_weights, 16 * N_TAIL_WEIGHTS)
                        pe.wait_ge(s_late_const, N_LATE_CONST)
                    if att:
                        for k in due(slot, "max"):
                            if k == 0:
                                pe.wait_ge(s_qst[att.par], att.loads() * SPLITS)
                                pe.wait_ge(s_kst[att.par], att.loads() * SPLITS)
                                wait(pe, s_mpart, (att - 1).count(10, 6))
                            if k == MAXES // 2:
                                pe.wait_ge(s_mpart, att.count(10, 1))
                            max_scores(att, k)
                        for group in range(2):
                            if slot == SLOT[f"turnM{group}"]:
                                pe.wait_ge(s_mx, att.count(2 * MAXES, (group + 1) * MAXES))
                                pe.transpose(p_max[0:16, 0, 0:P],
                                             maxes[:, 4 * group:4 * group + 4, :].rearrange("p h t -> p (h t)"),
                                             ident[:, :]).then_inc(s_mT, 1)
                        for k in due(slot, "scores"):
                            if k % 8 == 0:
                                pe.wait_ge(s_mrow[k // 8], att.count(16 * MAX_ROWS, 16 * MAX_ROWS))
                            if k == 0:
                                wait(pe, s_near, att.count(NT))
                            exp_scores(att, k)
                        for k in due(slot, "use"):
                            if k == 0:
                                wait(pe, s_nmp, att.count(1))
                            if k == 0:
                                pe.wait_ge(s_v, att.count(1, 1))
                            use_probs(att, k)
                    if front:
                        if slot == SLOT["turn0"]:
                            pe.wait_ge(s_fh, front.count(3, 1))
                            wait(pe, s_kf, front.count(1))
                            wait(pe, s_v, front.count(1))
                            turn(p_f[:, 0, :], lambda t: f_h[:, t, :]).then_inc(s_fturn, 1)
                        if slot == SLOT["seq"]:
                            pe.wait_ge(s_fhT, front.count(3, 1))
                            for t in range(NT):
                                last = pe.matmul(p_f[:, 1, t * P:t * P + P], f_hT[:, t * P:t * P + P], wt[:, W0, :],
                                                 start=True, stop=True)
                            last.then_inc(s_seqp, 1)
                        for i in due(slot, "agg"):
                            if i == 0:
                                pe.wait_ge(s_seq, front.count(1, 1))
                                pe.wait_ge(s_adj[front.par], front.loads())
                            for t in range(NT):
                                last = pe.matmul(p_f4[:, i, 0:D + 1], adj_T[:, front.par, t, i * P:i * P + P],
                                                 seq[:, t, :], start=(t == 0), stop=(t == NT - 1))
                            if i == NT - 1:
                                last.then_inc(s_agg, 1)
                        if slot == SLOT["turn2"]:
                            pe.wait_ge(s_fz, front.count(1, 1))
                            pe.wait_ge(s_din, front.count(1, 1))
                            turn(p_f[:, 0, :], lambda t: f_z[:, t, :]).then_inc(s_fturn, 1)
                        if slot == SLOT["uv"]:
                            pe.wait_ge(s_fhT, front.count(3, 2))
                            for t in range(NT):
                                last = pe.matmul(p_f4[:, t, :], f_hT[:, t * P:t * P + P],
                                                 w_lap[:, :, :].rearrange("p a n -> p (a n)"), start=True, stop=True)
                            last.then_inc(s_uv, 1)
                        for i in due(slot, "lap"):
                            if i == 0:
                                pe.wait_ge(s_us, front.count(1, 1))
                                pe.wait_ge(s_vl, front.count(1, 1))
                            for t in range(NT):
                                last = pe.matmul(p_f[:, 0, i * P:i * P + P], adj_T[:, front.par, t, i * P:i * P + P],
                                                 u_scaled[:, t, :], start=(t == 0), stop=(t == NT - 1))
                            if i == NT - 1:
                                last.then_inc(s_lap, 1)
                        if slot == SLOT["turn3"]:
                            pe.wait_ge(s_fh, front.count(3, 3))
                            pe.wait_ge(s_pre, front.count(1, 1))
                            turn(p_f[:, 0, :], lambda t: f_h[:, t, :]).then_inc(s_fturn, 1)
                        if slot == SLOT["qk"]:
                            pe.wait_ge(s_fhT, front.count(3, 3))
                            pe.matmul(p_f[:, 1, :], wt[:, WQ, :], f_hT[:, :], start=True, stop=True).then_inc(s_qp, 1)
                            pe.matmul(p_f[:, 0, :], wt[:, WK, :], f_hT[:, :], start=True, stop=True).then_inc(s_kp, 1)
                        if slot == SLOT["v"]:
                            pe.wait_ge(s_qf, front.count(1, 1))
                            for t in range(NT):
                                last = pe.matmul(p_f[:, 1, t * P:t * P + P], f_hT[:, t * P:t * P + P], wt[:, WV, :],
                                                 start=True, stop=True)
                            last.then_inc(s_vp, 1)
                    for tail, at in placed(newest_tail, late, slot):
                        if at == SLOT["outT"]:
                            pe.wait_ge(s_oT, tail.count(2, 2))
                            for group in range(2):
                                last = turn(p_exp[:, group, :], lambda t: o_T[:, group, t * P:t * P + P])
                            last.then_inc(s_on, 1)
                        if at == SLOT["turnY"]:
                            pe.wait_ge(s_y, tail.count(1, 1))
                            turn(p_exp[:, 0, :], lambda t: y[:, t, :]).then_inc(s_yTp, 1)
                        if at == SLOT["proj"]:
                            pe.wait_ge(s_yT, tail.count(1, 1))
                            for t in range(NT):
                                last = pe.matmul(p_exp[:, 1, t * P:t * P + P], y_T[:, t * P:t * P + P], wt[:, WO, :],
                                                 start=True, stop=True)
                            last.then_inc(s_pj, 1)
                        if at == SLOT["turn4"]:
                            pe.wait_ge(s_th, tail.count(1, 1))
                            wait(pe, s_x4, tail.count(1))
                            turn(p_conv[:, :], lambda t: t_h[:, t, :]).then_inc(s_tturn, 1)
                        if at == SLOT["conv1"]:
                            pe.wait_ge(s_thT, tail.count(1, 1))
                            pe.matmul(p_conv[:, :], wt[:, WC1, :], t_hT[:, :], start=True, stop=True).then_inc(s_c1, 1)
                            pe.wait_ge(s_x3, tail.count(1, 1))
                            for t in range(NT):
                                last = pe.matmul(p_e4[:, t, 0:D + NSE], t_hT[:, t * P:t * P + P], w_emb[:, :],
                                                 start=True, stop=True)
                            last.then_inc(s_embp, 1)
                        for k in due(at, "conv2"):
                            if k == 0:
                                pe.wait_ge(s_cl, tail.count(1, 1))
                            pe.matmul(p_conv[:, :], w_conv2h[:, k, :], conv_h[:, k:k + N], start=(k == 0), stop=False)
                            pe.matmul(p_conv[:, :], w_conv2l[:, k, :], conv_h[:, k:k + N], start=False, stop=False)
                            mm = pe.matmul(p_conv[:, :], w_conv2h[:, k, :], conv_l[:, k:k + N], start=False,
                                           stop=(k == TAPS - 1))
                            if k == TAPS - 1:
                                mm.then_inc(s_c2, 1)
                        if at == SLOT["turnE"]:
                            pe.wait_ge(s_sc, tail.count(10, 9))
                            for side, tile in enumerate((dl, dr)):
                                for t in range(NT):
                                    last = pe.transpose(p_exp[:, side, t * P // 2:(t + 1) * P // 2].bitcast(BF16),
                                                        tile[:, t, :], ident_b[:, :])
                            last.then_inc(s_dT, 1)
                        for half in due(at, "dist"):
                            pe.wait_ge(s_dc, tail.count(1, 1))
                            wait(pe, s_near, tail.count(NT, 2 * half))
                            for t in (2 * half, 2 * half + 1):
                                last = pe.matmul(p_exp[:, t % 2, :], dl_T[:, t * P:t * P + P], dr_T[:, :],
                                                 start=True, stop=True)
                            last.then_inc(s_dp, 1)
                        for t in due(at, "nmp"):
                            pe.wait_ge(s_nm, tail.count(NT, t + 1))
                            if t == 0:
                                pe.wait_ge(s_msg, tail.count(1, 1))
                                wait(pe, s_hn, tail.count(1))
                            mm = pe.matmul(p_out[:, :], msg[:, t, :], near[:, t, :], start=(t == 0),
                                           stop=(t == NT - 1))
                            if t == NT - 1:
                                mm.then_inc(s_np, 1)
                        def gate(dst, cols, rows_in):
                            for n, (k, rhs) in enumerate(rows_in):
                                last = pe.matmul(dst, w_gru[:, k, cols * D:cols * D + D], rhs[:, :], start=(n == 0),
                                                 stop=(n == len(rows_in) - 1))
                            return last

                        def gate_inputs():
                            pe.wait_ge(s_nmp, tail.count(1, 1))
                            pe.wait_ge(s_xc, tail.count(1, 1))

                        x_parts = [(1, nmp_T), (0, xconv_T)]
                        if at == SLOT["grur"]:
                            gate_inputs()
                            if at >= SLOTS and newest_tail:
                                pe.wait_ge(s_oT, newest_tail.count(2, 2))
                            gate(p_out[:, :], 0, [(2, t_hT)] + x_parts).then_inc(s_gr, 1)
                        if at == SLOT["gruz"]:
                            gate_inputs()
                            gate(p_conv[:, :], 1, [(2, t_hT)] + x_parts).then_inc(s_gz, 1)
                        if at == SLOT["gruh"]:
                            pe.wait_ge(s_tr, tail.count(1, 1))
                            gate(p_out[:, :], 2, [(2, t_hT)]).then_inc(s_gh, 1)
                        if at == SLOT["grun"]:
                            pe.wait_ge(s_tz, tail.count(1, 1))
                            gate(p_conv[:, :], 2, x_parts).then_inc(s_gn, 1)
                        if at == SLOT["back"]:
                            pe.wait_ge(s_new, tail.count(1, 1))
                            turn(p_conv[:, :], lambda t: new_T[:, t * P:t * P + P]).then_inc(s_nb, 1)

            pipeline(pe, iteration)


def kernel(**inputs):
    import numpy as np
    import concourse.bacc as bacc
    from concourse.bass_utils import run_bass_kernel_spmd

    a = {k: np.asarray(v) for k, v in inputs.items()}
    f = np.float32
    ih, hh = a["L3_gnn_w_ih"], a["L3_gnn_w_hh"]
    blocks = [a["L0_gnn_W"], a["L1_gnn_W_self"], a["L1_gnn_W_neigh"], a["L2_gnn_Wq"].T, a["L2_gnn_Wk"].T,
              a["L2_gnn_Wv"].T, a["L2_gnn_Wo"].T, a["L3_gnn_conv1_w"][:, :, 0].T, a["L3_gnn_w_msg"].T]
    blocks += [ih[k * D:k * D + D, 0:D].T for k in range(3)]
    blocks += [ih[k * D:k * D + D, D:2 * D].T for k in range(3)]
    blocks += [hh[k * D:k * D + D, :].T for k in range(3)]
    rows = np.concatenate([np.broadcast_to(v, (P, v.size)) for v in (
        a["L0_gnn_bias"], a["L2_gnn_bo"], a["L3_gnn_b_msg"], a["L3_gnn_b_se"])] + [a["L3_gnn_w_se"].T], axis=1)
    params = np.stack([a["L1_gnn_gamma"], a["L1_gnn_beta"], np.broadcast_to(a["L0_gnn_prelu_a"], (P,)),
                       a["L3_gnn_bn1_g"], a["L3_gnn_bn1_b"], a["L3_gnn_bn1_m"], a["L3_gnn_bn1_v"],
                       a["L3_gnn_bn2_g"], a["L3_gnn_bn2_b"], a["L3_gnn_bn2_m"], a["L3_gnn_bn2_v"],
                       *a["L3_gnn_b_ih"].reshape(3, D), *a["L3_gnn_b_hh"].reshape(3, D)], axis=1)
    arrays = {
        "x": a["x"],
        "adj_t": np.transpose(a["adj"], (0, 2, 1)),
        "weights": np.stack(blocks),
        "rows": rows,
        "params": params,
        "conv2": np.transpose(a["L3_gnn_conv2_w"], (2, 1, 0)),
    }
    arrays = {k: np.ascontiguousarray(v) for k, v in arrays.items()}
    nc = bacc.Bacc("TRN2", target_bir_lowering=False, num_devices=1)
    args = [nc.dram_tensor(k, v.shape, mybir.dt.from_np(v.dtype), kind="ExternalInput").ap()
            for k, v in arrays.items()]
    out = nc.dram_tensor("out", (B, N, D), F32, kind="ExternalOutput").ap()
    build(nc, *args, out)
    r = run_bass_kernel_spmd(nc, [arrays], core_ids=[0])
    return r.results[0]["out"]
```
